# Optimizing a Trainium2 kernel written in Bass

```python
import numpy as np
import jax
import jax.numpy as jnp

def _softmax(x, axis=-1):
    return jax.nn.softmax(x, axis=axis)

def _gelu(x):
    return jax.nn.gelu(x, approximate=True)

def _silu(x):
    return jax.nn.silu(x)

def _sigmoid(x):
    return jax.nn.sigmoid(x)

def _layernorm(x, axis=-1, eps=1e-05):
    m = jnp.mean(x, axis=axis, keepdims=True)
    v = jnp.var(x, axis=axis, keepdims=True)
    return (x - m) / jnp.sqrt(v + eps)

def _scatter_add(tgt, idx, src, axis=0):
    return tgt.at[idx].add(src)

def _segment_sum(src, seg, n):
    return jax.ops.segment_sum(src, seg, n)
kernel_name = 'mk_gnn_resnorm_d4_gnn_r32_29bca6'

def setup_inputs(seed: int=0):
    np.random.seed(seed)
    _w = jnp.asarray

    def _rec_inputs():
        import jax
        import jax.numpy as jnp
        _gk = jax.random.key(seed)
        x = -0.0003713 + 1 * jax.random.normal(jax.random.fold_in(_gk, 1), (3125, 128), jnp.float32)
        src = jax.random.randint(jax.random.fold_in(_gk, 2), (100000,), 0, 3125, jnp.int32)
        dst = jnp.minimum((3125 * jax.random.uniform(jax.random.fold_in(_gk, 3), (100000,)) ** 2.0).astype(jnp.int32), 99999)
        _o = jnp.argsort(dst, stable=True)
        src = src[_o]
        dst = dst[_o]
        edge_attr_32 = 0.000189758 + 1.00013 * jax.random.normal(jax.random.fold_in(_gk, 12), (100000, 32), jnp.float32)
        edge_attr_64 = -5.3897e-05 + 0.999841 * jax.random.normal(jax.random.fold_in(_gk, 13), (100000, 64), jnp.float32)
        edge_weight = -0.000414295 + 0.999828 * jax.random.normal(jax.random.fold_in(_gk, 15), (100000,), jnp.float32)
        return (x, src, dst, edge_attr_32, edge_attr_64, edge_weight)
    x, src, dst, edge_attr_32, edge_attr_64, edge_weight = _rec_inputs()

    def _L0_gnn_setup():
        import jax, jax.numpy as jnp
        import numpy as np
        N = 3125
        E = 12500
        ND = 128
        ED = 64
        HD = 128
        EPS = 1e-05

        def _layernorm(x, g, b):
            m = x.mean(-1, keepdims=True)
            v = ((x - m) ** 2).mean(-1, keepdims=True)
            return (x - m) / jnp.sqrt(v + EPS) * g + b
        key = jax.random.key(seed)
        ks = jax.random.split(key, 16)

        def lin(k, fi, fo):
            s = 1.0 / np.sqrt(fi)
            kw, kb = jax.random.split(k)
            return (jax.random.uniform(kw, (fi, fo), jnp.float32, -s, s), jax.random.uniform(kb, (fo,), jnp.float32, -s, s))
        msg_w1, msg_b1 = lin(ks[3], 2 * ND + ED, HD)
        msg_w2, msg_b2 = lin(ks[4], HD, HD)
        upd_w1, upd_b1 = lin(ks[5], ND + HD, HD)
        upd_w2, upd_b2 = lin(ks[6], HD, ND)
        return {'node_feats': jax.random.normal(ks[0], (N, ND), jnp.float32), 'edge_feats': jax.random.normal(ks[1], (E, ED), jnp.float32), 'edge_index': jax.random.randint(ks[2], (2, E), 0, N, dtype=jnp.int32), 'msg_w1': msg_w1, 'msg_b1': msg_b1, 'ln1_g': jnp.ones((HD,), jnp.float32), 'ln1_b': jnp.zeros((HD,), jnp.float32), 'msg_w2': msg_w2, 'msg_b2': msg_b2, 'upd_w1': upd_w1, 'upd_b1': upd_b1, 'ln2_g': jnp.ones((HD,), jnp.float32), 'ln2_b': jnp.zeros((HD,), jnp.float32), 'upd_w2': upd_w2, 'upd_b2': upd_b2}
    _L0_gnn_all = _L0_gnn_setup()
    _L0_gnn_in = {k: v for k, v in _L0_gnn_all.items() if k in ('msg_w1', 'msg_b1', 'ln1_g', 'ln1_b', 'msg_w2', 'msg_b2', 'upd_w1', 'upd_b1', 'ln2_g', 'ln2_b', 'upd_w2', 'upd_b2')}
    del _L0_gnn_all

    def _L1_gnn_setup():
        import jax, jax.numpy as jnp
        import numpy as np
        N_NODES = 3125
        N_EDGES = 50000
        D_FEAT = 128
        key = jax.random.key(seed)
        k1, k2, k3, k4 = jax.random.split(key, 4)
        feat = jax.random.normal(k1, (N_NODES, D_FEAT), dtype=jnp.float32)
        edge_weight = jax.random.normal(k2, (N_EDGES,), dtype=jnp.float32)
        beta = jnp.ones((1,), dtype=jnp.float32)
        eps = jnp.zeros((1,), dtype=jnp.float32)
        src = jax.random.randint(k3, (N_EDGES,), 0, N_NODES, dtype=jnp.int64)
        dst = jax.random.randint(k4, (N_EDGES,), 0, N_NODES, dtype=jnp.int64)
        return {'feat': feat, 'edge_weight': edge_weight, 'beta': beta, 'eps': eps, 'src': src, 'dst': dst}
    _L1_gnn_all = _L1_gnn_setup()
    _L1_gnn_in = {k: v for k, v in _L1_gnn_all.items() if k in ('beta', 'eps')}
    del _L1_gnn_all

    def _L2_gnn_setup():
        import jax, jax.numpy as jnp
        import numpy as np
        N_NODES = 3125
        N_EDGES = 50000
        IN_DIM = 128
        OUT_DIM = 128
        EDGE_DIM = 32
        EPS = 1e-05

        def _layernorm(h, gamma, beta):
            mu = jnp.mean(h, axis=-1, keepdims=True)
            var = jnp.var(h, axis=-1, keepdims=True)
            return (h - mu) * jax.lax.rsqrt(var + EPS) * gamma + beta
        key = jax.random.key(seed)
        ks = jax.random.split(key, 10)
        hid = OUT_DIM * 2
        x = jax.random.normal(ks[0], (N_NODES, IN_DIM), dtype=jnp.float32)
        edge_index = jax.random.randint(ks[1], (2, N_EDGES), 0, N_NODES, dtype=jnp.int64)
        edge_attr = jax.random.normal(ks[2], (N_EDGES, EDGE_DIM), dtype=jnp.float32)
        W1 = jax.random.normal(ks[3], (IN_DIM + EDGE_DIM, hid), dtype=jnp.float32) / np.sqrt(IN_DIM + EDGE_DIM)
        b1 = jnp.zeros((hid,), jnp.float32)
        g1 = jnp.ones((hid,), jnp.float32)
        be1 = jnp.zeros((hid,), jnp.float32)
        W2 = jax.random.normal(ks[4], (hid, OUT_DIM), dtype=jnp.float32) / np.sqrt(hid)
        b2 = jnp.zeros((OUT_DIM,), jnp.float32)
        Wu = jax.random.normal(ks[5], (IN_DIM + OUT_DIM, OUT_DIM), dtype=jnp.float32) / np.sqrt(IN_DIM + OUT_DIM)
        bu = jnp.zeros((OUT_DIM,), jnp.float32)
        gu = jnp.ones((OUT_DIM,), jnp.float32)
        beu = jnp.zeros((OUT_DIM,), jnp.float32)
        return {'x': x, 'edge_index': edge_index, 'edge_attr': edge_attr, 'W1': W1, 'b1': b1, 'g1': g1, 'be1': be1, 'W2': W2, 'b2': b2, 'Wu': Wu, 'bu': bu, 'gu': gu, 'beu': beu}
    _L2_gnn_all = _L2_gnn_setup()
    _L2_gnn_in = {k: v for k, v in _L2_gnn_all.items() if k in ('W1', 'b1', 'g1', 'be1', 'W2', 'b2', 'Wu', 'bu', 'gu', 'beu')}
    del _L2_gnn_all

    def _L3_gnn_setup():
        import jax, jax.numpy as jnp
        import numpy as np
        N_NODES = 10000
        N_EDGES = 20000
        IN_CH = 128
        OUT_CH = 128
        key = jax.random.key(seed)
        k1, k2, k3, k4 = jax.random.split(key, 4)
        x = jax.random.normal(k1, (N_NODES, IN_CH), dtype=jnp.float32)
        edge_index = jax.random.randint(k2, (2, N_EDGES), 0, N_NODES, dtype=jnp.int64)
        bound = 1.0 / np.sqrt(2 * IN_CH)
        W = jax.random.uniform(k3, (OUT_CH, 2 * IN_CH), dtype=jnp.float32, minval=-bound, maxval=bound)
        b = jax.random.uniform(k4, (OUT_CH,), dtype=jnp.float32, minval=-bound, maxval=bound)
        return {'x': x, 'W': W, 'b': b, 'edge_index': edge_index}
    _L3_gnn_all = _L3_gnn_setup()
    _L3_gnn_in = {k: v for k, v in _L3_gnn_all.items() if k in ('W', 'b')}
    del _L3_gnn_all
    return {'x': x, 'src': src, 'dst': dst, 'edge_attr_32': edge_attr_32, 'edge_attr_64': edge_attr_64, 'edge_weight': edge_weight, 'L0_gnn_msg_w1': _L0_gnn_in['msg_w1'], 'L0_gnn_msg_b1': _L0_gnn_in['msg_b1'], 'L0_gnn_ln1_g': _L0_gnn_in['ln1_g'], 'L0_gnn_ln1_b': _L0_gnn_in['ln1_b'], 'L0_gnn_msg_w2': _L0_gnn_in['msg_w2'], 'L0_gnn_msg_b2': _L0_gnn_in['msg_b2'], 'L0_gnn_upd_w1': _L0_gnn_in['upd_w1'], 'L0_gnn_upd_b1': _L0_gnn_in['upd_b1'], 'L0_gnn_ln2_g': _L0_gnn_in['ln2_g'], 'L0_gnn_ln2_b': _L0_gnn_in['ln2_b'], 'L0_gnn_upd_w2': _L0_gnn_in['upd_w2'], 'L0_gnn_upd_b2': _L0_gnn_in['upd_b2'], 'L1_gnn_beta': _L1_gnn_in['beta'], 'L1_gnn_eps': _L1_gnn_in['eps'], 'L2_gnn_W1': _L2_gnn_in['W1'], 'L2_gnn_b1': _L2_gnn_in['b1'], 'L2_gnn_g1': _L2_gnn_in['g1'], 'L2_gnn_be1': _L2_gnn_in['be1'], 'L2_gnn_W2': _L2_gnn_in['W2'], 'L2_gnn_b2': _L2_gnn_in['b2'], 'L2_gnn_Wu': _L2_gnn_in['Wu'], 'L2_gnn_bu': _L2_gnn_in['bu'], 'L2_gnn_gu': _L2_gnn_in['gu'], 'L2_gnn_beu': _L2_gnn_in['beu'], 'L3_gnn_W': _L3_gnn_in['W'], 'L3_gnn_b': _L3_gnn_in['b']}

def reference(x, src, dst, edge_attr_32, edge_attr_64, edge_weight, L0_gnn_msg_w1, L0_gnn_msg_b1, L0_gnn_ln1_g, L0_gnn_ln1_b, L0_gnn_msg_w2, L0_gnn_msg_b2, L0_gnn_upd_w1, L0_gnn_upd_b1, L0_gnn_ln2_g, L0_gnn_ln2_b, L0_gnn_upd_w2, L0_gnn_upd_b2, L1_gnn_beta, L1_gnn_eps, L2_gnn_W1, L2_gnn_b1, L2_gnn_g1, L2_gnn_be1, L2_gnn_W2, L2_gnn_b2, L2_gnn_Wu, L2_gnn_bu, L2_gnn_gu, L2_gnn_beu, L3_gnn_W, L3_gnn_b):
    import jax
    import jax.numpy as jnp

    def _L0_gnn_ref(node_feats, edge_feats, edge_index, msg_w1, msg_b1, ln1_g, ln1_b, msg_w2, msg_b2, upd_w1, upd_b1, ln2_g, ln2_b, upd_w2, upd_b2):
        import jax, jax.numpy as jnp
        import numpy as np
        N = 3125
        E = 12500
        ND = 128
        ED = 64
        HD = 128
        EPS = 1e-05

        def _layernorm(x, g, b):
            m = x.mean(-1, keepdims=True)
            v = ((x - m) ** 2).mean(-1, keepdims=True)
            return (x - m) / jnp.sqrt(v + EPS) * g + b
        src, tgt = (edge_index[0], edge_index[1])
        src_bi = jnp.concatenate([src, tgt], 0)
        tgt_bi = jnp.concatenate([tgt, src], 0)
        ef_bi = jnp.concatenate([edge_feats, edge_feats], 0)
        mi = jnp.concatenate([node_feats[src_bi], node_feats[tgt_bi], ef_bi], 1)
        h = jax.nn.relu(_layernorm(mi @ msg_w1 + msg_b1, ln1_g, ln1_b)) @ msg_w2 + msg_b2
        agg = jax.ops.segment_sum(h, tgt_bi, num_segments=node_feats.shape[0])
        ui = jnp.concatenate([node_feats, agg], 1)
        upd = jax.nn.relu(_layernorm(ui @ upd_w1 + upd_b1, ln2_g, ln2_b)) @ upd_w2 + upd_b2
        return node_feats + upd

    def _L1_gnn_ref(feat, edge_weight, beta, eps, src, dst):
        import jax, jax.numpy as jnp
        import numpy as np
        N_NODES = 3125
        N_EDGES = 50000
        D_FEAT = 128
        n = feat.shape[0]
        norm = jnp.sqrt(jnp.sum(feat * feat, axis=-1, keepdims=True))
        norm_h = feat / jnp.maximum(norm, 1e-12)
        e = beta[0] * edge_weight
        seg_max = jax.ops.segment_max(e, src, num_segments=n)
        p = jnp.exp(e - seg_max[src])
        seg_sum = jax.ops.segment_sum(p, src, num_segments=n)
        p = p / seg_sum[src]
        msg = norm_h[src] * p[:, None]
        agg = jax.ops.segment_sum(msg, dst, num_segments=n)
        return (1.0 + eps[0]) * feat + agg

    def _L2_gnn_ref(x, edge_index, edge_attr, W1, b1, g1, be1, W2, b2, Wu, bu, gu, beu):
        import jax, jax.numpy as jnp
        import numpy as np
        N_NODES = 3125
        N_EDGES = 50000
        IN_DIM = 128
        OUT_DIM = 128
        EDGE_DIM = 32
        EPS = 1e-05

        def _layernorm(h, gamma, beta):
            mu = jnp.mean(h, axis=-1, keepdims=True)
            var = jnp.var(h, axis=-1, keepdims=True)
            return (h - mu) * jax.lax.rsqrt(var + EPS) * gamma + beta
        row, col = (edge_index[0], edge_index[1])
        msg_in = jnp.concatenate([x[row], edge_attr], axis=-1)
        h = msg_in @ W1 + b1
        h = jax.nn.gelu(_layernorm(h, g1, be1), approximate=False)
        msg = h @ W2 + b2
        agg = jax.ops.segment_sum(msg, col, num_segments=x.shape[0])
        u = jnp.concatenate([x, agg], axis=-1) @ Wu + bu
        u = jax.nn.gelu(_layernorm(u, gu, beu), approximate=False)
        return u + x

    def _L3_gnn_ref(x, W, b, edge_index):
        import jax, jax.numpy as jnp
        import numpy as np
        N_NODES = 10000
        N_EDGES = 20000
        IN_CH = 128
        OUT_CH = 128
        src, dst = (edge_index[0], edge_index[1])
        x_i = x[dst]
        x_j = x[src]
        feat = jnp.concatenate([x_i, x_j - x_i], axis=-1)
        msg = feat @ W.T + b
        out = jax.ops.segment_max(msg, dst, num_segments=x.shape[0])
        return jnp.where(jnp.isfinite(out), out, 0.0)
    edge_index = jnp.stack([src, dst])
    x = _layernorm(x + _L0_gnn_ref(x, edge_attr_64, edge_index, L0_gnn_msg_w1, L0_gnn_msg_b1, L0_gnn_ln1_g, L0_gnn_ln1_b, L0_gnn_msg_w2, L0_gnn_msg_b2, L0_gnn_upd_w1, L0_gnn_upd_b1, L0_gnn_ln2_g, L0_gnn_ln2_b, L0_gnn_upd_w2, L0_gnn_upd_b2), axis=-1)
    x = _layernorm(x + _L1_gnn_ref(x, edge_weight, L1_gnn_beta, L1_gnn_eps, src, dst), axis=-1)
    x = _layernorm(x + _L2_gnn_ref(x, edge_index, edge_attr_32, L2_gnn_W1, L2_gnn_b1, L2_gnn_g1, L2_gnn_be1, L2_gnn_W2, L2_gnn_b2, L2_gnn_Wu, L2_gnn_bu, L2_gnn_gu, L2_gnn_beu), axis=-1)
    x = _layernorm(x + _L3_gnn_ref(x, L3_gnn_W, L3_gnn_b, edge_index), axis=-1)
    return x

_drawn_inputs = setup_inputs


def setup_inputs(seed=0):
    import zlib

    import numpy as np

    out = dict(_drawn_inputs(seed))
    spreads = {'L0_gnn_ln1_g': (1.0, 0.2),
     'L0_gnn_ln1_b': (0.0, 0.411),
     'L0_gnn_ln2_g': (1.0, 0.2),
     'L0_gnn_ln2_b': (0.0, 0.363),
     'L2_gnn_b1': (0.0, 0.1),
     'L2_gnn_g1': (1.0, 0.2),
     'L2_gnn_be1': (0.0, 0.1),
     'L2_gnn_b2': (0.0, 0.1),
     'L2_gnn_bu': (0.0, 0.8),
     'L2_gnn_gu': (1.0, 0.2),
     'L2_gnn_beu': (0.0, 0.1)}
    factors = {'edge_attr_64': 3.768,
     'edge_weight': 6.197,
     'L0_gnn_msg_b1': 4.205,
     'L0_gnn_upd_b1': 55.77}
    for name, (base, spread) in spreads.items():
        noise = np.random.default_rng([zlib.crc32(name.encode()), seed]).standard_normal(out[name].shape)
        drawn = base * np.exp(spread * noise) if base else spread * noise
        out[name] = jnp.asarray(drawn.astype(out[name].dtype))
    for name, factor in factors.items():
        out[name] = (out[name] * factor).astype(out[name].dtype)
    return out
```

```python
import concourse.bass as bass
from concourse import mybir
from contextlib import ExitStack

P = 128
N = 3125
NBLK = 25
NPAD = NBLK * P
DUMMY = NPAD - 1
E = 100000
NCH = 784
EP = NCH * P
CB = 4
NBAT = NCH // CB
NG = NBAT // 2
GE = 2 * CB * P
TR = NPAD + P
KT = 8
XW = 132
SUB = 28
NSAMP = NCH * P // SUB
BIG = 3.0e38
EPS = 1e-5

F32 = mybir.dt.float32
BF16 = mybir.dt.bfloat16
I32 = mybir.dt.int32
ALU = mybir.AluOpType
ACT = mybir.ActivationFunctionType
AX = mybir.AxisListType.X


class Queues:

    def __init__(self, nc, ctx):
        self.nc, self.ctx = nc, ctx
        self.q = {n: [] for n in ("pe", "dve", "act", "pool", "sp")}
        self.seen = {n: {} for n in self.q}
        self.count = {}
        self.sems = {}
        self.own = {n: self.sem("s_" + n) for n in self.q}

    def sem(self, name):
        s = self.ctx.enter_context(self.nc.semaphore(name))
        self.sems[name] = s
        self.count[name] = 0
        return name

    def wait(self, eng, after):
        for tok in after:
            if tok is None:
                continue
            if isinstance(tok, list):
                self.wait(eng, tok)
                continue
            name, v = tok
            if self.seen[eng].get(name, 0) < v:
                self.seen[eng][name] = v
                s = self.sems[name]
                self.q[eng].append(lambda e, s=s, v=v: e.wait_ge(s, v))

    def op(self, eng, fn, *after):
        self.wait(eng, after)
        name = self.own[eng]
        self.count[name] += 1
        s = self.sems[name]
        self.q[eng].append(lambda e: fn(e).then_inc(s, 1))
        return (name, self.count[name])

    def dma(self, eng, name, fn, *after):
        self.wait(eng, after)
        self.count[name] += 16
        s = self.sems[name]
        self.q[eng].append(lambda e: fn(e).then_inc(s, 16))
        return (name, self.count[name])

    def barrier(self):
        toks = [(n, c) for n, c in self.count.items() if c]
        for eng in self.q:
            self.wait(eng, toks)


class Arena:

    def __init__(self, t, words):
        self.t, self.words, self.at = t, words, 0

    def reset(self):
        self.at = 0

    def get(self, *shape, dt=F32):
        n = 1
        for s in shape:
            n *= s
        w = n if dt != BF16 else (n + 1) // 2
        w = (w + 7) // 8 * 8
        assert self.at + w <= self.words, (self.at, w)
        v = self.t[:, self.at:self.at + w]
        self.at += w
        if dt != F32:
            v = v.bitcast(dt)
        v = v[:, 0:n]
        if len(shape) == 2:
            v = v.rearrange("p (a b) -> p a b", b=shape[1])
        if len(shape) == 3:
            v = v.rearrange("p (a b c) -> p a b c", b=shape[1], c=shape[2])
        return v


def build(nc, A, out):
    with ExitStack() as ctx:
        Q = Queues(nc, ctx)
        op, dma = Q.op, Q.dma

        def sb(name, shape, dt=F32):
            return ctx.enter_context(nc.sbuf_tensor(name, [P] + shape, dt))

        def dram(name, shape, dt=F32):
            return nc.dram_tensor(name, shape, dt).ap()

        AW = 41500
        arena = Arena(sb("arena", [AW]), AW)
        PS = ctx.enter_context(nc.psum_tensor("PS", [P, 4096], F32))

        def bank(i, n=512):
            return PS[:, 512 * i:512 * i + n]

        ident = sb("ident", [P])
        ltri = sb("ltri", [P])
        iotaf = sb("iotaf", [P])
        pcol = sb("pcol", [1])
        nodeid = sb("nodeid", [NBLK])
        mhalf = sb("mhalf", [P])
        xn = sb("xn", [NBLK, P])
        srcF = sb("srcF", [NCH])
        srcI = sb("srcI", [NCH], I32)
        dstI = sb("dstI", [NCH], I32)
        eF = sb("eF", [NCH])
        beta = sb("beta", [1])
        epsc = sb("epsc", [1])
        endI = sb("endI", [NBLK], I32)
        deg = sb("deg", [NBLK])
        has = sb("has", [NBLK])
        Mx = sb("Mx", [NBLK])
        Sx = sb("Sx", [NBLK])
        small = sb("small", [16, NBLK])
        W1ab = sb("W1ab", [2 * P])
        We = sb("We", [P])
        cols = sb("cols", [8])
        wA = sb("wA", [2 * P])
        wB = sb("wB", [2 * P])
        wC = sb("wC", [2 * P])
        wD = sb("wD", [2 * P])
        vec = sb("vec", [8, 2 * P])

        dF = dram("dF", (EP,))
        sF = dram("sF", (EP,))
        wF = dram("wF", (EP,))
        keepR = dram("keepR", (EP,), BF16)
        negR = dram("negR", (EP,), BF16)
        sampR = dram("sampR", (NSAMP,))
        ubR = dram("ubR", (NPAD + 1,))
        T0 = dram("T0", (NPAD, 2 * P))
        T1 = dram("T1", (NPAD, XW))
        T2 = dram("T2", (NPAD, 2 * P))
        T3 = dram("T3", (NPAD, P))
        tabs = [dram(f"tab{k}", (TR, XW)) for k in range(KT)]
        stat = dram("stat", (NCH * TR, 2))
        H0 = dram("H0", (EP, P))
        H1 = dram("H1", (EP, P))
        H2 = dram("H2", (EP, 2 * P))
        H3 = dram("H3", (EP, P))

        s_ld = Q.sem("s_ld")
        s_st = Q.sem("s_st")
        s_init = Q.sem("s_init")
        s_g = Q.sem("s_g")

        def row(v, n):
            return v.rearrange("(a n) -> a n", a=1).to_broadcast([P, n])

        state = {"last": None}

        def step(eng, fn):
            state["last"] = op(eng, fn, state["last"])
            return state["last"]

        def load(fns, eng="sp", sem=s_ld):
            for fn in fns:
                tok = dma(eng, sem, fn, state["last"])
            state["last"] = [state["last"], tok]
            return tok

        op("pool", lambda e: e.memset(ident[:, :], 0.0))
        op("pool", lambda e: e.memset(ltri[:, :], 1.0))
        op("pool", lambda e: e.memset(mhalf[:, :], -0.5))
        op("pool", lambda e: e.iota(pcol[:, :], [[0, 1]], base=NPAD, channel_multiplier=1,
                                    allow_small_or_imprecise_dtypes=True))
        a = op("pool", lambda e: e.iota(nodeid[:, :], [[P, NBLK]], base=0, channel_multiplier=1,
                                        allow_small_or_imprecise_dtypes=True))
        op("pool", lambda e: e.affine_select(out=ident[:, :], in_=ident[:, :], compare_op=ALU.not_equal, fill=1.0,
                                             base=0, pattern=[[-1, P]], channel_multiplier=1), a)
        a = op("pool", lambda e: e.affine_select(out=ltri[:, :], in_=ltri[:, :], compare_op=ALU.is_gt, fill=0.0,
                                                 base=0, pattern=[[-1, P]], channel_multiplier=1), a)
        state["last"] = a

        def bc(v, n=NBLK):
            return v.unsqueeze(1).to_broadcast([P, n, v.shape[1]])

        def bf(v, f=P):
            return v.unsqueeze(2).to_broadcast([P, v.shape[1], f])

        def flat(v):
            return v.rearrange("p a b -> p (a b)")

        PN = PS[:, 0:NPAD].rearrange("p (b f) -> p b f", f=P)

        def center(w, n, parts, c):
            step("dve", lambda e: e.tensor_reduce(small[0:parts, 6, c:c + 1], w, AX, ALU.add))
            step("dve", lambda e: e.tensor_scalar(small[0:parts, 7, c:c + 1], small[0:parts, 6, c:c + 1],
                                                  1.0 / n, None, ALU.mult))
            step("dve", lambda e: e.tensor_scalar(w, w, small[0:parts, 7, c:c + 1], None, ALU.subtract))

        def transposed(src, dst):
            def go(e):
                for b in range(NBLK):
                    ins = e.transpose(PN[:, b, :], src[:, b, :], ident[:, :])
                return ins
            step("pe", go)
            step("act", lambda e: e.activation(dst, PN, ACT.Copy))

        def product(pairs):
            def go(e):
                for b in range(NBLK):
                    for i, (t, w) in enumerate(pairs):
                        ins = e.matmul(PN[:, b, :], t[:, b, :], w, start=(i == 0), stop=(i == len(pairs) - 1))
                return ins
            step("pe", go)

        def table(xT, w, width, T, big):
            for b0 in range(0, NBLK, 13):
                nb_ = min(13, NBLK - b0)

                def go(e, b0=b0, nb_=nb_):
                    for b in range(nb_):
                        ins = e.matmul(PS[:, b * width:(b + 1) * width], xT[:, b0 + b, :], w, start=True, stop=True)
                    return ins
                step("pe", go)
                step("act", lambda e, b0=b0, nb_=nb_: e.activation(
                    flat(big)[:, b0 * width:(b0 + nb_) * width], PS[:, 0:nb_ * width], ACT.Copy))
            load([lambda e: e.dma_start(T.rearrange("(b p) d -> p b d", p=P), big)])

        def rstd_of(v, rs, n):
            step("dve", lambda e: e.tensor_scalar(v, v, 1.0 / n, EPS, ALU.mult, ALU.add))
            step("pool", lambda e: e.tensor_tensor(rs, v, mhalf[:, 0:NBLK], ALU.pow))

        def ln_affine(u, sq, g, b):
            step("dve", lambda e: e.tensor_tensor(sq, u, u, ALU.mult))
            step("dve", lambda e: e.tensor_reduce(small[:, 8, :], sq, AX, ALU.add))
            rstd_of(small[:, 8, :], small[:, 9, :], P)
            step("dve", lambda e: e.tensor_tensor(u, u, bf(small[:, 9, :]), ALU.mult))
            step("dve", lambda e: e.tensor_tensor(u, u, bc(g), ALU.mult))
            step("dve", lambda e: e.tensor_tensor(u, u, bc(b), ALU.add))

        def ln_plain(y, sq):
            step("dve", lambda e: e.tensor_reduce(small[:, 8, :], y, AX, ALU.add))
            step("dve", lambda e: e.tensor_scalar(small[:, 8, :], small[:, 8, :], 1.0 / P, None, ALU.mult))
            step("dve", lambda e: e.tensor_tensor(y, y, bf(small[:, 8, :]), ALU.subtract))
            step("dve", lambda e: e.tensor_tensor(sq, y, y, ALU.mult))
            step("dve", lambda e: e.tensor_reduce(small[:, 9, :], sq, AX, ALU.add))
            rstd_of(small[:, 9, :], small[:, 10, :], P)
            step("dve", lambda e: e.tensor_tensor(xn[:, :, :], y, bf(small[:, 10, :]), ALU.mult))

        def gather_ends(H, w, dst):
            load([lambda e, b=b: e.indirect_dma_start(
                out=dst[:, b, :], out_offset=None, in_=H,
                in_offset=bass.IndirectOffsetOnAxis(ap=endI[:, b:b + 1], axis=0)) for b in range(NBLK)],
                "pool", s_g)

        ring_sems = {}

        def ring(name, n):
            if name not in ring_sems:
                ring_sems[name] = [Q.sem(f"{name}{i}") for i in range(n)]
            return ring_sems[name]

        def gather(sems, b, T, idx, dst, *after):
            s = sems[b % len(sems)]
            for c in range(CB):
                tok = dma("pool", s, lambda e, c=c: e.indirect_dma_start(
                    out=dst[:, c, :], out_offset=None, in_=T,
                    in_offset=bass.IndirectOffsetOnAxis(ap=idx[:, CB * b + c:CB * b + c + 1], axis=0)), *after)
            return tok

        def pipeline(stages):
            last = max(lag for lag, _ in stages)
            for i in range(NBAT + last):
                for lag, fn in stages:
                    if 0 <= i - lag < NBAT:
                        fn(i - lag)

        def ident4(n):
            return ident[:, :].unsqueeze(1).to_broadcast([P, n, P])

        gs_sem, gd_sem = ring("gs", 6), ring("gd", 4)
        e_sem, s_sem, w_sem, k_sem = ring("le", 2), ring("lsr", 3), ring("lw", 3), ring("lk", 4)
        o_sem, tab_sem, st_sem = ring("so", 3), ring("tb", KT), ring("sst", 8)
        tk = {}

        def g0(name, b):
            return tk.get((name, b))

        def put(name, b, tok):
            tk[(name, b)] = tok
            return tok

        def grow(v, g):
            return row(v[g * GE:(g + 1) * GE], GE)

        def backend(b, nh, psT, psB, s, Ob, H, rowsR, after_T, op0, op1, init, srcs=None):
            g, h0 = b // 2, (b % 2) * CB * P
            kr = rowsR[g % 4][:, h0:h0 + CB * P]

            def scan(e):
                for h in range(nh):
                    ins = e.tensor_tensor_scan(s[b % 2][:, h, :], kr, psT[h] if srcs is None else srcs[h],
                                               s[(b - 1) % 2][:, h, CB * P - 1:CB * P] if b else init, op0, op1)
                return ins
            put("scan", b, op("dve", scan, after_T, g0("kR", g), g0("scan", b - 1), g0("B", b - 2)))

        def backend2(b, nh, psB, s, Ob, H):
            def B(e):
                for c in range(CB):
                    for h in range(nh):
                        ins = e.transpose(psB[:, (c * nh + h) * P:(c * nh + h + 1) * P],
                                          s[b % 2][:, h, c * P:(c + 1) * P], ident[:, :])
                return ins
            put("B", b, op("pe", B, g0("scan", b), g0("O", b - 1)))
            put("O", b, op("act", lambda e: e.activation(flat(Ob[b % 3]), psB, ACT.Copy),
                           g0("B", b), g0("so", b - 3)))
            put("so", b, dma("sp", o_sem[b % 3], lambda e: e.dma_start(
                H[b * CB * P:(b + 1) * CB * P, :].rearrange("(c p) f -> p c f", p=P), Ob[b % 3]), g0("O", b)))

        def rows_load(b, rowsR, R):
            if b % 2 == 0:
                g = b // 2
                put("kR", g, dma("sp", k_sem[g % 4], lambda e: e.dma_start(rowsR[g % 4], grow(R, g)),
                                 g0("scan", b - 7)))

        v_ = vec[:, :, :]
        gsem = gs_sem

        def edge_lists():
            dI = arena.get(NCH, dt=I32)
            dP = arena.get(NCH, dt=I32)
            sI = arena.get(NCH, dt=I32)
            wI = arena.get(NCH)
            dFt = arena.get(NCH)
            sFt = arena.get(NCH)
            kt = arena.get(NCH)
            kb = arena.get(NCH, dt=BF16)
            nb = arena.get(NCH, dt=BF16)
            samp = arena.get(SUB)
            rows = arena.get(3, 7, P)
            sampB = arena.get(NSAMP)
            junk = arena.get(NSAMP)
            zero = arena.get(3 * TR)
            sub = arena.get(NBLK, SUB)
            onep = arena.get(1)

            load([
                lambda e: e.dma_start(dI, A["dst"][1:EP + 1].rearrange("(p j) -> p j", j=NCH)),
                lambda e: e.dma_start(dP, A["dst"][0:EP].rearrange("(p j) -> p j", j=NCH)),
                lambda e: e.dma_start(sI, A["src"].rearrange("(p j) -> p j", j=NCH)),
                lambda e: e.dma_start(wI, A["edge_weight"].rearrange("(p j) -> p j", j=NCH)),
                lambda e: e.dma_start(xn[:, :, :], A["x"].rearrange("(b p) d -> p b d", p=P)),
                lambda e: e.dma_start(beta[:, :], row(A["L1_gnn_beta"], 1)),
                lambda e: e.dma_start(epsc[:, :], row(A["L1_gnn_eps"], 1)),
            ])

            def conv(e):
                e.tensor_copy(dFt, dI)
                e.tensor_copy(sFt, sI)
                e.tensor_tensor(kt, dI, dP, ALU.is_equal)
                e.memset(zero, 0.0)
                e.memset(onep, 0.0)
                e.memset(samp, 0.0)
                return e.tensor_scalar(wI, wI, beta[:, 0:1], None, ALU.mult)
            step("dve", conv)

            def conv2(e):
                e.tensor_copy(kb, kt)
                e.tensor_copy(samp, dFt.rearrange("p (a b) -> p a b", b=SUB)[:, :, 0])
                return e.tensor_scalar(nb, kt, -1.0, BIG, ALU.add, ALU.mult)
            step("dve", conv2)

            for k in range(KT):
                dma("sp", s_init, lambda e, k=k: e.dma_start(
                    tabs[k].rearrange("(p r) c -> p (r c)", p=P), zero[:, 0:TR // P * XW]), state["last"])
            load([
                lambda e: e.dma_start(dF.rearrange("(p j) -> p j", j=NCH), dFt),
                lambda e: e.dma_start(sF.rearrange("(p j) -> p j", j=NCH), sFt),
                lambda e: e.dma_start(wF.rearrange("(p j) -> p j", j=NCH), wI),
                lambda e: e.dma_start(keepR.rearrange("(p j) -> p j", j=NCH), kb),
                lambda e: e.dma_start(negR.rearrange("(p j) -> p j", j=NCH), nb),
                lambda e: e.dma_start(sampR.rearrange("(p j) -> p j", j=SUB), samp),
            ])
            zt = ("s_init", Q.count["s_init"])
            step("dve", lambda e: e.memset(zero.rearrange("p (a two) -> p a two", two=2)[:, :, 0], -BIG))
            Q.wait("dve", [zt])
            step("dve", lambda e: e.memset(zero.rearrange("p (a two) -> p a two", two=2)[:, :, 0], -BIG))
            SW = NCH * TR * 2 // P
            sv = stat.rearrange("(p r) c -> p (r c)", p=P)
            o = 0
            while o < SW:
                n = min(3 * TR // 2 * 2, SW - o)
                dma("act", s_init, lambda e, o=o, n=n: e.dma_start(sv[:, o:o + n], zero[:, 0:n]), state["last"])
                o += n
            load([lambda e, i=i, t=t: e.dma_start(rows[0:112, i, :, :], t.rearrange("(t q p) -> q t p", q=112, p=P))
                  for i, t in enumerate((sF, dF, wF))] +
                 [lambda e: e.dma_start(sampB, row(sampR, NSAMP))])

            def tr_lists(e):
                for i in range(3):
                    for t in range(7):
                        o = 1024 * i + 112 * t + (64 if t >= 4 else 0)
                        ins = e.transpose(PS[:, o:o + 112], rows[0:112, i, t, :], ident[0:112, 0:112])
                return ins
            step("pe", tr_lists)

            def ev_lists(e):
                for i, d in enumerate((srcF, dstI, eF)):
                    e.tensor_copy(d[:, 0:448], PS[:, 1024 * i:1024 * i + 448])
                    e.tensor_copy(d[:, 448:784], PS[:, 1024 * i + 512:1024 * i + 848])
                    if i == 0:
                        e.tensor_copy(srcI[:, 0:448], PS[:, 0:448])
                        ins = e.tensor_copy(srcI[:, 448:784], PS[:, 512:848])
                return ins
            step("dve", ev_lists)
            for b in range(NBLK):
                step("dve", lambda e, b=b: e.tensor_scalar(junk, sampB, nodeid[:, b:b + 1], 0.0, ALU.is_le, ALU.add,
                                                           accum_out=small[:, 0, b:b + 1]))
            kI = small[:, 1, :].bitcast(I32)
            step("dve", lambda e: e.tensor_scalar(small[:, 2, :], small[:, 0, :], -1.0, 0.0, ALU.add, ALU.max))
            step("dve", lambda e: e.tensor_copy(kI, small[:, 2, :]))
            dF28 = dF.rearrange("(s i) -> s i", i=SUB)
            load([lambda e, b=b: e.indirect_dma_start(
                out=sub[:, b, :], out_offset=None, in_=dF28,
                in_offset=bass.IndirectOffsetOnAxis(ap=kI[:, b:b + 1], axis=0)) for b in range(NBLK)],
                "pool", s_g)

            def cnt28(e):
                for b in range(NBLK):
                    ins = e.tensor_scalar(junk[:, SUB * b:SUB * b + SUB], sub[:, b, :], nodeid[:, b:b + 1], 0.0, ALU.is_le, ALU.add,
                                          accum_out=small[:, 3, b:b + 1])
                return ins
            step("dve", cnt28)
            step("dve", lambda e: e.scalar_tensor_tensor(out=small[:, 4, :], in0=small[:, 2, :], scalar=float(SUB),
                                                         in1=small[:, 3, :], op0=ALU.mult, op1=ALU.add))
            step("dve", lambda e: e.tensor_scalar(endI[:, :], small[:, 4, :], -1.0, 0.0, ALU.add, ALU.max))
            with nc.allow_non_contiguous_dma(reason="3200 counts, once"):
                load([lambda e: e.dma_start(ubR[0:1].rearrange("(a b) -> a b", a=1), onep[0:1, 0:1]),
                      lambda e: e.dma_start(ubR[1:NPAD + 1].rearrange("(b p) -> p b", p=P), small[:, 4, :],
                                            allow_slow_non_contiguous=True)])
                load([lambda e: e.dma_start(small[:, 5, :], ubR[0:NPAD].rearrange("(b p) -> p b", p=P),
                                            allow_slow_non_contiguous=True)])
            step("dve", lambda e: e.tensor_tensor(deg[:, :], small[:, 4, :], small[:, 5, :], ALU.subtract))
            step("dve", lambda e: e.tensor_scalar(has[:, :], deg[:, :], 0.5, None, ALU.is_gt))

        def L0_tables():
            Q.barrier()
            arena.reset()
            state["last"] = None
            xT = arena.get(NBLK, P)
            big = arena.get(NBLK, 2 * P)
            w1 = A["L0_gnn_msg_w1"]
            load([lambda e: e.dma_start(W1ab[:, 0:P], w1[0:P, :]),
                  lambda e: e.dma_start(W1ab[:, P:2 * P], w1[P:2 * P, :]),
                  lambda e: e.dma_start(We[0:64, :], w1[2 * P:2 * P + 64, :]),
                  lambda e: e.dma_start(We[64:65, :], A["L0_gnn_msg_b1"].rearrange("(a n) -> a n", a=1)),
                  lambda e: e.dma_start(cols[:, 0:1], A["L0_gnn_ln1_g"].rearrange("(n a) -> n a", a=1)),
                  lambda e: e.dma_start(cols[:, 1:2], A["L0_gnn_ln1_b"].rearrange("(n a) -> n a", a=1))])
            center(W1ab[:, 0:P], P, P, 0)
            center(W1ab[:, P:2 * P], P, P, 1)
            center(We[0:65, :], P, 65, 2)
            transposed(xn, xT)
            table(xT, W1ab[:, :], 2 * P, T0, big)

        def L0_edges():
            Q.barrier()
            arena.reset()
            Gs = [arena.get(CB, 2 * P) for _ in range(4)]
            Gd = [arena.get(CB, 2 * P) for _ in range(4)]
            eT = [arena.get(GE) for _ in range(2)]
            sR = [arena.get(GE) for _ in range(3)]
            wR = [arena.get(GE) for _ in range(3)]
            kR = [arena.get(GE, dt=BF16) for _ in range(4)]
            t0 = [arena.get(CB, 2, P) for _ in range(3)]
            Dg = [arena.get(2 * CB, P) for _ in range(2)]
            r1 = [arena.get(CB * P) for _ in range(2)]
            r2 = [arena.get(CB, P) for _ in range(2)]
            s1 = [arena.get(CB * P) for _ in range(2)]
            Ob = [arena.get(CB, P) for _ in range(3)]
            R2 = [arena.get(CB, P) for _ in range(2)]
            Sm = [arena.get(CB, P) for _ in range(4)]
            Vm = [arena.get(CB, P) for _ in range(3)]
            jk = arena.get(CB, P)
            jl = arena.get(CB, P)
            ja = arena.get(2 * CB, P, dt=BF16)
            X2 = [arena.get(CB, XW) for _ in range(6)]
            cb = [arena.get(CB) for _ in range(8)]
            aF = [arena.get(CB) for _ in range(2)]
            mF = [arena.get(CB) for _ in range(2)]
            iA = [arena.get(CB, dt=I32) for _ in range(8)]
            iT = [arena.get(CB, dt=I32) for _ in range(8)]
            var = [arena.get(2 * CB) for _ in range(4)]
            rst = [arena.get(2 * CB) for _ in range(4)]
            mm = [arena.get(CB) for _ in range(4)]
            ST = [arena.get(CB, 2) for _ in range(8)]
            dT = arena.get(NCH)
            coff = arena.get(NCH)

            a = op("dve", lambda e: e.tensor_scalar(dT, srcF[:, :], pcol[:, 0:1], -1.0, ALU.subtract, ALU.mult))
            op("pool", lambda e: e.iota(coff, [[TR, NCH]], base=0, channel_multiplier=0,
                                        allow_small_or_imprecise_dtypes=True))
            for x2 in X2:
                op("dve", lambda e, x2=x2: e.memset(x2[:, :, P:XW], 0.0))
            for t in eT:
                a = op("dve", lambda e, t=t: e.memset(t[64:65, :], 1.0))
            Q.barrier()

            def L0_load(b):
                if b % 2 == 0:
                    g = b // 2
                    put("eT", g, dma("sp", e_sem[g % 2], lambda e: e.dma_start(
                        eT[g % 2][0:64, :], A["ea64T"][:, g * GE:(g + 1) * GE]), g0("C", b - 3)))
                    put("sR", g, dma("sp", s_sem[g % 3], lambda e: e.dma_start(sR[g % 3], grow(sF, g)), g0("S", b - 5)))
                    put("wR", g, dma("sp", w_sem[g % 3], lambda e: e.dma_start(wR[g % 3], grow(wF, g)), g0("S", b - 5)))
                    put("kR", g, dma("sp", k_sem[g % 4], lambda e: e.dma_start(kR[g % 4], grow(keepR, g)),
                                     g0("scan", b - 7)))
                put("gs", b, gather(gs_sem[0:4], b, T0, srcI, Gs[b % 4], g0("t1", b - 4)))
                put("gd", b, gather(gd_sem, b, T0, dstI, Gd[b % 4], g0("t1", b - 4)))

            def L0_front(b):
                g, h = b // 2, b % 2
                h0 = h * CB * P

                def C(e):
                    for c in range(CB):
                        ins = e.matmul(bank(0)[:, c * P:(c + 1) * P], eT[g % 2][0:65, h0 + c * P:h0 + (c + 1) * P],
                                       We[0:65, :], start=True, stop=True)
                    return ins
                put("C", b, op("pe", C, g0("eT", g), g0("t2", b - 1)))
                t, s, d = t0[b % 3], Gs[b % 4].rearrange("p c (h f) -> p c h f", h=2), \
                    Gd[b % 4].rearrange("p c (h f) -> p c h f", h=2)

                def t1(e):
                    e.tensor_tensor(t[:, :, 0, :], s[:, :, 0, :], d[:, :, 1, :], ALU.add)
                    return e.tensor_tensor(t[:, :, 1, :], s[:, :, 1, :], d[:, :, 0, :], ALU.add)
                put("t1", b, op("dve", t1, g0("gs", b), g0("gd", b), g0("T", b - 3), g0("sq", b - 3)))
                pc = bank(0).rearrange("p (c f) -> p c f", f=P).unsqueeze(2).to_broadcast([P, CB, 2, P])
                put("t2", b, op("dve", lambda e: e.tensor_tensor(t, t, pc, ALU.add), g0("t1", b), g0("C", b)))
                sr, wr = sR[g % 3], wR[g % 3]

                def S(e):
                    for c in range(CB):
                        k = CB * b + c
                        r = slice(h0 + c * P, h0 + (c + 1) * P)
                        e.tensor_scalar(Sm[b % 4][:, c, :], sr[:, r], srcF[:, k:k + 1], 0.0, ALU.is_equal, ALU.add,
                                        accum_out=X2[b % 6][:, c, P:P + 1])
                        ins = e.tensor_scalar(Vm[b % 3][:, c, :], sr[:, r], srcF[:, k:k + 1], -BIG,
                                              ALU.not_equal, ALU.mult)
                    return ins
                put("S1", b, op("dve", S, g0("sR", g), g0("SS", b - 4), g0("sc", b - 6), g0("ex", b - 3)))

                def S2(e):
                    for c in range(CB):
                        r = slice(h0 + c * P, h0 + (c + 1) * P)
                        e.tensor_tensor_reduce(jl[:, c, :], Sm[b % 4][:, c, :], ltri[:, :], 1.0, 0.0, ALU.mult, ALU.add,
                                               cb[b % 8][:, c:c + 1])
                        ins = e.tensor_tensor_reduce(Vm[b % 3][:, c, :], Vm[b % 3][:, c, :], wr[:, r], 1.0, -BIG,
                                                     ALU.add, ALU.max, ST[b % 8][:, c, 0:1])
                    return ins
                put("S", b, op("dve", S2, g0("S1", b), g0("wR", g), g0("sst", b - 8), g0("S", b - 1)))
                sl = slice(CB * b, CB * b + CB)

                def S3(e):
                    e.tensor_scalar(mm[b % 4], ST[b % 8][:, :, 0], -1.0, None, ALU.mult)
                    return e.scalar_tensor_tensor(out=mF[b % 2], in0=cb[b % 8], scalar=0.5, in1=dT[:, sl],
                                                  op0=ALU.is_gt, op1=ALU.mult)
                put("S3", b, op("dve", S3, g0("S", b), g0("ex", b - 4)))
                put("S4", b, op("dve", lambda e: e.tensor_tensor(aF[b % 2], mF[b % 2], srcF[:, sl], ALU.add),
                                g0("S3", b)))

                def S5(e):
                    e.tensor_copy(iA[b % 8], aF[b % 2])
                    return e.tensor_tensor(iT[b % 8], aF[b % 2], coff[:, sl], ALU.add)
                put("S5", b, op("dve", S5, g0("S4", b), g0("sc", b - 8), g0("sst", b - 8)))

                def sq(e):
                    for c in range(CB):
                        for hh in range(2):
                            ins = e.activation(ja[:, 2 * c + hh, :], t[:, c, hh, :], ACT.Square,
                                               accum_out=var[b % 4][:, 2 * c + hh:2 * c + hh + 1])
                    return ins
                put("sq", b, op("act", sq, g0("t2", b), g0("D", b - 4), g0("sq", b - 1)))
                put("v", b, op("dve", lambda e: e.tensor_scalar(var[b % 4], var[b % 4], 1.0 / P, EPS,
                                                                ALU.mult, ALU.add), g0("sq", b)))

                def ex(e):
                    for c in range(CB):
                        ins = e.activation(Vm[b % 3][:, c, :], Vm[b % 3][:, c, :], ACT.Exp, bias=mm[b % 4][:, c:c + 1],
                                           accum_out=ST[b % 8][:, c, 1:2])
                    return ins
                put("ex", b, op("act", ex, g0("S3", b), g0("S", b)))

            def L0_mid(b):
                put("pow", b, op("pool", lambda e: e.tensor_tensor(rst[b % 4], var[b % 4], mhalf[:, 0:2 * CB], ALU.pow),
                                 g0("v", b), g0("D", b - 4)))
                for c in range(CB):
                    tok = dma("pool", st_sem[b % 8], lambda e, c=c: e.indirect_dma_start(
                        out=stat, out_offset=bass.IndirectOffsetOnAxis(ap=iT[b % 8][:, c:c + 1], axis=0),
                        in_=ST[b % 8][:, c, :], in_offset=None), g0("ex", b), g0("S5", b))
                put("sst", b, tok)

            def L0_diag(b):
                g, h0 = b // 2, (b % 2) * CB * P
                put("D", b, op("dve", lambda e: e.tensor_tensor(Dg[b % 2], ident4(2 * CB), bf(rst[b % 4]), ALU.mult),
                               g0("pow", b), g0("T", b - 2)))
                t = t0[b % 3]

                def T(e):
                    for c in range(CB):
                        for hh in range(2):
                            ins = e.matmul(bank(1 + hh)[:, c * P:(c + 1) * P], t[:, c, hh, :],
                                           Dg[b % 2][:, 2 * c + hh, :], start=True, stop=True)
                    return ins
                put("T", b, op("pe", T, g0("D", b), g0("r", b - 1)))

                def r(e):
                    e.activation(r1[b % 2], bank(1), ACT.Relu, bias=cols[:, 1:2], scale=cols[:, 0:1])
                    return e.activation(flat(r2[b % 2]), bank(2), ACT.Relu, bias=cols[:, 1:2], scale=cols[:, 0:1])
                put("r", b, op("act", r, g0("T", b), g0("scan", b - 2), g0("B", b - 2)))
                put("scan", b, op("dve", lambda e: e.tensor_tensor_scan(
                    s1[b % 2], kR[g % 4][:, h0:h0 + CB * P], r1[b % 2],
                    s1[(b - 1) % 2][:, CB * P - 1:CB * P] if b else 0.0, ALU.mult, ALU.add),
                    g0("r", b), g0("kR", g), g0("scan", b - 1), g0("B", b - 2)))

            def L0_back(b):
                def B(e):
                    for c in range(CB):
                        e.transpose(bank(3)[:, c * P:(c + 1) * P], s1[b % 2][:, c * P:(c + 1) * P], ident[:, :])
                    for c in range(CB):
                        ins = e.transpose(bank(4)[:, c * P:(c + 1) * P], r2[b % 2][:, c, :], ident[:, :])
                    return ins
                put("B", b, op("pe", B, g0("scan", b), g0("r", b), g0("O", b - 1), g0("R2", b - 1)))
                put("O", b, op("act", lambda e: e.activation(flat(Ob[b % 3]), bank(3), ACT.Copy),
                               g0("B", b), g0("so", b - 3)))
                put("R2", b, op("act", lambda e: e.activation(flat(R2[b % 2]), bank(4), ACT.Copy),
                                g0("B", b), g0("SS", b - 2)))
                put("so", b, dma("sp", o_sem[b % 3], lambda e: e.dma_start(
                    H0[b * CB * P:(b + 1) * CB * P, :].rearrange("(c p) f -> p c f", p=P), Ob[b % 3]), g0("O", b)))

                def SS(e):
                    for c in range(CB):
                        ins = e.matmul(bank(5)[:, c * P:(c + 1) * P], Sm[b % 4][:, c, :], R2[b % 2][:, c, :],
                                       start=True, stop=True)
                    return ins
                put("SS", b, op("pe", SS, g0("R2", b), g0("S1", b), g0("X", b - 1)))
                put("X", b, op("act", lambda e: e.activation(
                    X2[b % 6][:, :, 0:P], bank(5).rearrange("p (c f) -> p c f", f=P), ACT.Copy),
                    g0("SS", b), g0("sc", b - 6)))

            def L0_scatter(b):
                toks = []
                for c in range(CB):
                    k = CB * b + c
                    prev = tk.get(("tab", k - KT))
                    tok = dma("pool", tab_sem[k % KT], lambda e, c=c, k=k: e.indirect_dma_start(
                        out=tabs[k % KT], out_offset=bass.IndirectOffsetOnAxis(ap=iA[b % 8][:, c:c + 1], axis=0),
                        in_=X2[b % 6][:, c, :], in_offset=None, compute_op=ALU.add), g0("X", b), g0("S5", b), prev)
                    put("tab", k, tok)
                    toks.append(tok)
                put("sc", b, toks)

            pipeline([(6, L0_scatter), (5, L0_back), (4, L0_diag), (3, L0_mid), (2, L0_front), (0, L0_load)])

        def L0_nodes():
            Q.barrier()
            arena.reset()
            state["last"] = None
            tk.clear()
            F = arena.get(NBLK, P)
            Y = arena.get(NBLK, P)
            Z = arena.get(NBLK, P)
            tb = [arena.get(NBLK, XW) for _ in range(2)]
            xT = arena.get(NBLK, P)
            aT = arena.get(NBLK, P)
            load([lambda e: e.dma_start(wA[:, 0:P], A["L0_gnn_msg_w2"][:, :]),
                  lambda e: e.dma_start(wA[:, P:2 * P], A["L0_gnn_upd_w2"][:, :]),
                  lambda e: e.dma_start(wB[:, 0:P], A["L0_gnn_upd_w1"][0:P, :]),
                  lambda e: e.dma_start(wB[:, P:2 * P], A["L0_gnn_upd_w1"][P:2 * P, :])] +
                 [lambda e, i=i, n=n: e.dma_start(v_[:, i, 0:P], row(A[n], P)) for i, n in enumerate(
                     ("L0_gnn_msg_b2", "L0_gnn_upd_b1", "L0_gnn_ln2_g", "L0_gnn_ln2_b", "L0_gnn_upd_b2"))])
            center(wB[:, 0:P], P, P, 0)
            center(wB[:, P:2 * P], P, P, 1)
            center(v_[:, 1, 0:P], P, P, 2)
            gather_ends(H0, P, F)
            step("dve", lambda e: e.tensor_tensor(F, F, bf(has[:, :]), ALU.mult))
            step("dve", lambda e: e.tensor_copy(small[:, 11, :], deg[:, :]))
            tbs = ring("tbl", 2)
            adds = {}
            for k in range(KT):
                lt = dma("sp", tbs[k % 2], lambda e, k=k: e.dma_start(
                    tb[k % 2], tabs[k][0:NPAD, :].rearrange("(b p) d -> p b d", p=P)), adds.get(k - 2))

                def acc(e, k=k):
                    e.tensor_tensor(F, F, tb[k % 2][:, :, 0:P], ALU.add)
                    return e.tensor_tensor(small[:, 11, :], small[:, 11, :], tb[k % 2][:, :, P], ALU.add)
                adds[k] = state["last"] = op("dve", acc, state["last"], lt)
            transposed(F, aT)
            product([(aT, wA[:, 0:P])])
            step("dve", lambda e: e.tensor_tensor(Y, bc(v_[:, 0, 0:P]), bf(small[:, 11, :]), ALU.mult))
            step("dve", lambda e: e.tensor_tensor(Y, Y, PN, ALU.add))
            transposed(Y, aT)
            transposed(xn, xT)
            product([(xT, wB[:, 0:P]), (aT, wB[:, P:2 * P])])
            step("dve", lambda e: e.tensor_tensor(Y, PN, bc(v_[:, 1, 0:P]), ALU.add))
            ln_affine(Y, Z, v_[:, 2, 0:P], v_[:, 3, 0:P])
            step("dve", lambda e: e.tensor_scalar(Y, Y, 0.0, None, ALU.max))
            transposed(Y, aT)
            product([(aT, wA[:, P:2 * P])])
            step("dve", lambda e: e.tensor_tensor(Y, PN, bc(v_[:, 4, 0:P]), ALU.add))
            step("dve", lambda e: e.scalar_tensor_tensor(out=Y, in0=xn[:, :, :], scalar=2.0, in1=Y,
                                                         op0=ALU.mult, op1=ALU.add))
            ln_plain(Y, Z)

        def L1_statistics():
            Q.barrier()
            arena.reset()
            state["last"] = None
            NT = 7
            SP_ = NCH // NT
            stt = [arena.get(2 * TR) for _ in range(2)]
            Mp = arena.get(TR)
            Sp = arena.get(TR)
            dd = arena.get(TR)
            Mt = arena.get(NBLK, SP_)
            statv = stat.rearrange("(t q n) c -> t q (n c)", q=SP_, n=TR)
            sls = ring("sls", 2)
            q_ = slice(0, SP_)

            def two(v):
                return v.rearrange("p (n c) -> p n c", c=2)
            use = {}
            for ps_ in range(2):
                for t in range(NT):
                    i = ps_ * NT + t
                    lt = dma("sp", sls[i % 2], lambda e, t=t, i=i: e.dma_start(stt[i % 2][q_, :], statv[t]),
                             use.get(i - 2))
                    m, s = two(stt[i % 2])[q_, :, 0], two(stt[i % 2])[q_, :, 1]
                    if ps_ == 0:
                        if t == 0:
                            step_tok = op("dve", lambda e, m=m: e.tensor_copy(Mp[q_, :], m), state["last"], lt)
                        else:
                            step_tok = op("dve", lambda e, m=m: e.tensor_tensor(Mp[q_, :], Mp[q_, :], m, ALU.max),
                                          state["last"], lt)
                        use[i] = state["last"] = step_tok
                    else:
                        state["last"] = op("dve", lambda e, m=m: e.tensor_tensor(dd[q_, :], m, Mp[q_, :], ALU.subtract),
                                           state["last"], lt)
                        step("act", lambda e: e.activation(dd[q_, :], dd[q_, :], ACT.Exp))
                        use[i] = step("dve", lambda e, s=s, t=t: e.tensor_tensor(dd[q_, :] if t else Sp[q_, :],
                                                                                dd[q_, :], s, ALU.mult))
                        if t:
                            use[i] = step("dve", lambda e: e.tensor_tensor(Sp[q_, :], Sp[q_, :], dd[q_, :], ALU.add))
            PM = PS[:, 0:NBLK * P].rearrange("p (b f) -> p b f", f=P)[:, :, 0:SP_]

            def trM(src):
                def go(e):
                    for b in range(NBLK):
                        ins = e.transpose(PM[:, b, :], src[q_, b * P:(b + 1) * P], ident[q_, q_])
                    return ins
                return go
            step("pe", trM(Mp))
            step("dve", lambda e: e.tensor_reduce(Mx[:, :], PM, AX, ALU.max))
            step("dve", lambda e: e.tensor_tensor(Mt, PM, bf(Mx[:, :], SP_), ALU.subtract))
            step("act", lambda e: e.activation(Mt, Mt, ACT.Exp))
            step("pe", trM(Sp))
            step("dve", lambda e: e.tensor_tensor(Mt, Mt, PM, ALU.mult))
            step("dve", lambda e: e.tensor_reduce(Sx[:, :], Mt, AX, ALU.add))

        def L1_table():
            Q.barrier()
            arena.reset()
            Z = arena.get(NBLK, P)
            tX = arena.get(NBLK, XW)
            step("dve", lambda e: e.tensor_tensor(Z, xn[:, :, :], xn[:, :, :], ALU.mult))
            step("dve", lambda e: e.tensor_reduce(small[:, 0, :], Z, AX, ALU.add))
            step("dve", lambda e: e.tensor_scalar(small[:, 1, :], mhalf[:, 0:NBLK], -1.0, None, ALU.mult))
            step("pool", lambda e: e.tensor_tensor(small[:, 2, :], small[:, 0, :], small[:, 1, :], ALU.pow))
            step("dve", lambda e: e.tensor_scalar(small[:, 2, :], small[:, 2, :], 1e-12, None, ALU.max))
            step("dve", lambda e: e.tensor_scalar(small[:, 3, :], Sx[:, :], 0.5, None, ALU.is_lt))
            step("dve", lambda e: e.tensor_tensor(small[:, 3, :], small[:, 3, :], Sx[:, :], ALU.add))
            step("dve", lambda e: e.tensor_tensor(small[:, 2, :], small[:, 2, :], small[:, 3, :], ALU.mult))
            step("dve", lambda e: e.reciprocal(small[:, 4, :], small[:, 2, :]))
            step("dve", lambda e: e.tensor_tensor(tX[:, :, 0:P], xn[:, :, :], bf(small[:, 4, :]), ALU.mult))
            step("dve", lambda e: e.memset(tX[:, :, P + 1:XW], 0.0))
            step("dve", lambda e: e.tensor_copy(tX[:, :, P], Mx[:, :]))
            load([lambda e: e.dma_start(T1.rearrange("(b p) d -> p b d", p=P), tX)])

        def L1_edges():
            Q.barrier()
            arena.reset()
            tk.clear()
            G = [arena.get(CB, XW) for _ in range(6)]
            kR = [arena.get(GE, dt=BF16) for _ in range(4)]
            Dg = [arena.get(CB, P) for _ in range(2)]
            s1 = [arena.get(1, CB * P) for _ in range(2)]
            Ob = [arena.get(CB, P) for _ in range(3)]
            pm = [arena.get(CB) for _ in range(4)]
            pp = [arena.get(CB) for _ in range(4)]

            def L1_load(b):
                rows_load(b, kR, keepR)
                put("gs", b, gather(gsem, b, T1, srcI, G[b % 6], g0("T", b - 6)))

            def L1_front(b):
                put("pm", b, op("dve", lambda e: e.tensor_tensor(pm[b % 4], eF[:, CB * b:CB * b + CB],
                                                                 G[b % 6][:, :, P], ALU.subtract),
                                g0("gs", b), g0("p", b - 4)))
                put("p", b, op("act", lambda e: e.activation(pp[b % 4], pm[b % 4], ACT.Exp), g0("pm", b), g0("D", b - 4)))
                put("D", b, op("dve", lambda e: e.tensor_tensor(Dg[b % 2], ident4(CB), bf(pp[b % 4]), ALU.mult),
                               g0("p", b), g0("T", b - 2)))

                def T(e):
                    for c in range(CB):
                        ins = e.matmul(bank(b % 3)[:, c * P:(c + 1) * P], G[b % 6][:, c, 0:P], Dg[b % 2][:, c, :],
                                       start=True, stop=True)
                    return ins
                put("T", b, op("pe", T, g0("D", b), g0("gs", b), g0("scan", b - 3)))

            pipeline([(4, lambda b: backend2(b, 1, bank(3), s1, Ob, H1)),
                      (3, lambda b: backend(b, 1, [bank(b % 3)], None, s1, Ob, H1, kR, g0("T", b), ALU.mult, ALU.add, 0.0)),
                      (2, L1_front), (0, L1_load)])

        def L1_nodes_L2_table():
            Q.barrier()
            arena.reset()
            state["last"] = None
            tk.clear()
            F = arena.get(NBLK, P)
            Y = arena.get(NBLK, P)
            Z = arena.get(NBLK, P)
            xT = arena.get(NBLK, P)
            big = arena.get(NBLK, 2 * P)
            gather_ends(H1, P, F)
            step("dve", lambda e: e.tensor_tensor(F, F, bf(has[:, :]), ALU.mult))
            step("dve", lambda e: e.tensor_scalar(small[:, 0, 0:1], epsc[:, :], 2.0, None, ALU.add))
            step("dve", lambda e: e.scalar_tensor_tensor(out=Y, in0=xn[:, :, :], scalar=small[:, 0, 0:1], in1=F,
                                                         op0=ALU.mult, op1=ALU.add))
            ln_plain(Y, Z)

            W1 = A["L2_gnn_W1"]
            load([lambda e: e.dma_start(W1ab[:, :], W1[0:P, :]),
                  lambda e: e.dma_start(wC[0:32, :], W1[P:P + 32, :]),
                  lambda e: e.dma_start(wC[32:33, :], A["L2_gnn_b1"].rearrange("(a n) -> a n", a=1))] +
                 [lambda e, i=i, n=n: e.dma_start(cols[:, 2 * i:2 * i + 2], A[n].rearrange("(h n) -> n h", n=P),
                                                  allow_slow_non_contiguous=True)
                  for i, n in enumerate(("L2_gnn_g1", "L2_gnn_be1"))])
            center(W1ab[:, :], 2 * P, P, 0)
            center(wC[0:33, :], 2 * P, 33, 1)
            transposed(xn, xT)
            table(xT, W1ab[:, :], 2 * P, T2, big)

        def L2_edges():
            Q.barrier()
            arena.reset()
            tk.clear()
            G = [arena.get(CB, 2 * P) for _ in range(6)]
            kR = [arena.get(GE, dt=BF16) for _ in range(4)]
            eT = [arena.get(GE) for _ in range(2)]
            Dg = [arena.get(CB, P) for _ in range(2)]
            hT = [arena.get(2, CB * P) for _ in range(2)]
            s2 = [arena.get(2, CB * P) for _ in range(2)]
            Ob = [arena.get(CB, 2 * P) for _ in range(3)]
            ja = arena.get(CB, 2 * P, dt=BF16)
            var = [arena.get(CB) for _ in range(4)]
            rst = [arena.get(CB) for _ in range(4)]
            for t in eT:
                op("dve", lambda e, t=t: e.memset(t[32:33, :], 1.0))
            Q.barrier()

            def L2_load(b):
                rows_load(b, kR, keepR)
                if b % 2 == 0:
                    g = b // 2
                    put("eT", g, dma("sp", e_sem[g % 2], lambda e: e.dma_start(
                        eT[g % 2][0:32, :], A["ea32T"][:, g * GE:(g + 1) * GE]), g0("C", b - 3)))
                put("gs", b, gather(gsem, b, T2, srcI, G[b % 6], g0("T", b - 6)))

            psC = PS[:, 0:1024]

            def L2_front(b):
                g, h0 = b // 2, (b % 2) * CB * P

                def C(e):
                    for c in range(CB):
                        ins = e.matmul(psC[:, c * 2 * P:(c + 1) * 2 * P], eT[g % 2][0:33, h0 + c * P:h0 + (c + 1) * P],
                                       wC[0:33, :], start=True, stop=True)
                    return ins
                put("C", b, op("pe", C, g0("eT", g), g0("t", b - 1)))
                t = G[b % 6]
                put("t", b, op("dve", lambda e: e.tensor_tensor(flat(t), flat(t), psC, ALU.add), g0("gs", b), g0("C", b)))

                def sq(e):
                    for c in range(CB):
                        ins = e.activation(ja[:, c, :], t[:, c, :], ACT.Square, accum_out=var[b % 4][:, c:c + 1])
                    return ins
                put("sq", b, op("act", sq, g0("t", b), g0("D", b - 4), g0("sq", b - 1)))
                put("v", b, op("dve", lambda e: e.tensor_scalar(var[b % 4], var[b % 4], 1.0 / (2 * P), EPS,
                                                                ALU.mult, ALU.add), g0("sq", b)))

            def L2_mid(b):
                put("pow", b, op("pool", lambda e: e.tensor_tensor(rst[b % 4], var[b % 4], mhalf[:, 0:CB], ALU.pow),
                                 g0("v", b), g0("D", b - 4)))
                put("D", b, op("dve", lambda e: e.tensor_tensor(Dg[b % 2], ident4(CB), bf(rst[b % 4]), ALU.mult),
                               g0("pow", b), g0("T", b - 2)))
                t = G[b % 6]

                def T(e):
                    for h in range(2):
                        for c in range(CB):
                            ins = e.matmul(bank(2 + h)[:, c * P:(c + 1) * P], t[:, c, h * P:(h + 1) * P],
                                           Dg[b % 2][:, c, :], start=True, stop=True)
                    return ins
                put("T", b, op("pe", T, g0("D", b), g0("sq", b), g0("r", b - 1)))

                def r(e):
                    for h in range(2):
                        ins = e.activation(hT[b % 2][:, h, :], bank(2 + h), ACT.Gelu, bias=cols[:, 2 + h:3 + h],
                                           scale=cols[:, h:h + 1])
                    return ins
                put("r", b, op("act", r, g0("T", b), g0("scan", b - 2)))

            pipeline([(5, lambda b: backend2(b, 2, PS[:, 2048:3072], s2, Ob, H2)),
                      (4, lambda b: backend(b, 2, None, None, s2, Ob, H2, kR, g0("r", b), ALU.mult, ALU.add, 0.0,
                                            srcs=[hT[b % 2][:, 0, :], hT[b % 2][:, 1, :]])),
                      (3, L2_mid), (2, L2_front), (0, L2_load)])

        def L2_nodes_L3_table():
            Q.barrier()
            arena.reset()
            state["last"] = None
            tk.clear()
            F = arena.get(NBLK, 2 * P)
            Y = arena.get(NBLK, P)
            Z = arena.get(NBLK, P)
            xT = arena.get(NBLK, P)
            aT = arena.get(NBLK, P)
            bT = arena.get(NBLK, P)
            load([lambda e: e.dma_start(wA[:, 0:P], A["L2_gnn_W2"][0:P, :]),
                  lambda e: e.dma_start(wA[:, P:2 * P], A["L2_gnn_W2"][P:2 * P, :]),
                  lambda e: e.dma_start(wB[:, 0:P], A["L2_gnn_Wu"][0:P, :]),
                  lambda e: e.dma_start(wB[:, P:2 * P], A["L2_gnn_Wu"][P:2 * P, :]),
                  lambda e: e.dma_start(wC[:, 0:P], A["WaT"][:, :]),
                  lambda e: e.dma_start(wD[:, 0:P], A["WbT"][:, :])] +
                 [lambda e, i=i, n=n: e.dma_start(v_[:, i, 0:P], row(A[n], P)) for i, n in enumerate(
                     ("L2_gnn_b2", "L2_gnn_bu", "L2_gnn_gu", "L2_gnn_beu", "L3_gnn_b"))])
            center(wB[:, 0:P], P, P, 0)
            center(wB[:, P:2 * P], P, P, 1)
            center(v_[:, 1, 0:P], P, P, 2)
            step("dve", lambda e: e.tensor_tensor(wC[:, 0:P], wC[:, 0:P], wD[:, 0:P], ALU.subtract))
            gather_ends(H2, 2 * P, F)
            step("dve", lambda e: e.tensor_tensor(F, F, bf(has[:, :], 2 * P), ALU.mult))
            transposed(F[:, :, 0:P], aT)
            transposed(F[:, :, P:2 * P], bT)
            product([(aT, wA[:, 0:P]), (bT, wA[:, P:2 * P])])
            step("dve", lambda e: e.tensor_tensor(Y, bc(v_[:, 0, 0:P]), bf(deg[:, :]), ALU.mult))
            step("dve", lambda e: e.tensor_tensor(Y, Y, PN, ALU.add))
            transposed(Y, aT)
            transposed(xn, xT)
            product([(xT, wB[:, 0:P]), (aT, wB[:, P:2 * P])])
            step("dve", lambda e: e.tensor_tensor(Y, PN, bc(v_[:, 1, 0:P]), ALU.add))
            ln_affine(Y, Z, v_[:, 2, 0:P], v_[:, 3, 0:P])
            step("act", lambda e: e.activation(Y, Y, ACT.Gelu))
            step("dve", lambda e: e.scalar_tensor_tensor(out=Y, in0=xn[:, :, :], scalar=2.0, in1=Y,
                                                         op0=ALU.mult, op1=ALU.add))
            ln_plain(Y, Z)

            transposed(xn, xT)
            product([(xT, wD[:, 0:P])])
            step("act", lambda e: e.activation(Y, PN, ACT.Copy))
            load([lambda e: e.dma_start(T3.rearrange("(b p) d -> p b d", p=P), Y)])

        def L3_edges():
            Q.barrier()
            arena.reset()
            tk.clear()
            G = [arena.get(CB, P) for _ in range(6)]
            kR = [arena.get(GE, dt=BF16) for _ in range(4)]
            s1 = [arena.get(1, CB * P) for _ in range(2)]
            Ob = [arena.get(CB, P) for _ in range(3)]

            def L3_load(b):
                rows_load(b, kR, negR)
                put("gs", b, gather(gsem, b, T3, srcI, G[b % 6], g0("T", b - 6)))

            def L3_front(b):
                def T(e):
                    for c in range(CB):
                        ins = e.transpose(bank(b % 3)[:, c * P:(c + 1) * P], G[b % 6][:, c, :], ident[:, :])
                    return ins
                put("T", b, op("pe", T, g0("gs", b), g0("scan", b - 3)))

            pipeline([(4, lambda b: backend2(b, 1, bank(3), s1, Ob, H3)),
                      (3, lambda b: backend(b, 1, [bank(b % 3)], None, s1, Ob, H3, kR, g0("T", b), ALU.add, ALU.max, -BIG)),
                      (2, L3_front), (0, L3_load)])

        def L3_nodes():
            Q.barrier()
            arena.reset()
            state["last"] = None
            tk.clear()
            F = arena.get(NBLK, P)
            Y = arena.get(NBLK, P)
            Z = arena.get(NBLK, P)
            xT = arena.get(NBLK, P)
            gather_ends(H3, P, F)
            transposed(xn, xT)
            product([(xT, wC[:, 0:P])])
            step("dve", lambda e: e.tensor_tensor(Y, PN, bc(v_[:, 4, 0:P]), ALU.add))
            step("dve", lambda e: e.tensor_tensor(Y, Y, F, ALU.add))
            step("dve", lambda e: e.tensor_tensor(Y, Y, bf(has[:, :]), ALU.mult))
            step("dve", lambda e: e.tensor_tensor(Y, Y, xn[:, :, :], ALU.add))
            ln_plain(Y, Z)
            nf = N // P
            load([lambda e: e.dma_start(out[0:nf * P, :].rearrange("(b p) d -> p b d", p=P), xn[:, 0:nf, :]),
                  lambda e: e.dma_start(out[nf * P:N, :], xn[0:N - nf * P, nf, :])])
            Q.barrier()

        edge_lists()
        L0_tables()
        L0_edges()
        L0_nodes()
        L1_statistics()
        L1_table()
        L1_edges()
        L1_nodes_L2_table()
        L2_edges()
        L2_nodes_L3_table()
        L3_edges()
        L3_nodes()

        block = ctx.enter_context(nc.Block())

        @block.sync
        def _(e):
            for f in Q.q["sp"]:
                f(e)

        @block.tensor
        def _(e):
            for f in Q.q["pe"]:
                f(e)

        @block.vector
        def _(e):
            for f in Q.q["dve"]:
                f(e)

        @block.scalar
        def _(e):
            for f in Q.q["act"]:
                f(e)

        @block.gpsimd
        def _(e):
            for f in Q.q["pool"]:
                f(e)


def kernel(**inputs):
    import numpy as np
    import concourse.bacc as bacc
    from concourse.bass_utils import run_bass_kernel_spmd

    a = {k: np.asarray(v) for k, v in inputs.items()}

    def padded(v, n, fill):
        return np.concatenate([v, np.full((n - v.shape[0],) + v.shape[1:], fill, v.dtype)], 0)

    x = padded(a.pop("x"), NPAD, 0)
    src = padded(a.pop("src"), EP, DUMMY)
    dst = a.pop("dst")
    dst = np.concatenate([np.full((1,), -1, dst.dtype), padded(dst, EP, DUMMY)])
    ew = padded(a.pop("edge_weight"), EP, 0)
    e32 = np.ascontiguousarray(padded(a.pop("edge_attr_32"), EP, 0).T)
    e64 = np.ascontiguousarray(padded(a.pop("edge_attr_64"), EP, 0).T)
    W = a.pop("L3_gnn_W")
    arrays = {"x": x, "src": src, "dst": dst, "edge_weight": ew, "ea32T": e32, "ea64T": e64,
              "WaT": np.ascontiguousarray(W[:, 0:P].T), "WbT": np.ascontiguousarray(W[:, P:2 * P].T)}
    arrays.update(a)
    nc = bacc.Bacc("TRN2", target_bir_lowering=False, num_devices=1)
    feed, A = {}, {}
    for name, v in arrays.items():
        feed[f"in_{name}"] = np.ascontiguousarray(v)
        A[name] = nc.dram_tensor(f"in_{name}", v.shape, mybir.dt.from_np(v.dtype), kind="ExternalInput").ap()
    out = nc.dram_tensor("out_x", (N, P), F32, kind="ExternalOutput").ap()
    build(nc, A, out)
    r = run_bass_kernel_spmd(nc, [feed], core_ids=[0])
    return r.results[0]["out_x"]
```

```python
import concourse.bass as bass
from concourse import mybir
from contextlib import ExitStack

P = 128
N = 3125
NBLK = 25
NPAD = NBLK * P
DUMMY = NPAD - 1
E = 100000
NCH = 784
EP = NCH * P
CB = 4
NBAT = NCH // CB
NG = NBAT // 2
GE = 2 * CB * P
TR = NPAD + P
KT = 4
XW = 132
SUB = 28
NSAMP = NCH * P // SUB
BIG = 3.0e38
MAGIC = float(0x5f3759df)
EPS = 1e-5

F32 = mybir.dt.float32
BF16 = mybir.dt.bfloat16
I32 = mybir.dt.int32
ALU = mybir.AluOpType
ACT = mybir.ActivationFunctionType
AX = mybir.AxisListType.X


class Queues:

    def __init__(self, nc, ctx):
        self.nc, self.ctx = nc, ctx
        self.q = {n: [] for n in ("pe", "dve", "act", "pool", "sp")}
        self.seen = {n: {} for n in self.q}
        self.count = {}
        self.sems = {}
        self.own = {n: self.sem("s_" + n) for n in self.q}

    def sem(self, name):
        s = self.ctx.enter_context(self.nc.semaphore(name))
        self.sems[name] = s
        self.count[name] = 0
        return name

    def wait(self, eng, after):
        for tok in after:
            if tok is None:
                continue
            if isinstance(tok, list):
                self.wait(eng, tok)
                continue
            name, v = tok
            if self.seen[eng].get(name, 0) < v:
                self.seen[eng][name] = v
                s = self.sems[name]
                self.q[eng].append(lambda e, s=s, v=v: e.wait_ge(s, v))

    def op(self, eng, fn, *after):
        self.wait(eng, after)
        name = self.own[eng]
        self.count[name] += 1
        s = self.sems[name]
        self.q[eng].append(lambda e: fn(e).then_inc(s, 1))
        return (name, self.count[name])

    def dma(self, eng, name, fn, *after):
        self.wait(eng, after)
        self.count[name] += 16
        s = self.sems[name]
        self.q[eng].append(lambda e: fn(e).then_inc(s, 16))
        return (name, self.count[name])

    def barrier(self):
        toks = [(n, c) for n, c in self.count.items() if c]
        for eng in self.q:
            self.wait(eng, toks)


class Arena:

    def __init__(self, t, words):
        self.t, self.words, self.at = t, words, 0

    def reset(self):
        self.at = 0

    def get(self, *shape, dt=F32):
        n = 1
        for s in shape:
            n *= s
        w = n if dt != BF16 else (n + 1) // 2
        w = (w + 7) // 8 * 8
        assert self.at + w <= self.words, (self.at, w)
        v = self.t[:, self.at:self.at + w]
        self.at += w
        if dt != F32:
            v = v.bitcast(dt)
        v = v[:, 0:n]
        if len(shape) == 2:
            v = v.rearrange("p (a b) -> p a b", b=shape[1])
        if len(shape) == 3:
            v = v.rearrange("p (a b c) -> p a b c", b=shape[1], c=shape[2])
        return v


def build(nc, A, out):
    with ExitStack() as ctx:
        Q = Queues(nc, ctx)
        op, dma = Q.op, Q.dma

        def sb(name, shape, dt=F32):
            return ctx.enter_context(nc.sbuf_tensor(name, [P] + shape, dt))

        def dram(name, shape, dt=F32):
            return nc.dram_tensor(name, shape, dt).ap()

        AW = 40400
        arena = Arena(sb("arena", [AW]), AW)
        PS = ctx.enter_context(nc.psum_tensor("PS", [P, 4096], F32))

        def bank(i, n=512):
            return PS[:, 512 * i:512 * i + n]

        ident = sb("ident", [P])
        ltri = sb("ltri", [P])
        iotaf = sb("iotaf", [P])
        pcol = sb("pcol", [1])
        nodeid = sb("nodeid", [NBLK])
        onesF = sb("onesF", [P])
        xn = sb("xn", [NBLK, P])
        srcF = sb("srcF", [NCH])
        srcI = sb("srcI", [NCH], I32)
        dstF = sb("dstF", [NCH])
        loF = sb("loF", [NCH])
        hiF = sb("hiF", [NCH])
        idxG = sb("idxG", [NCH], I32)
        wcol = sb("wcol", [NG])
        d0I = sb("d0I", [NG], I32)
        flag = sb("flag", [2], I32)
        eF = sb("eF", [NCH])
        beta = sb("beta", [1])
        epsc = sb("epsc", [1])
        endI = sb("endI", [NBLK], I32)
        deg = sb("deg", [NBLK])
        has = sb("has", [NBLK])
        Mx = sb("Mx", [NBLK])
        Sx = sb("Sx", [NBLK])
        small = sb("small", [16, NBLK])
        W1ab = sb("W1ab", [2 * P])
        We = sb("We", [2 * P])
        cols = sb("cols", [8])
        wA = sb("wA", [2 * P])
        wB = sb("wB", [2 * P])
        wC = sb("wC", [2 * P])
        wD = sb("wD", [2 * P])
        vec = sb("vec", [5, P])

        dF = dram("dF", (EP,))
        sF = dram("sF", (EP,))
        wF = dram("wF", (EP,))
        keepR = dram("keepR", (EP,), BF16)
        negR = dram("negR", (EP,), BF16)
        sampR = dram("sampR", (NSAMP,))
        ubR = dram("ubR", (NPAD + 1,))
        T0b = dram("T0b", (TR, 2 * P))
        T0 = dram("T0", (NPAD, 2 * P))
        T1 = dram("T1", (NPAD, XW))
        T2 = dram("T2", (NPAD, 2 * P))
        T3 = dram("T3", (NPAD, P))
        tabs = [dram(f"tab{k}", (TR, XW)) for k in range(KT)]
        H0 = dram("H0", (EP, P))
        H1 = dram("H1", (EP, P))
        H2 = dram("H2", (EP, 2 * P))
        H3 = dram("H3", (EP, P))

        s_ld = Q.sem("s_ld")
        s_st = Q.sem("s_st")
        s_init = Q.sem("s_init")
        s_g = Q.sem("s_g")

        def row(v, n):
            return v.rearrange("(a n) -> a n", a=1).to_broadcast([P, n])

        state = {"last": None}

        def step(eng, fn):
            state["last"] = op(eng, fn, state["last"])
            return state["last"]

        def load(fns, eng="sp", sem=s_ld):
            for fn in fns:
                tok = dma(eng, sem, fn, state["last"])
            state["last"] = [state["last"], tok]
            return tok

        op("pool", lambda e: e.memset(ident[:, :], 0.0))
        op("pool", lambda e: e.memset(ltri[:, :], 1.0))
        op("pool", lambda e: e.memset(onesF[:, :], 1.0))
        op("pool", lambda e: e.iota(iotaf[:, :], [[1, P]], base=0, channel_multiplier=0,
                                    allow_small_or_imprecise_dtypes=True))
        op("pool", lambda e: e.iota(pcol[:, :], [[0, 1]], base=NPAD, channel_multiplier=1,
                                    allow_small_or_imprecise_dtypes=True))
        a = op("pool", lambda e: e.iota(nodeid[:, :], [[P, NBLK]], base=0, channel_multiplier=1,
                                        allow_small_or_imprecise_dtypes=True))
        op("pool", lambda e: e.affine_select(out=ident[:, :], in_=ident[:, :], compare_op=ALU.not_equal, fill=1.0,
                                             base=0, pattern=[[-1, P]], channel_multiplier=1), a)
        a = op("pool", lambda e: e.affine_select(out=ltri[:, :], in_=ltri[:, :], compare_op=ALU.is_gt, fill=0.0,
                                                 base=0, pattern=[[-1, P]], channel_multiplier=1), a)
        state["last"] = a

        def bc(v, n=NBLK):
            return v.unsqueeze(1).to_broadcast([P, n, v.shape[1]])

        def bf(v, f=P):
            return v.unsqueeze(2).to_broadcast([P, v.shape[1], f])

        def flat(v):
            return v.rearrange("p a b -> p (a b)")

        PN = PS[:, 0:NPAD].rearrange("p (b f) -> p b f", f=P)

        def center(w, n, parts, c):
            step("dve", lambda e: e.tensor_reduce(small[0:parts, 6, c:c + 1], w, AX, ALU.add))
            step("dve", lambda e: e.tensor_scalar(small[0:parts, 7, c:c + 1], small[0:parts, 6, c:c + 1],
                                                  1.0 / n, None, ALU.mult))
            step("dve", lambda e: e.tensor_scalar(w, w, small[0:parts, 7, c:c + 1], None, ALU.subtract))

        def transposed(src, dst):
            def go(e):
                for b in range(NBLK):
                    ins = e.transpose(PN[:, b, :], src[:, b, :], ident[:, :])
                return ins
            step("pe", go)
            step("act", lambda e: e.activation(dst, PN, ACT.Copy))

        def product(pairs):
            def go(e):
                for b in range(NBLK):
                    for i, (t, w) in enumerate(pairs):
                        ins = e.matmul(PN[:, b, :], t[:, b, :], w, start=(i == 0), stop=(i == len(pairs) - 1))
                return ins
            step("pe", go)

        def table(xT, w, width, T, big):
            for b0 in range(0, NBLK, 13):
                nb_ = min(13, NBLK - b0)

                def go(e, b0=b0, nb_=nb_):
                    for b in range(nb_):
                        ins = e.matmul(PS[:, b * width:(b + 1) * width], xT[:, b0 + b, :], w, start=True, stop=True)
                    return ins
                step("pe", go)
                step("act", lambda e, b0=b0, nb_=nb_: e.activation(
                    flat(big)[:, b0 * width:(b0 + nb_) * width], PS[:, 0:nb_ * width], ACT.Copy))
            load([lambda e: e.dma_start(T.rearrange("(b p) d -> p b d", p=P), big)])

        def rsqrt(v, rs, h, a, *after):
            def guess(e):
                e.tensor_scalar(h, v, -0.5, None, ALU.mult)
                return e.tensor_scalar(a.bitcast(I32), v.bitcast(I32), 1, None, ALU.logical_shift_right)
            tok = op("dve", guess, *after)
            tok = op("dve", lambda e: e.tensor_scalar(rs.bitcast(I32), a.bitcast(I32), -1.0, MAGIC,
                                                      ALU.mult, ALU.add), tok)
            for _ in range(3):
                tok = op("dve", lambda e: e.tensor_tensor(a, rs, rs, ALU.mult), tok)
                tok = op("dve", lambda e: e.tensor_tensor(a, a, h, ALU.mult), tok)
                tok = op("dve", lambda e: e.scalar_tensor_tensor(out=rs, in0=a, scalar=1.5, in1=rs,
                                                                 op0=ALU.add, op1=ALU.mult), tok)
            return tok

        def rstd_of(v, rs, n):
            step("dve", lambda e: e.tensor_scalar(v, v, 1.0 / n, EPS, ALU.mult, ALU.add))
            state["last"] = rsqrt(v, rs, small[:, 14, :], small[:, 15, :], state["last"])

        def ln_affine(u, sq, g, b):
            step("dve", lambda e: e.tensor_tensor(sq, u, u, ALU.mult))
            step("dve", lambda e: e.tensor_reduce(small[:, 8, :], sq, AX, ALU.add))
            rstd_of(small[:, 8, :], small[:, 9, :], P)
            step("dve", lambda e: e.tensor_tensor(u, u, bf(small[:, 9, :]), ALU.mult))
            step("dve", lambda e: e.tensor_tensor(u, u, bc(g), ALU.mult))
            step("dve", lambda e: e.tensor_tensor(u, u, bc(b), ALU.add))

        def ln_plain(y, sq):
            step("dve", lambda e: e.tensor_reduce(small[:, 8, :], y, AX, ALU.add))
            step("dve", lambda e: e.tensor_scalar(small[:, 8, :], small[:, 8, :], 1.0 / P, None, ALU.mult))
            step("dve", lambda e: e.tensor_tensor(y, y, bf(small[:, 8, :]), ALU.subtract))
            step("dve", lambda e: e.tensor_tensor(sq, y, y, ALU.mult))
            step("dve", lambda e: e.tensor_reduce(small[:, 9, :], sq, AX, ALU.add))
            rstd_of(small[:, 9, :], small[:, 10, :], P)
            step("dve", lambda e: e.tensor_tensor(xn[:, :, :], y, bf(small[:, 10, :]), ALU.mult))

        def gather_ends(H, w, dst):
            load([lambda e, b=b: e.indirect_dma_start(
                out=dst[:, b, :], out_offset=None, in_=H,
                in_offset=bass.IndirectOffsetOnAxis(ap=endI[:, b:b + 1], axis=0)) for b in range(NBLK)],
                "pool", s_g)

        ring_sems = {}

        def ring(name, n):
            if name not in ring_sems:
                ring_sems[name] = [Q.sem(f"{name}{i}") for i in range(n)]
            return ring_sems[name]

        def gather(sems, b, T, idx, dst, *after):
            s = sems[b % len(sems)]
            for c in range(CB):
                tok = dma("pool", s, lambda e, c=c: e.indirect_dma_start(
                    out=dst[:, c, :], out_offset=None, in_=T,
                    in_offset=bass.IndirectOffsetOnAxis(ap=idx[:, CB * b + c:CB * b + c + 1], axis=0)), *after)
            return tok

        def pipeline(stages):
            last = max(lag for lag, _ in stages)
            for i in range(NBAT + last):
                for lag, fn in stages:
                    if 0 <= i - lag < NBAT:
                        fn(i - lag)

        def ident4(n):
            return ident[:, :].unsqueeze(1).to_broadcast([P, n, P])

        gs_sem, gx_sem = ring("gs", 8), ring("gx", 1)
        e_sem, s_sem, w_sem, k_sem = ring("le", 2), ring("lsr", 3), ring("lw", 3), ring("lk", 4)
        d_sem, t_sem = ring("ld", 3), ring("ltw", 3)
        o_sem, tab_sem = ring("so", 3), ring("tb", KT)
        tk = {}

        def g0(name, b):
            return tk.get((name, b))

        def put(name, b, tok):
            tk[(name, b)] = tok
            return tok

        def grow(v, g):
            return row(v[g * GE:(g + 1) * GE], GE)

        def backend(b, nh, psT, psB, s, Ob, H, rowsR, after_T, op0, op1, init, srcs=None):
            g, h0 = b // 2, (b % 2) * CB * P
            kr = rowsR[g % 4][:, h0:h0 + CB * P]

            def scan(e):
                for h in range(nh):
                    ins = e.tensor_tensor_scan(s[b % 2][:, h, :], kr, psT[h] if srcs is None else srcs[h],
                                               s[(b - 1) % 2][:, h, CB * P - 1:CB * P] if b else init, op0, op1)
                return ins
            put("scan", b, op("dve", scan, after_T, g0("kR", g), g0("scan", b - 1), g0("B", b - 2)))

        def backend2(b, nh, psB, s, Ob, H):
            def B(e):
                for c in range(CB):
                    for h in range(nh):
                        ins = e.transpose(psB[:, (c * nh + h) * P:(c * nh + h + 1) * P],
                                          s[b % 2][:, h, c * P:(c + 1) * P], ident[:, :])
                return ins
            put("B", b, op("pe", B, g0("scan", b), g0("O", b - 1)))
            put("O", b, op("act", lambda e: e.activation(flat(Ob[b % 3]), psB, ACT.Copy),
                           g0("B", b), g0("so", b - 3)))
            put("so", b, dma("sp", o_sem[b % 3], lambda e: e.dma_start(
                H[b * CB * P:(b + 1) * CB * P, :].rearrange("(c p) f -> p c f", p=P), Ob[b % 3]), g0("O", b)))

        def rows_load(b, rowsR, R):
            if b % 2 == 0:
                g = b // 2
                put("kR", g, dma("sp", k_sem[g % 4], lambda e: e.dma_start(rowsR[g % 4], grow(R, g)),
                                 g0("scan", b - 7)))

        v_ = vec[:, :, :]
        gsem = gs_sem

        def edge_lists():
            dI = arena.get(NCH, dt=I32)
            dP = arena.get(NCH, dt=I32)
            sI = arena.get(NCH, dt=I32)
            wI = arena.get(NCH)
            dFt = arena.get(NCH)
            sFt = arena.get(NCH)
            kt = arena.get(NCH)
            kb = arena.get(NCH, dt=BF16)
            nb = arena.get(NCH, dt=BF16)
            samp = arena.get(SUB)
            rows = arena.get(3, 7, P)
            sampB = arena.get(NSAMP)
            junk = arena.get(NSAMP)
            zero = arena.get(3 * TR)
            sub = arena.get(NBLK, SUB)
            onep = arena.get(1)

            load([
                lambda e: e.dma_start(dI, A["dst"][1:EP + 1].rearrange("(p j) -> p j", j=NCH)),
                lambda e: e.dma_start(dP, A["dst"][0:EP].rearrange("(p j) -> p j", j=NCH)),
                lambda e: e.dma_start(sI, A["src"].rearrange("(p j) -> p j", j=NCH)),
                lambda e: e.dma_start(wI, A["edge_weight"].rearrange("(p j) -> p j", j=NCH)),
                lambda e: e.dma_start(xn[:, :, :], A["x"].rearrange("(b p) d -> p b d", p=P)),
                lambda e: e.dma_start(beta[:, :], row(A["L1_gnn_beta"], 1)),
                lambda e: e.dma_start(epsc[:, :], row(A["L1_gnn_eps"], 1)),
            ])

            def conv(e):
                e.tensor_copy(dFt, dI)
                e.tensor_copy(sFt, sI)
                e.tensor_tensor(kt, dI, dP, ALU.is_equal)
                e.memset(zero, 0.0)
                e.memset(onep, 0.0)
                e.memset(samp, 0.0)
                return e.tensor_scalar(wI, wI, beta[:, 0:1], None, ALU.mult)
            step("dve", conv)

            def conv2(e):
                e.tensor_copy(kb, kt)
                e.tensor_copy(samp, dFt.rearrange("p (a b) -> p a b", b=SUB)[:, :, 0])
                return e.tensor_scalar(nb, kt, -1.0, BIG, ALU.add, ALU.mult)
            step("dve", conv2)

            for k in range(KT):
                dma("sp", s_init, lambda e, k=k: e.dma_start(
                    tabs[k].rearrange("(p r) c -> p (r c)", p=P), zero[:, 0:TR // P * XW]), state["last"])
            load([
                lambda e: e.dma_start(dF.rearrange("(p j) -> p j", j=NCH), dFt),
                lambda e: e.dma_start(sF.rearrange("(p j) -> p j", j=NCH), sFt),
                lambda e: e.dma_start(wF.rearrange("(p j) -> p j", j=NCH), wI),
                lambda e: e.dma_start(keepR.rearrange("(p j) -> p j", j=NCH), kb),
                lambda e: e.dma_start(negR.rearrange("(p j) -> p j", j=NCH), nb),
                lambda e: e.dma_start(sampR.rearrange("(p j) -> p j", j=SUB), samp),
            ])
            dma("sp", s_init, lambda e: e.dma_start(T0b[NPAD:TR, :], zero[:, 0:2 * P]), state["last"])
            load([lambda e, i=i, t=t: e.dma_start(rows[0:112, i, :, :], t.rearrange("(t q p) -> q t p", q=112, p=P))
                  for i, t in enumerate((sF, dF, wF))] +
                 [lambda e: e.dma_start(sampB, row(sampR, NSAMP))])

            def tr_lists(e):
                for i in range(3):
                    for t in range(7):
                        o = 1024 * i + 112 * t + (64 if t >= 4 else 0)
                        ins = e.transpose(PS[:, o:o + 112], rows[0:112, i, t, :], ident[0:112, 0:112])
                return ins
            step("pe", tr_lists)

            def ev_lists(e):
                for i, d in enumerate((srcF, dstF, eF)):
                    e.tensor_copy(d[:, 0:448], PS[:, 1024 * i:1024 * i + 448])
                    e.tensor_copy(d[:, 448:784], PS[:, 1024 * i + 512:1024 * i + 848])
                    if i == 0:
                        e.tensor_copy(srcI[:, 0:448], PS[:, 0:448])
                        ins = e.tensor_copy(srcI[:, 448:784], PS[:, 512:848])
                return ins
            step("dve", ev_lists)
            for b in range(NBLK):
                step("dve", lambda e, b=b: e.tensor_scalar(junk, sampB, nodeid[:, b:b + 1], 0.0, ALU.is_le, ALU.add,
                                                           accum_out=small[:, 0, b:b + 1]))
            kI = small[:, 1, :].bitcast(I32)
            step("dve", lambda e: e.tensor_scalar(small[:, 2, :], small[:, 0, :], -1.0, 0.0, ALU.add, ALU.max))
            step("dve", lambda e: e.tensor_copy(kI, small[:, 2, :]))
            dF28 = dF.rearrange("(s i) -> s i", i=SUB)
            load([lambda e, b=b: e.indirect_dma_start(
                out=sub[:, b, :], out_offset=None, in_=dF28,
                in_offset=bass.IndirectOffsetOnAxis(ap=kI[:, b:b + 1], axis=0)) for b in range(NBLK)],
                "pool", s_g)

            def cnt28(e):
                for b in range(NBLK):
                    ins = e.tensor_scalar(junk[:, SUB * b:SUB * b + SUB], sub[:, b, :], nodeid[:, b:b + 1], 0.0, ALU.is_le, ALU.add,
                                          accum_out=small[:, 3, b:b + 1])
                return ins
            step("dve", cnt28)
            step("dve", lambda e: e.scalar_tensor_tensor(out=small[:, 4, :], in0=small[:, 2, :], scalar=float(SUB),
                                                         in1=small[:, 3, :], op0=ALU.mult, op1=ALU.add))
            step("dve", lambda e: e.tensor_scalar(endI[:, :], small[:, 4, :], -1.0, 0.0, ALU.add, ALU.max))
            with nc.allow_non_contiguous_dma(reason="3200 counts, once"):
                load([lambda e: e.dma_start(ubR[0:1].rearrange("(a b) -> a b", a=1), onep[0:1, 0:1]),
                      lambda e: e.dma_start(ubR[1:NPAD + 1].rearrange("(b p) -> p b", p=P), small[:, 4, :],
                                            allow_slow_non_contiguous=True)])
                load([lambda e: e.dma_start(small[:, 5, :], ubR[0:NPAD].rearrange("(b p) -> p b", p=P),
                                            allow_slow_non_contiguous=True)])
            step("dve", lambda e: e.tensor_tensor(deg[:, :], small[:, 4, :], small[:, 5, :], ALU.subtract))
            step("dve", lambda e: e.tensor_scalar(has[:, :], deg[:, :], 0.5, None, ALU.is_gt))

            loI, hiI = arena.get(NCH, dt=I32), arena.get(NCH, dt=I32)
            d0B, rel, out_w = arena.get(NG), arena.get(NG, 8), arena.get(NG, 8)

            def digits(e):
                e.tensor_scalar(loI, srcI[:, :], 127, None, ALU.bitwise_and)
                return e.tensor_scalar(hiI, srcI[:, :], 7, None, ALU.logical_shift_right)
            step("dve", digits)

            def digits2(e):
                e.tensor_copy(loF[:, :], loI)
                return e.tensor_copy(hiF[:, :], hiI)
            step("dve", digits2)
            step("pe", lambda e: e.matmul(PS[:, 0:NG], onesF[0:1, :], dstF[0:1, 0:NCH:8], start=True, stop=True))
            step("dve", lambda e: e.tensor_copy(d0B, PS[:, 0:NG]))
            step("dve", lambda e: e.tensor_scalar(small[:, 12, 0:1], pcol[:, :], -float(NPAD), None, ALU.add))

            def windows(e):
                e.tensor_scalar(wcol[:, :], d0B, small[:, 12, 0:1], None, ALU.add)
                e.tensor_copy(d0I[:, :], d0B)
                return e.tensor_tensor(rel, dstF[:, :].rearrange("p (g c) -> p g c", c=8), bf(d0B, 8), ALU.subtract)
            step("dve", windows)
            step("dve", lambda e: e.tensor_scalar(out_w, rel, float(P), None, ALU.is_ge))
            fl = out_w.rearrange("p g c -> p (g c)")

            def outside(e):
                e.tensor_reduce(small[:, 13, 0:1], fl, AX, ALU.add)
                return e.scalar_tensor_tensor(out=rel.rearrange("p g c -> p (g c)"), in0=dstF[:, :],
                                              scalar=-float(DUMMY), in1=fl, op0=ALU.add, op1=ALU.mult)
            step("dve", outside)
            step("dve", lambda e: e.tensor_scalar(idxG[:, :], rel.rearrange("p g c -> p (g c)"), float(DUMMY), None,
                                                  ALU.add))
            step("pe", lambda e: e.matmul(PS[:, 0:1], onesF[:, :], small[:, 13, 0:1], start=True, stop=True))
            step("dve", lambda e: e.tensor_copy(flag[:, 0:1], PS[:, 0:1]))

        def L0_tables():
            Q.barrier()
            arena.reset()
            state["last"] = None
            xT = arena.get(NBLK, P)
            big = arena.get(NBLK, 2 * P)
            w1 = A["L0_gnn_msg_w1"]
            load([lambda e: e.dma_start(W1ab[:, 0:P], w1[0:P, :]),
                  lambda e: e.dma_start(W1ab[:, P:2 * P], w1[P:2 * P, :]),
                  lambda e: e.dma_start(We[0:64, 0:P], w1[2 * P:2 * P + 64, :]),
                  lambda e: e.dma_start(We[64:65, 0:P], A["L0_gnn_msg_b1"].rearrange("(a n) -> a n", a=1)),
                  lambda e: e.dma_start(cols[:, 0:1], A["L0_gnn_ln1_g"].rearrange("(n a) -> n a", a=1)),
                  lambda e: e.dma_start(cols[:, 1:2], A["L0_gnn_ln1_b"].rearrange("(n a) -> n a", a=1))])
            center(W1ab[:, 0:P], P, P, 0)
            center(W1ab[:, P:2 * P], P, P, 1)
            center(We[0:65, 0:P], P, 65, 2)
            step("dve", lambda e: e.tensor_copy(We[0:65, P:2 * P], We[0:65, 0:P]))
            transposed(xn, xT)
            table(xT, W1ab[:, :], 2 * P, T0, big)
            W1ba = arena.get(2 * P)

            def swap(e):
                e.tensor_copy(W1ba[:, 0:P], W1ab[:, P:2 * P])
                return e.tensor_copy(W1ba[:, P:2 * P], W1ab[:, 0:P])
            step("dve", swap)
            table(xT, W1ba, 2 * P, T0b[0:NPAD, :], big)

        def L0_edges():
            Q.barrier()
            arena.reset()
            NR = 7
            Gs = [arena.get(CB, 2 * P) for _ in range(NR)]
            eT = [arena.get(GE) for _ in range(2)]
            sR = [arena.get(GE) for _ in range(2)]
            wR = [arena.get(GE) for _ in range(2)]
            dR = [arena.get(GE) for _ in range(2)]
            kR = [arena.get(GE, dt=BF16) for _ in range(4)]
            Tw = [arena.get(2 * P) for _ in range(3)]
            OT = [arena.get(CB * P) for _ in range(2)]
            Dg = [arena.get(2 * CB, P) for _ in range(2)]
            r1 = [arena.get(CB * P) for _ in range(2)]
            r2 = [arena.get(CB, P) for _ in range(2)]
            s1 = [arena.get(CB * P) for _ in range(2)]
            Ob = [arena.get(CB, P) for _ in range(2)]
            R2 = [arena.get(CB, P) for _ in range(2)]
            Sm = [arena.get(CB, P) for _ in range(6)]
            Vm = [arena.get(CB, P) for _ in range(2)]
            jl = arena.get(CB, P)
            ja = arena.get(2 * CB, P, dt=BF16)
            X2 = [arena.get(CB, XW) for _ in range(3)]
            cn = [arena.get(CB) for _ in range(8)]
            aF = [arena.get(CB) for _ in range(2)]
            mF = [arena.get(CB) for _ in range(2)]
            iA = [arena.get(CB, dt=I32) for _ in range(10)]
            var = [arena.get(4 * CB) for _ in range(3)]
            rst = [arena.get(4 * CB) for _ in range(3)]
            nh_, na_ = arena.get(4 * CB), arena.get(4 * CB)
            mm = [arena.get(CB) for _ in range(4)]
            C2 = 2 * CB
            cb = [arena.get(C2) for _ in range(4)]
            mg = [arena.get(C2) for _ in range(4)]
            sg = [arena.get(C2) for _ in range(4)]
            OL = arena.get(C2, P)
            OH = arena.get(C2, NBLK)
            fst = arena.get(C2)
            RH = arena.get(C2, 2, NBLK)
            DM = [arena.get(C2 + 1, NBLK) for _ in range(2)]
            DS = [arena.get(C2 + 1, NBLK) for _ in range(2)]
            DX = arena.get(C2 + 1, NBLK)

            op("dve", lambda e: e.memset(DM[0][:, C2, :], -BIG))
            op("dve", lambda e: e.memset(DS[0][:, C2, :], 0.0))
            for x2 in X2:
                op("dve", lambda e, x2=x2: e.memset(x2[:, :, P:XW], 0.0))
            for t in eT:
                op("dve", lambda e, t=t: e.memset(t[64:65, :], 1.0))
            Q.barrier()
            out_of_window = {}
            Q.q["pool"].append(lambda e: out_of_window.update(v=e.value_load(flag[0:1, 0:1], min_val=0,
                                                                             max_val=EP)))
            psC = PS[:, 0:1024]

            def L0_load(b):
                if b % 2 == 0:
                    g = b // 2
                    put("eT", g, dma("sp", e_sem[g % 2], lambda e: e.dma_start(
                        eT[g % 2][0:64, :], A["ea64T"][:, g * GE:(g + 1) * GE]), g0("C", b - 3)))
                    put("sR", g, dma("sp", s_sem[g % 2], lambda e: e.dma_start(sR[g % 2], grow(sF, g)), g0("S1", b - 3)))
                    put("wR", g, dma("sp", w_sem[g % 2], lambda e: e.dma_start(wR[g % 2], grow(wF, g)), g0("S", b - 3)))
                    put("dR", g, dma("sp", d_sem[g % 2], lambda e: e.dma_start(dR[g % 2], grow(dF, g)), g0("OT", b - 3)))
                    put("kR", g, dma("sp", k_sem[g % 4], lambda e: e.dma_start(kR[g % 4], grow(keepR, g)),
                                     g0("scan", b - 7)))

                    def window(e):
                        v = e.value_load(d0I[0:1, g:g + 1], min_val=0, max_val=NPAD - 1)
                        return e.dma_start(Tw[g % 3], T0b[bass.ds(v, P), :])
                    put("Tw", g, dma("sp", t_sem[g % 3], window, g0("C", b - 5)))
                put("gs", b, gather(gs_sem[0:NR], b, T0, srcI, Gs[b % NR], g0("T", b - NR)))

            def L0_outside(b):
                seen = dict(Q.seen["pool"])
                got = g0("gs", b)
                x = gx_sem[0]

                def go(e):
                    with e.If(out_of_window["v"] > 0):
                        e.wait_ge(Q.sems[got[0]], got[1])
                        for c in range(CB):
                            e.indirect_dma_start(
                                out=Gs[b % NR][:, c, :], out_offset=None, in_=T0b[:, :],
                                in_offset=bass.IndirectOffsetOnAxis(ap=idxG[:, CB * b + c:CB * b + c + 1], axis=0),
                                compute_op=ALU.add).then_inc(Q.sems[x], 16)
                        e.wait_ge(Q.sems[x], 16 * CB * (b + 1))
                Q.q["pool"].append(go)
                assert seen == Q.seen["pool"]
                put("gx", b, op("pool", lambda e: e.engine_nop()))

            def L0_OT(b):
                g, h0 = b // 2, b % 2 * CB * P
                put("OT", b, op("dve", lambda e: e.tensor_scalar(OT[b % 2], dR[g % 2][:, h0:h0 + CB * P],
                                                                 wcol[:, g:g + 1], None, ALU.is_equal),
                                g0("dR", g), g0("C", b - 2)))

            def L0_C(b):
                g, h0 = b // 2, b % 2 * CB * P

                def C(e):
                    for c in range(CB):
                        e.matmul(psC[:, c * 2 * P:(c + 1) * 2 * P], eT[g % 2][0:65, h0 + c * P:h0 + (c + 1) * P],
                                 We[0:65, :], start=True, stop=False)
                        ins = e.matmul(psC[:, c * 2 * P:(c + 1) * 2 * P], OT[b % 2][:, c * P:(c + 1) * P],
                                       Tw[g % 3], start=False, stop=True)
                    return ins
                put("C", b, op("pe", C, g0("eT", g), g0("OT", b), g0("Tw", g), g0("t", b - 1)))

            def L0_t(b):
                t = Gs[b % NR]
                put("t", b, op("dve", lambda e: e.tensor_tensor(flat(t), flat(t), psC, ALU.add),
                               g0("gs", b), g0("gx", b), g0("C", b)))

            def L0_S1(b):
                g, h0 = b // 2, b % 2 * CB * P

                def S(e):
                    for c in range(CB):
                        k = CB * b + c
                        r = slice(h0 + c * P, h0 + (c + 1) * P)
                        ins = e.tensor_scalar(Sm[b % 6][:, c, :], sR[g % 2][:, r], srcF[:, k:k + 1], 0.0,
                                              ALU.is_equal, ALU.add, accum_out=cn[b % 8][:, c:c + 1])
                    return ins
                put("S1", b, op("dve", S, g0("sR", g), g0("SS", b - 6), g0("X", b - 8)))

            def L0_V(b):
                put("V", b, op("act", lambda e: e.activation(flat(Vm[b % 2]), flat(Sm[b % 6]), ACT.Copy, bias=-BIG,
                                                             scale=BIG), g0("S1", b), g0("ex", b - 2)))

            def L0_S2(b):
                g, h0 = b // 2, b % 2 * CB * P
                o = b % 2 * CB
                old = g0("RH", 2 * g - 7)

                def S2(e):
                    for c in range(CB):
                        r = slice(h0 + c * P, h0 + (c + 1) * P)
                        e.tensor_tensor_reduce(jl[:, c, :], Sm[b % 6][:, c, :], ltri[:, :], 1.0, 0.0, ALU.mult,
                                               ALU.add, cb[g % 4][:, o + c:o + c + 1])
                        ins = e.tensor_tensor_reduce(Vm[b % 2][:, c, :], Vm[b % 2][:, c, :], wR[g % 2][:, r], 1.0,
                                                     -BIG, ALU.add, ALU.max, mg[g % 4][:, o + c:o + c + 1])
                    return ins
                put("S", b, op("dve", S2, g0("V", b), g0("wR", g), g0("S", b - 1), old))
                sl = slice(CB * b, CB * b + CB)

                def S3(e):
                    e.tensor_scalar(mm[b % 4], mg[g % 4][:, o:o + CB], -1.0, None, ALU.mult)
                    e.tensor_scalar(aF[b % 2], cb[g % 4][:, o:o + CB], 0.5, None, ALU.is_lt)
                    return e.tensor_scalar(mF[b % 2], srcF[:, sl], pcol[:, 0:1], None, ALU.subtract)
                put("S3", b, op("dve", S3, g0("S", b), g0("ex", b - 4), g0("S4", b - 2)))
                put("S3b", b, op("dve", lambda e: e.tensor_tensor(mF[b % 2], mF[b % 2], aF[b % 2], ALU.mult),
                                 g0("S3", b)))
                put("S4", b, op("dve", lambda e: e.tensor_scalar(iA[b % 10], mF[b % 2], pcol[:, 0:1], None, ALU.add),
                                g0("S3b", b), g0("sc", b - 10)))

            def L0_sq(b):
                g, o, t = b // 2, b % 2 * CB, Gs[b % NR]

                def sq(e):
                    for c in range(CB):
                        for hh in range(2):
                            i = 2 * (o + c) + hh
                            ins = e.activation(ja[:, 2 * c + hh, :], t[:, c, hh * P:(hh + 1) * P], ACT.Square,
                                               accum_out=var[g % 3][:, i:i + 1])
                    return ins
                put("sq", b, op("act", sq, g0("t", b), g0("rs", 2 * g - 5), g0("sq", b - 1)))

            def L0_ex(b):
                g, o = b // 2, b % 2 * CB

                def ex(e):
                    for c in range(CB):
                        ins = e.activation(Vm[b % 2][:, c, :], Vm[b % 2][:, c, :], ACT.Exp,
                                           bias=mm[b % 4][:, c:c + 1], accum_out=sg[g % 4][:, o + c:o + c + 1])
                    return ins
                put("ex", b, op("act", ex, g0("S3", b), g0("S", b), g0("RH", 2 * g - 7)))

            def L0_rs(b):
                if b % 2:
                    g = b // 2
                    v = var[g % 3]
                    tok = op("dve", lambda e: e.tensor_scalar(v, v, 1.0 / P, EPS, ALU.mult, ALU.add), g0("sq", b))
                    tok = rsqrt(v, rst[g % 3], nh_, na_, tok, g0("D", b - 6))
                    put("rs", b, tok)
                    put("rs", b - 1, tok)

            def L0_A(b):
                if b % 2 == 0:
                    return
                g = b // 2
                sl = slice(C2 * g, C2 * g + C2)

                def onehot(e):
                    e.tensor_tensor(OL, bc(iotaf[:, :], C2), bf(loF[:, sl]), ALU.is_equal)
                    e.tensor_tensor(OH, bc(iotaf[:, 0:NBLK], C2), bf(hiF[:, sl], NBLK), ALU.is_equal)
                    return e.tensor_scalar(fst, cb[g % 4], 0.5, None, ALU.is_lt)
                tok = op("dve", onehot, g0("Z", b - 2), g0("S", b), g0("RH", b - 2))
                tok = op("dve", lambda e: e.tensor_tensor(OH, OH, bf(fst, NBLK), ALU.mult), tok)

                def rh(e):
                    e.tensor_tensor(RH[:, :, 0, :], OH, bf(mg[g % 4], NBLK), ALU.mult)
                    return e.tensor_tensor(RH[:, :, 1, :], OH, bf(sg[g % 4], NBLK), ALU.mult)
                put("RH", b, op("dve", rh, tok, g0("ex", b)))

                def Z(e):
                    for c in range(C2):
                        ins = e.matmul(bank(7)[:, c * 50:(c + 1) * 50], OL[:, c, :],
                                       RH[:, c, :, :].rearrange("p a b -> p (a b)"), start=True, stop=True)
                    return ins
                put("Z", b, op("pe", Z, g0("RH", b), g0("mul", b - 2)))

            zz = bank(7, 50 * C2).rearrange("p (c t n) -> p c t n", t=2, n=NBLK)

            def L0_dm(b):
                if b % 2 == 0:
                    return
                g = b // 2
                dm, dmn = DM[g % 2], DM[(g + 1) % 2]
                tok = op("dve", lambda e: e.tensor_scalar(dm[:, 0:C2, :], zz[:, :, 1, :], 0.5, -BIG, ALU.is_lt,
                                                          ALU.mult), g0("Z", b), g0("df", b - 4))
                tok = op("dve", lambda e: e.tensor_tensor(dm[:, 0:C2, :], dm[:, 0:C2, :], zz[:, :, 0, :], ALU.add),
                         tok)
                tok = op("dve", lambda e: e.tensor_reduce(dmn[:, C2, :], dm.rearrange("p s n -> p n s"), AX,
                                                          ALU.max), tok, g0("df", b - 2))
                put("df", b, op("dve", lambda e: e.tensor_tensor(DX, dm, bc(dmn[:, C2, :], C2 + 1), ALU.subtract),
                                tok, g0("mul", b - 2)))

            def L0_DX(b):
                if b % 2:
                    put("DX", b, op("act", lambda e: e.activation(DX, DX, ACT.Exp), g0("df", b)))

            def L0_mul(b):
                if b % 2 == 0:
                    return
                ds, dsn = DS[b // 2 % 2], DS[(b // 2 + 1) % 2]

                def mul(e):
                    e.tensor_tensor(ds[:, 0:C2, :], DX[:, 0:C2, :], zz[:, :, 1, :], ALU.mult)
                    return e.tensor_tensor(ds[:, C2, :], DX[:, C2, :], ds[:, C2, :], ALU.mult)
                put("mul", b, op("dve", mul, g0("DX", b), g0("red", b - 2)))
                put("red", b, op("dve", lambda e: e.tensor_reduce(dsn[:, C2, :], ds.rearrange("p s n -> p n s"), AX,
                                                                  ALU.add), g0("mul", b)))

            def L0_D(b):
                o = b % 2 * C2
                put("D", b, op("dve", lambda e: e.tensor_tensor(Dg[b % 2], ident4(2 * CB),
                                                                bf(rst[b // 2 % 3][:, o:o + C2]), ALU.mult),
                               g0("rs", b), g0("T", b - 2)))

            def L0_T(b):
                t = Gs[b % NR]

                def T(e):
                    for c in range(CB):
                        for hh in range(2):
                            ins = e.matmul(bank(2 + hh)[:, c * P:(c + 1) * P], t[:, c, hh * P:(hh + 1) * P],
                                           Dg[b % 2][:, 2 * c + hh, :], start=True, stop=True)
                    return ins
                put("T", b, op("pe", T, g0("D", b), g0("r", b - 1), g0("sq", b)))

            def L0_r(b):
                def r(e):
                    e.activation(r1[b % 2], bank(2), ACT.Relu, bias=cols[:, 1:2], scale=cols[:, 0:1])
                    return e.activation(flat(r2[b % 2]), bank(3), ACT.Relu, bias=cols[:, 1:2], scale=cols[:, 0:1])
                put("r", b, op("act", r, g0("T", b), g0("scan", b - 2), g0("B", b - 2)))

            def L0_scan(b):
                g, h0 = b // 2, b % 2 * CB * P
                put("scan", b, op("dve", lambda e: e.tensor_tensor_scan(
                    s1[b % 2], kR[g % 4][:, h0:h0 + CB * P], r1[b % 2],
                    s1[(b - 1) % 2][:, CB * P - 1:CB * P] if b else 0.0, ALU.mult, ALU.add),
                    g0("r", b), g0("kR", g), g0("scan", b - 1), g0("B", b - 2)))

            def L0_B(b):
                def B(e):
                    for c in range(CB):
                        e.transpose(bank(4)[:, c * P:(c + 1) * P], s1[b % 2][:, c * P:(c + 1) * P], ident[:, :])
                    for c in range(CB):
                        ins = e.transpose(bank(5)[:, c * P:(c + 1) * P], r2[b % 2][:, c, :], ident[:, :])
                    return ins
                put("B", b, op("pe", B, g0("scan", b), g0("r", b), g0("O", b - 1), g0("R2", b - 1)))

            def L0_OR(b):
                put("R2", b, op("act", lambda e: e.activation(flat(R2[b % 2]), bank(5), ACT.Copy),
                                g0("B", b), g0("SS", b - 2)))
                put("O", b, op("act", lambda e: e.activation(flat(Ob[b % 2]), bank(4), ACT.Copy),
                               g0("B", b), g0("so", b - 2)))
                put("so", b, dma("sp", o_sem[b % 2], lambda e: e.dma_start(
                    H0[b * CB * P:(b + 1) * CB * P, :].rearrange("(c p) f -> p c f", p=P), Ob[b % 2]), g0("O", b)))

            def L0_SS(b):
                def SS(e):
                    for c in range(CB):
                        ins = e.matmul(bank(6)[:, c * P:(c + 1) * P], Sm[b % 6][:, c, :], R2[b % 2][:, c, :],
                                       start=True, stop=True)
                    return ins
                put("SS", b, op("pe", SS, g0("R2", b), g0("S1", b), g0("X", b - 1)))

            def L0_X(b):
                def X(e):
                    e.activation(X2[b % 3][:, :, P], cn[b % 8], ACT.Copy)
                    return e.activation(X2[b % 3][:, :, 0:P], bank(6).rearrange("p (c f) -> p c f", f=P), ACT.Copy)
                put("X", b, op("act", X, g0("SS", b), g0("sc", b - 3)))

            def L0_scatter(b):
                toks = []
                for c in range(CB):
                    k = CB * b + c
                    prev = tk.get(("tab", k - KT))
                    tok = dma("pool", tab_sem[k % KT], lambda e, c=c, k=k: e.indirect_dma_start(
                        out=tabs[k % KT], out_offset=bass.IndirectOffsetOnAxis(ap=iA[b % 10][:, c:c + 1], axis=0),
                        in_=X2[b % 3][:, c, :], in_offset=None, compute_op=ALU.add), g0("X", b), g0("S4", b), prev)
                    put("tab", k, tok)
                    toks.append(tok)
                put("sc", b, toks)

            pipeline([(9, L0_scatter), (8, L0_X), (3, L0_t), (3, L0_V), (6, L0_T), (7, L0_B), (2, L0_C), (2, L0_S1),
                      (4, L0_ex), (6, L0_r), (6, L0_dm), (3, L0_S2), (7, L0_OR), (4, L0_rs), (5, L0_D), (7, L0_mul),
                      (5, L0_A), (7, L0_SS), (3, L0_sq), (6, L0_DX), (1, L0_OT), (6, L0_scan), (1, L0_outside),
                      (0, L0_load)])
            last = g0("red", NBAT - 1)
            op("dve", lambda e: e.tensor_copy(Mx[:, :], DM[NG % 2][:, C2, :]), last)
            op("dve", lambda e: e.tensor_copy(Sx[:, :], DS[NG % 2][:, C2, :]), last)

        def L0_nodes():
            Q.barrier()
            arena.reset()
            state["last"] = None
            tk.clear()
            F = arena.get(NBLK, P)
            Y = arena.get(NBLK, P)
            Z = arena.get(NBLK, P)
            tb = [arena.get(NBLK, XW) for _ in range(2)]
            xT = arena.get(NBLK, P)
            aT = arena.get(NBLK, P)
            load([lambda e: e.dma_start(wA[:, 0:P], A["L0_gnn_msg_w2"][:, :]),
                  lambda e: e.dma_start(wA[:, P:2 * P], A["L0_gnn_upd_w2"][:, :]),
                  lambda e: e.dma_start(wB[:, 0:P], A["L0_gnn_upd_w1"][0:P, :]),
                  lambda e: e.dma_start(wB[:, P:2 * P], A["L0_gnn_upd_w1"][P:2 * P, :])] +
                 [lambda e, i=i, n=n: e.dma_start(v_[:, i, 0:P], row(A[n], P)) for i, n in enumerate(
                     ("L0_gnn_msg_b2", "L0_gnn_upd_b1", "L0_gnn_ln2_g", "L0_gnn_ln2_b", "L0_gnn_upd_b2"))])
            center(wB[:, 0:P], P, P, 0)
            center(wB[:, P:2 * P], P, P, 1)
            center(v_[:, 1, 0:P], P, P, 2)
            gather_ends(H0, P, F)
            step("dve", lambda e: e.tensor_tensor(F, F, bf(has[:, :]), ALU.mult))
            step("dve", lambda e: e.tensor_copy(small[:, 11, :], deg[:, :]))
            tbs = ring("tbl", 2)
            adds = {}
            for k in range(KT):
                lt = dma("sp", tbs[k % 2], lambda e, k=k: e.dma_start(
                    tb[k % 2], tabs[k][0:NPAD, :].rearrange("(b p) d -> p b d", p=P)), adds.get(k - 2))

                def acc(e, k=k):
                    e.tensor_tensor(F, F, tb[k % 2][:, :, 0:P], ALU.add)
                    return e.tensor_tensor(small[:, 11, :], small[:, 11, :], tb[k % 2][:, :, P], ALU.add)
                adds[k] = state["last"] = op("dve", acc, state["last"], lt)
            transposed(F, aT)
            product([(aT, wA[:, 0:P])])
            step("dve", lambda e: e.tensor_tensor(Y, bc(v_[:, 0, 0:P]), bf(small[:, 11, :]), ALU.mult))
            step("dve", lambda e: e.tensor_tensor(Y, Y, PN, ALU.add))
            transposed(Y, aT)
            transposed(xn, xT)
            product([(xT, wB[:, 0:P]), (aT, wB[:, P:2 * P])])
            step("dve", lambda e: e.tensor_tensor(Y, PN, bc(v_[:, 1, 0:P]), ALU.add))
            ln_affine(Y, Z, v_[:, 2, 0:P], v_[:, 3, 0:P])
            step("dve", lambda e: e.tensor_scalar(Y, Y, 0.0, None, ALU.max))
            transposed(Y, aT)
            product([(aT, wA[:, P:2 * P])])
            step("dve", lambda e: e.tensor_tensor(Y, PN, bc(v_[:, 4, 0:P]), ALU.add))
            step("dve", lambda e: e.scalar_tensor_tensor(out=Y, in0=xn[:, :, :], scalar=2.0, in1=Y,
                                                         op0=ALU.mult, op1=ALU.add))
            ln_plain(Y, Z)

        def L1_table():
            Q.barrier()
            arena.reset()
            Z = arena.get(NBLK, P)
            tX = arena.get(NBLK, XW)
            step("dve", lambda e: e.tensor_tensor(Z, xn[:, :, :], xn[:, :, :], ALU.mult))
            step("dve", lambda e: e.tensor_reduce(small[:, 0, :], Z, AX, ALU.add))
            step("dve", lambda e: e.tensor_scalar(small[:, 1, :], small[:, 0, :], 1e-35, None, ALU.max))
            state["last"] = rsqrt(small[:, 1, :], small[:, 2, :], small[:, 14, :], small[:, 15, :], state["last"])
            step("dve", lambda e: e.tensor_tensor(small[:, 2, :], small[:, 2, :], small[:, 0, :], ALU.mult))
            step("dve", lambda e: e.tensor_scalar(small[:, 2, :], small[:, 2, :], 1e-12, None, ALU.max))
            step("dve", lambda e: e.tensor_scalar(small[:, 3, :], Sx[:, :], 0.5, None, ALU.is_lt))
            step("dve", lambda e: e.tensor_tensor(small[:, 3, :], small[:, 3, :], Sx[:, :], ALU.add))
            step("dve", lambda e: e.tensor_tensor(small[:, 2, :], small[:, 2, :], small[:, 3, :], ALU.mult))
            step("dve", lambda e: e.reciprocal(small[:, 4, :], small[:, 2, :]))
            step("dve", lambda e: e.tensor_tensor(tX[:, :, 0:P], xn[:, :, :], bf(small[:, 4, :]), ALU.mult))
            step("dve", lambda e: e.memset(tX[:, :, P + 1:XW], 0.0))
            step("dve", lambda e: e.tensor_copy(tX[:, :, P], Mx[:, :]))
            load([lambda e: e.dma_start(T1.rearrange("(b p) d -> p b d", p=P), tX)])

        def L1_edges():
            Q.barrier()
            arena.reset()
            tk.clear()
            G = [arena.get(CB, XW) for _ in range(6)]
            kR = [arena.get(GE, dt=BF16) for _ in range(4)]
            Dg = [arena.get(CB, P) for _ in range(2)]
            s1 = [arena.get(1, CB * P) for _ in range(2)]
            Ob = [arena.get(CB, P) for _ in range(3)]
            pm = [arena.get(CB) for _ in range(4)]
            pp = [arena.get(CB) for _ in range(4)]

            def L1_load(b):
                rows_load(b, kR, keepR)
                put("gs", b, gather(gsem[0:6], b, T1, srcI, G[b % 6], g0("T", b - 6)))

            def L1_front(b):
                put("pm", b, op("dve", lambda e: e.tensor_tensor(pm[b % 4], eF[:, CB * b:CB * b + CB],
                                                                 G[b % 6][:, :, P], ALU.subtract),
                                g0("gs", b), g0("p", b - 4)))
                put("p", b, op("act", lambda e: e.activation(pp[b % 4], pm[b % 4], ACT.Exp), g0("pm", b), g0("D", b - 4)))
                put("D", b, op("dve", lambda e: e.tensor_tensor(Dg[b % 2], ident4(CB), bf(pp[b % 4]), ALU.mult),
                               g0("p", b), g0("T", b - 2)))

                def T(e):
                    for c in range(CB):
                        ins = e.matmul(bank(b % 3)[:, c * P:(c + 1) * P], G[b % 6][:, c, 0:P], Dg[b % 2][:, c, :],
                                       start=True, stop=True)
                    return ins
                put("T", b, op("pe", T, g0("D", b), g0("gs", b), g0("scan", b - 3)))

            pipeline([(4, lambda b: backend2(b, 1, bank(3), s1, Ob, H1)),
                      (3, lambda b: backend(b, 1, [bank(b % 3)], None, s1, Ob, H1, kR, g0("T", b), ALU.mult, ALU.add, 0.0)),
                      (2, L1_front), (0, L1_load)])

        def L1_nodes_L2_table():
            Q.barrier()
            arena.reset()
            state["last"] = None
            tk.clear()
            F = arena.get(NBLK, P)
            Y = arena.get(NBLK, P)
            Z = arena.get(NBLK, P)
            xT = arena.get(NBLK, P)
            big = arena.get(NBLK, 2 * P)
            gather_ends(H1, P, F)
            step("dve", lambda e: e.tensor_tensor(F, F, bf(has[:, :]), ALU.mult))
            step("dve", lambda e: e.tensor_scalar(small[:, 0, 0:1], epsc[:, :], 2.0, None, ALU.add))
            step("dve", lambda e: e.scalar_tensor_tensor(out=Y, in0=xn[:, :, :], scalar=small[:, 0, 0:1], in1=F,
                                                         op0=ALU.mult, op1=ALU.add))
            ln_plain(Y, Z)

            W1 = A["L2_gnn_W1"]
            load([lambda e: e.dma_start(W1ab[:, :], W1[0:P, :]),
                  lambda e: e.dma_start(wC[0:32, :], W1[P:P + 32, :]),
                  lambda e: e.dma_start(wC[32:33, :], A["L2_gnn_b1"].rearrange("(a n) -> a n", a=1))] +
                 [lambda e, i=i, n=n: e.dma_start(cols[:, 2 * i:2 * i + 2], A[n].rearrange("(h n) -> n h", n=P),
                                                  allow_slow_non_contiguous=True)
                  for i, n in enumerate(("L2_gnn_g1", "L2_gnn_be1"))])
            center(W1ab[:, :], 2 * P, P, 0)
            center(wC[0:33, :], 2 * P, 33, 1)
            transposed(xn, xT)
            table(xT, W1ab[:, :], 2 * P, T2, big)

        def L2_edges():
            Q.barrier()
            arena.reset()
            tk.clear()
            G = [arena.get(CB, 2 * P) for _ in range(8)]
            kR = [arena.get(GE, dt=BF16) for _ in range(4)]
            eT = [arena.get(GE) for _ in range(2)]
            Dg = [arena.get(CB, P) for _ in range(2)]
            hT = [arena.get(2, CB * P) for _ in range(2)]
            s2 = [arena.get(2, CB * P) for _ in range(2)]
            Ob = [arena.get(CB, 2 * P) for _ in range(3)]
            ja = arena.get(CB, 2 * P, dt=BF16)
            var = [arena.get(2 * CB) for _ in range(3)]
            rst = [arena.get(2 * CB) for _ in range(3)]
            nh_, na_ = arena.get(2 * CB), arena.get(2 * CB)
            for t in eT:
                op("dve", lambda e, t=t: e.memset(t[32:33, :], 1.0))
            Q.barrier()

            def L2_load(b):
                rows_load(b, kR, keepR)
                if b % 2 == 0:
                    g = b // 2
                    put("eT", g, dma("sp", e_sem[g % 2], lambda e: e.dma_start(
                        eT[g % 2][0:32, :], A["ea32T"][:, g * GE:(g + 1) * GE]), g0("C", b - 3)))
                put("gs", b, gather(gsem, b, T2, srcI, G[b % 8], g0("T", b - 8)))

            psC = PS[:, 0:1024]

            def L2_front(b):
                g, h0 = b // 2, (b % 2) * CB * P

                def C(e):
                    for c in range(CB):
                        ins = e.matmul(psC[:, c * 2 * P:(c + 1) * 2 * P], eT[g % 2][0:33, h0 + c * P:h0 + (c + 1) * P],
                                       wC[0:33, :], start=True, stop=True)
                    return ins
                put("C", b, op("pe", C, g0("eT", g), g0("t", b - 1)))

            def L2_t(b):
                t = G[b % 8]
                put("t", b, op("dve", lambda e: e.tensor_tensor(flat(t), flat(t), psC, ALU.add), g0("gs", b), g0("C", b)))


            def L2_sq(b):
                g, o, t = b // 2, b % 2 * CB, G[b % 8]

                def sq(e):
                    for c in range(CB):
                        ins = e.activation(ja[:, c, :], t[:, c, :], ACT.Square, accum_out=var[g % 3][:, o + c:o + c + 1])
                    return ins
                put("sq", b, op("act", sq, g0("t", b), g0("rs", 2 * g - 5), g0("sq", b - 1)))

            def L2_rstd(b):
                if b % 2 == 0:
                    return
                g = b // 2
                v = var[g % 3]
                tok = op("dve", lambda e: e.tensor_scalar(v, v, 1.0 / (2 * P), EPS, ALU.mult, ALU.add), g0("sq", b))
                tok = rsqrt(v, rst[g % 3], nh_, na_, tok, g0("D", b - 6))
                put("rs", b, tok)
                put("rs", b - 1, tok)

            def L2_D(b):
                o = b % 2 * CB
                put("D", b, op("dve", lambda e: e.tensor_tensor(Dg[b % 2], ident4(CB),
                                                                bf(rst[b // 2 % 3][:, o:o + CB]), ALU.mult),
                               g0("rs", b), g0("T", b - 2)))

            def L2_T(b):
                t = G[b % 8]

                def T(e):
                    for h in range(2):
                        for c in range(CB):
                            ins = e.matmul(bank(2 + h)[:, c * P:(c + 1) * P], t[:, c, h * P:(h + 1) * P],
                                           Dg[b % 2][:, c, :], start=True, stop=True)
                    return ins
                put("T", b, op("pe", T, g0("D", b), g0("sq", b), g0("r", b - 1)))

            def L2_r(b):
                def r(e):
                    for h in range(2):
                        ins = e.activation(hT[b % 2][:, h, :], bank(2 + h), ACT.Gelu, bias=cols[:, 2 + h:3 + h],
                                           scale=cols[:, h:h + 1])
                    return ins
                put("r", b, op("act", r, g0("T", b), g0("scan", b - 2)))

            def L2_scan(b):
                backend(b, 2, None, None, s2, Ob, H2, kR, g0("r", b), ALU.mult, ALU.add, 0.0,
                        srcs=[hT[b % 2][:, 0, :], hT[b % 2][:, 1, :]])

            def L2_back(b):
                backend2(b, 2, PS[:, 2048:3072], s2, Ob, H2)

            pipeline([(3, L2_t), (6, L2_T), (2, L2_front), (6, L2_r), (8, L2_back), (3, L2_sq), (7, L2_scan),
                      (4, L2_rstd), (5, L2_D), (0, L2_load)])


        def L2_nodes_L3_table():
            Q.barrier()
            arena.reset()
            state["last"] = None
            tk.clear()
            F = arena.get(NBLK, 2 * P)
            Y = arena.get(NBLK, P)
            Z = arena.get(NBLK, P)
            xT = arena.get(NBLK, P)
            aT = arena.get(NBLK, P)
            bT = arena.get(NBLK, P)
            load([lambda e: e.dma_start(wA[:, 0:P], A["L2_gnn_W2"][0:P, :]),
                  lambda e: e.dma_start(wA[:, P:2 * P], A["L2_gnn_W2"][P:2 * P, :]),
                  lambda e: e.dma_start(wB[:, 0:P], A["L2_gnn_Wu"][0:P, :]),
                  lambda e: e.dma_start(wB[:, P:2 * P], A["L2_gnn_Wu"][P:2 * P, :]),
                  lambda e: e.dma_start(wC[:, 0:P], A["WaT"][:, :]),
                  lambda e: e.dma_start(wD[:, 0:P], A["WbT"][:, :])] +
                 [lambda e, i=i, n=n: e.dma_start(v_[:, i, 0:P], row(A[n], P)) for i, n in enumerate(
                     ("L2_gnn_b2", "L2_gnn_bu", "L2_gnn_gu", "L2_gnn_beu", "L3_gnn_b"))])
            center(wB[:, 0:P], P, P, 0)
            center(wB[:, P:2 * P], P, P, 1)
            center(v_[:, 1, 0:P], P, P, 2)
            step("dve", lambda e: e.tensor_tensor(wC[:, 0:P], wC[:, 0:P], wD[:, 0:P], ALU.subtract))
            gather_ends(H2, 2 * P, F)
            step("dve", lambda e: e.tensor_tensor(F, F, bf(has[:, :], 2 * P), ALU.mult))
            transposed(F[:, :, 0:P], aT)
            transposed(F[:, :, P:2 * P], bT)
            product([(aT, wA[:, 0:P]), (bT, wA[:, P:2 * P])])
            step("dve", lambda e: e.tensor_tensor(Y, bc(v_[:, 0, 0:P]), bf(deg[:, :]), ALU.mult))
            step("dve", lambda e: e.tensor_tensor(Y, Y, PN, ALU.add))
            transposed(Y, aT)
            transposed(xn, xT)
            product([(xT, wB[:, 0:P]), (aT, wB[:, P:2 * P])])
            step("dve", lambda e: e.tensor_tensor(Y, PN, bc(v_[:, 1, 0:P]), ALU.add))
            ln_affine(Y, Z, v_[:, 2, 0:P], v_[:, 3, 0:P])
            step("act", lambda e: e.activation(Y, Y, ACT.Gelu))
            step("dve", lambda e: e.scalar_tensor_tensor(out=Y, in0=xn[:, :, :], scalar=2.0, in1=Y,
                                                         op0=ALU.mult, op1=ALU.add))
            ln_plain(Y, Z)

            transposed(xn, xT)
            product([(xT, wD[:, 0:P])])
            step("act", lambda e: e.activation(Y, PN, ACT.Copy))
            load([lambda e: e.dma_start(T3.rearrange("(b p) d -> p b d", p=P), Y)])

        def L3_edges():
            Q.barrier()
            arena.reset()
            tk.clear()
            G = [arena.get(CB, P) for _ in range(6)]
            kR = [arena.get(GE, dt=BF16) for _ in range(4)]
            s1 = [arena.get(1, CB * P) for _ in range(2)]
            Ob = [arena.get(CB, P) for _ in range(3)]

            def L3_load(b):
                rows_load(b, kR, negR)
                put("gs", b, gather(gsem[0:6], b, T3, srcI, G[b % 6], g0("T", b - 6)))

            def L3_front(b):
                def T(e):
                    for c in range(CB):
                        ins = e.transpose(bank(b % 3)[:, c * P:(c + 1) * P], G[b % 6][:, c, :], ident[:, :])
                    return ins
                put("T", b, op("pe", T, g0("gs", b), g0("scan", b - 3)))

            pipeline([(4, lambda b: backend2(b, 1, bank(3), s1, Ob, H3)),
                      (3, lambda b: backend(b, 1, [bank(b % 3)], None, s1, Ob, H3, kR, g0("T", b), ALU.add, ALU.max, -BIG)),
                      (2, L3_front), (0, L3_load)])

        def L3_nodes():
            Q.barrier()
            arena.reset()
            state["last"] = None
            tk.clear()
            F = arena.get(NBLK, P)
            Y = arena.get(NBLK, P)
            Z = arena.get(NBLK, P)
            xT = arena.get(NBLK, P)
            gather_ends(H3, P, F)
            transposed(xn, xT)
            product([(xT, wC[:, 0:P])])
            step("dve", lambda e: e.tensor_tensor(Y, PN, bc(v_[:, 4, 0:P]), ALU.add))
            step("dve", lambda e: e.tensor_tensor(Y, Y, F, ALU.add))
            step("dve", lambda e: e.tensor_tensor(Y, Y, bf(has[:, :]), ALU.mult))
            step("dve", lambda e: e.tensor_tensor(Y, Y, xn[:, :, :], ALU.add))
            ln_plain(Y, Z)
            nf = N // P
            load([lambda e: e.dma_start(out[0:nf * P, :].rearrange("(b p) d -> p b d", p=P), xn[:, 0:nf, :]),
                  lambda e: e.dma_start(out[nf * P:N, :], xn[0:N - nf * P, nf, :])])
            Q.barrier()

        edge_lists()
        L0_tables()
        L0_edges()
        L0_nodes()
        L1_table()
        L1_edges()
        L1_nodes_L2_table()
        L2_edges()
        L2_nodes_L3_table()
        L3_edges()
        L3_nodes()

        block = ctx.enter_context(nc.Block())

        @block.sync
        def _(e):
            for f in Q.q["sp"]:
                f(e)

        @block.tensor
        def _(e):
            for f in Q.q["pe"]:
                f(e)

        @block.vector
        def _(e):
            for f in Q.q["dve"]:
                f(e)

        @block.scalar
        def _(e):
            for f in Q.q["act"]:
                f(e)

        @block.gpsimd
        def _(e):
            for f in Q.q["pool"]:
                f(e)


def kernel(**inputs):
    import numpy as np
    import concourse.bacc as bacc
    from concourse.bass_utils import run_bass_kernel_spmd

    a = {k: np.asarray(v) for k, v in inputs.items()}

    def padded(v, n, fill):
        return np.concatenate([v, np.full((n - v.shape[0],) + v.shape[1:], fill, v.dtype)], 0)

    x = padded(a.pop("x"), NPAD, 0)
    src = padded(a.pop("src"), EP, DUMMY)
    dst = a.pop("dst")
    dst = np.concatenate([np.full((1,), -1, dst.dtype), padded(dst, EP, DUMMY)])
    ew = padded(a.pop("edge_weight"), EP, 0)
    e32 = np.ascontiguousarray(padded(a.pop("edge_attr_32"), EP, 0).T)
    e64 = np.ascontiguousarray(padded(a.pop("edge_attr_64"), EP, 0).T)
    W = a.pop("L3_gnn_W")
    arrays = {"x": x, "src": src, "dst": dst, "edge_weight": ew, "ea32T": e32, "ea64T": e64,
              "WaT": np.ascontiguousarray(W[:, 0:P].T), "WbT": np.ascontiguousarray(W[:, P:2 * P].T)}
    arrays.update(a)
    nc = bacc.Bacc("TRN2", target_bir_lowering=False, num_devices=1)
    feed, A = {}, {}
    for name, v in arrays.items():
        feed[f"in_{name}"] = np.ascontiguousarray(v)
        A[name] = nc.dram_tensor(f"in_{name}", v.shape, mybir.dt.from_np(v.dtype), kind="ExternalInput").ap()
    out = nc.dram_tensor("out_x", (N, P), F32, kind="ExternalOutput").ap()
    build(nc, A, out)
    r = run_bass_kernel_spmd(nc, [feed], core_ids=[0])
    return r.results[0]["out_x"]
```

```python
import concourse.bass as bass
from concourse import mybir
from contextlib import ExitStack

P = 128
N = 3125
NBLK = 25
NPAD = NBLK * P
DUMMY = NPAD - 1
E = 100000
NCH = 784
EP = NCH * P
CB = 4
NBAT = NCH // CB
NG = NBAT // 2
GE = 2 * CB * P
TR = NPAD + P
KT = 4
XW = 132
BIG = 3.0e38
MASK = 2.0 ** 120
MAGIC = float(0x5f3759df)
EPS = 1e-5

F32 = mybir.dt.float32
BF16 = mybir.dt.bfloat16
I32 = mybir.dt.int32
ALU = mybir.AluOpType
ACT = mybir.ActivationFunctionType
AX = mybir.AxisListType.X


class Queues:

    def __init__(self, nc, ctx, prefix="s_"):
        self.nc, self.ctx = nc, ctx
        self.q = {n: [] for n in ("pe", "dve", "act", "pool", "sp")}
        self.seen = {n: {} for n in self.q}
        self.count = {}
        self.sems = {}
        self.own = {n: self.sem(prefix + n) for n in self.q}

    def sem(self, name):
        s = self.ctx.enter_context(self.nc.semaphore(name))
        self.sems[name] = s
        self.count[name] = 0
        return name

    def wait(self, eng, after):
        for tok in after:
            if tok is None:
                continue
            if isinstance(tok, list):
                self.wait(eng, tok)
                continue
            name, v = tok
            if self.seen[eng].get(name, 0) < v:
                self.seen[eng][name] = v
                s = self.sems[name]
                self.q[eng].append(lambda e, s=s, v=v: e.wait_ge(s, v))

    def op(self, eng, fn, *after):
        self.wait(eng, after)
        name = self.own[eng]
        self.count[name] += 1
        s = self.sems[name]
        self.q[eng].append(lambda e: fn(e).then_inc(s, 1))
        return (name, self.count[name])

    def dma(self, eng, name, fn, *after):
        self.wait(eng, after)
        self.count[name] += 16
        s = self.sems[name]
        self.q[eng].append(lambda e: fn(e).then_inc(s, 16))
        return (name, self.count[name])

    def dma_either(self, eng, name, cond, yes, no, *after):
        self.wait(eng, after)
        self.count[name] += 16
        s = self.sems[name]

        def go(e):
            with e.If(cond()):
                yes(e).then_inc(s, 16)
            with e.Else():
                no(e).then_inc(s, 16)
        self.q[eng].append(go)
        return (name, self.count[name])

    def branch(self, other, cond):
        for eng, q in self.q.items():
            def go(e, eng=eng, sub=list(other.q[eng])):
                with e.If(cond(eng)):
                    for f in sub:
                        f(e)
            q.append(go)

    def barrier(self):
        toks = [(n, c) for n, c in self.count.items() if c]
        for eng in self.q:
            self.wait(eng, toks)


class Arena:

    def __init__(self, t, words):
        self.t, self.words, self.at = t, words, 0

    def reset(self):
        self.at = 0

    def get(self, *shape, dt=F32):
        n = 1
        for s in shape:
            n *= s
        w = n if dt != BF16 else (n + 1) // 2
        w = (w + 7) // 8 * 8
        assert self.at + w <= self.words, (self.at, w)
        v = self.t[:, self.at:self.at + w]
        self.at += w
        if dt != F32:
            v = v.bitcast(dt)
        v = v[:, 0:n]
        if len(shape) == 2:
            v = v.rearrange("p (a b) -> p a b", b=shape[1])
        if len(shape) == 3:
            v = v.rearrange("p (a b c) -> p a b c", b=shape[1], c=shape[2])
        return v


def build(nc, A, out):
    with ExitStack() as ctx:
        Q = Queues(nc, ctx)
        op, dma = Q.op, Q.dma

        def sb(name, shape, dt=F32):
            return ctx.enter_context(nc.sbuf_tensor(name, [P] + shape, dt))

        def dram(name, shape, dt=F32):
            return nc.dram_tensor(name, shape, dt).ap()

        AW = 40400
        arena = Arena(sb("arena", [AW]), AW)
        PS = ctx.enter_context(nc.psum_tensor("PS", [P, 4096], F32))

        def bank(i, n=512):
            return PS[:, 512 * i:512 * i + n]

        ident = sb("ident", [P])
        ltri = sb("ltri", [P])
        iotaf = sb("iotaf", [P])
        pcol = sb("pcol", [1])
        nodeid = sb("nodeid", [NBLK])
        onesF = sb("onesF", [P])
        xn = sb("xn", [NBLK, P])
        srcF = sb("srcF", [NCH])
        srcI = sb("srcI", [NCH], I32)
        dstF = sb("dstF", [NCH])
        loF = sb("loF", [NCH])
        hiF = sb("hiF", [NCH])
        idxG = sb("idxG", [NCH], I32)
        wcol = sb("wcol", [NG])
        d0I = sb("d0I", [NG], I32)
        flag = sb("flag", [2], I32)
        eF = sb("eF", [NCH])
        beta = sb("beta", [1])
        epsc = sb("epsc", [1])
        endI = sb("endI", [NBLK], I32)
        deg = sb("deg", [NBLK])
        has = sb("has", [NBLK])
        Mx = sb("Mx", [NBLK])
        Sx = sb("Sx", [NBLK])
        small = sb("small", [16, NBLK])
        W1ab = sb("W1ab", [2 * P])
        We = sb("We", [2 * P])
        cols = sb("cols", [8])
        wA = sb("wA", [2 * P])
        wB = sb("wB", [2 * P])
        wC = sb("wC", [2 * P])
        wD = sb("wD", [2 * P])
        vec = sb("vec", [5, P])
        onep = sb("onep", [1])
        wX = sb("wX", [2 * P], BF16)
        wY = sb("wY", [2 * P], BF16)

        dF = dram("dF", (EP,))
        sF = dram("sF", (EP,))
        wF = dram("wF", (EP,))
        keepR = dram("keepR", (EP,), BF16)
        negR = dram("negR", (EP,), BF16)
        ubR = dram("ubR", (NPAD + 1,))
        T0b = dram("T0b", (TR, 2 * P))
        keyR = dram("keyR", (EP,), I32)
        Rs = dram("Rs", (EP, 99))
        eTs = dram("eTs", (96, EP))
        srt = dram("srt", (3, EP + 1))
        S32 = dram("S32", (P, EP), BF16)
        T0 = dram("T0", (NPAD, 2 * P))
        T1 = dram("T1", (NPAD, XW))
        T2 = dram("T2", (NPAD, 2 * P))
        T3 = dram("T3", (NPAD, P))
        tabs = [dram(f"tab{k}", (TR, XW)) for k in range(KT)]
        H0 = dram("H0", (EP, P))
        H1 = dram("H1", (EP, P))
        H2 = dram("H2", (EP, 2 * P))
        H3 = dram("H3", (EP, P))

        s_ld = Q.sem("s_ld")
        s_st = Q.sem("s_st")
        s_init = Q.sem("s_init")
        s_g = Q.sem("s_g")
        s_h = Q.sem("s_h")

        def row(v, n):
            return v.rearrange("(a n) -> a n", a=1).to_broadcast([P, n])

        state = {"last": None}

        def step(eng, fn):
            state["last"] = op(eng, fn, state["last"])
            return state["last"]

        def load(fns, eng="sp", sem=s_ld):
            for fn in fns:
                tok = dma(eng, sem, fn, state["last"])
            state["last"] = [state["last"], tok]
            return tok

        op("pool", lambda e: e.memset(ident[:, :], 0.0))
        op("pool", lambda e: e.memset(ltri[:, :], 1.0))
        op("pool", lambda e: e.memset(onesF[:, :], 1.0))
        op("pool", lambda e: e.iota(iotaf[:, :], [[1, P]], base=0, channel_multiplier=0,
                                    allow_small_or_imprecise_dtypes=True))
        op("pool", lambda e: e.iota(pcol[:, :], [[0, 1]], base=NPAD, channel_multiplier=1,
                                    allow_small_or_imprecise_dtypes=True))
        a = op("pool", lambda e: e.iota(nodeid[:, :], [[P, NBLK]], base=0, channel_multiplier=1,
                                        allow_small_or_imprecise_dtypes=True))
        op("pool", lambda e: e.affine_select(out=ident[:, :], in_=ident[:, :], compare_op=ALU.not_equal, fill=1.0,
                                             base=0, pattern=[[-1, P]], channel_multiplier=1), a)
        a = op("pool", lambda e: e.affine_select(out=ltri[:, :], in_=ltri[:, :], compare_op=ALU.is_gt, fill=0.0,
                                                 base=0, pattern=[[-1, P]], channel_multiplier=1), a)
        state["last"] = a

        def bc(v, n=NBLK):
            return v.unsqueeze(1).to_broadcast([P, n, v.shape[1]])

        def bf(v, f=P):
            return v.unsqueeze(2).to_broadcast([P, v.shape[1], f])

        def flat(v):
            return v.rearrange("p a b -> p (a b)")

        PN = PS[:, 0:NPAD].rearrange("p (b f) -> p b f", f=P)

        def center(w, n, parts, c):
            step("dve", lambda e: e.tensor_reduce(small[0:parts, 6, c:c + 1], w, AX, ALU.add))
            step("dve", lambda e: e.tensor_scalar(small[0:parts, 7, c:c + 1], small[0:parts, 6, c:c + 1],
                                                  1.0 / n, None, ALU.mult))
            step("dve", lambda e: e.tensor_scalar(w, w, small[0:parts, 7, c:c + 1], None, ALU.subtract))

        def transposed(src, dst):
            def go(e):
                for b in range(NBLK):
                    ins = e.transpose(PN[:, b, :], src[:, b, :], ident[:, :])
                return ins
            step("pe", go)
            step("act", lambda e: e.activation(dst, PN, ACT.Copy))

        def table(xT, w, width, T, big, bias=None):
            for b0 in range(0, NBLK, 13):
                nb_ = min(13, NBLK - b0)

                def go(e, b0=b0, nb_=nb_):
                    for b in range(nb_):
                        ins = e.matmul(PS[:, b * width:(b + 1) * width], xT[:, b0 + b, :], w, start=True, stop=True)
                    return ins
                step("pe", go)
                if bias is None:
                    step("act", lambda e, b0=b0, nb_=nb_: e.activation(
                        flat(big)[:, b0 * width:(b0 + nb_) * width], PS[:, 0:nb_ * width], ACT.Copy))
                else:
                    step("dve", lambda e, b0=b0, nb_=nb_: e.tensor_tensor(
                        big[:, b0:b0 + nb_, :], PS[:, 0:nb_ * width].rearrange("p (b f) -> p b f", f=width),
                        bc(bias, nb_), ALU.add))
            load([lambda e: e.dma_start(T.rearrange("(b p) d -> p b d", p=P), big)])

        def rsqrt_steps(v, rs, h, a):
            def guess(e):
                e.tensor_scalar(h, v, -0.5, None, ALU.mult)
                return e.tensor_scalar(a.bitcast(I32), v.bitcast(I32), 1, None, ALU.logical_shift_right)
            steps = [guess, lambda e: e.tensor_scalar(rs.bitcast(I32), a.bitcast(I32), -1.0, MAGIC,
                                                      ALU.mult, ALU.add)]
            for _ in range(3):
                steps += [lambda e: e.tensor_tensor(a, rs, rs, ALU.mult),
                          lambda e: e.tensor_tensor(a, a, h, ALU.mult),
                          lambda e: e.scalar_tensor_tensor(out=rs, in0=a, scalar=1.5, in1=rs,
                                                           op0=ALU.add, op1=ALU.mult)]
            return steps

        def rsqrt(v, rs, h, a, *after):
            toks = list(after)
            for fn in rsqrt_steps(v, rs, h, a):
                toks = [op("dve", fn, *toks)]
            return toks[0]

        HALF = ((0, 12), (12, NBLK))

        def halves(stages, starts=(None, None)):
            last = [[state["last"], t] for t in starts]
            for st in stages:
                for i, (a, b) in enumerate(HALF):
                    state["last"] = last[i]
                    st(a, b)
                    last[i] = state["last"]
            state["last"] = last

        def on(eng, fn):
            return lambda a, b: step(eng, lambda e: fn(e, slice(a, b)))

        def turn(src):
            def go(a, b):
                def tr(e):
                    for i in range(a, b):
                        ins = e.transpose(PN[:, i, :], src[:, i, :], ident[:, :])
                    return ins
                step("pe", tr)
            return go

        def out_of_psum(dst, func=ACT.Copy, **kw):
            return on("act", lambda e, s: e.activation(dst[:, s, :], PN[:, s, :], func, **kw))

        def times(pairs):
            def go(a, b):
                def mm(e):
                    for i in range(a, b):
                        for n, (t, w) in enumerate(pairs):
                            ins = e.matmul(PN[:, i, :], t[:, i, :], w, start=(n == 0), stop=(n == len(pairs) - 1))
                    return ins
                step("pe", mm)
            return go

        def row_sums(src, junk, k, func):
            def go(a, b):
                def acc(e):
                    for i in range(a, b):
                        ins = e.activation(junk[:, i, :], src[:, i, :], func, accum_out=small[:, k, i:i + 1])
                    return ins
                if a == 0:
                    step("act", acc)
                    return
                t = src[:, a:b, :]
                if func == ACT.Square:
                    t = junk[:, a:b, :]
                    step("dve", lambda e: e.tensor_tensor(t, src[:, a:b, :], src[:, a:b, :], ALU.mult))
                step("dve", lambda e: e.tensor_reduce(small[:, k, a:b], t, AX, ALU.add))
            return go

        def inverse_root(k, r):
            n = len(rsqrt_steps(*[small[:, i, 0:1] for i in (k, r, 14, 15)]))
            return [lambda a, b, j=j: step("dve", rsqrt_steps(*[small[:, i, a:b] for i in (k, r, 14, 15)])[j])
                    for j in range(n)]

        def rstd(y, junk):
            return [row_sums(y, junk, 8, ACT.Square),
                    on("dve", lambda e, s: e.tensor_scalar(small[:, 8, s], small[:, 8, s], 1.0 / P, EPS,
                                                           ALU.mult, ALU.add))] + inverse_root(8, 9)

        def scaled(dst, y, k):
            return on("dve", lambda e, s: e.tensor_tensor(dst[:, s, :], y[:, s, :], bf(small[:, k, s]), ALU.mult))

        def norm_to_x(y, junk):
            return [row_sums(y, junk, 8, ACT.Copy),
                    on("dve", lambda e, s: e.tensor_scalar(small[:, 10, s], small[:, 8, s], 1.0 / P, None, ALU.mult)),
                    on("dve", lambda e, s: e.tensor_tensor(y[:, s, :], y[:, s, :], bf(small[:, 10, s]),
                                                           ALU.subtract))] + rstd(y, junk) + [scaled(xn, y, 9)]

        def gather_ends(H, dst):
            toks = []
            for (a, b), sem in zip(HALF, (s_g, s_h)):
                for i in range(a, b):
                    tok = dma("pool", sem, lambda e, i=i: e.indirect_dma_start(
                        out=dst[:, i, :], out_offset=None, in_=H,
                        in_offset=bass.IndirectOffsetOnAxis(ap=endI[:, i:i + 1], axis=0)))
                toks.append(tok)
            return toks

        B7 = PS[:, 3584:3712]

        def folded(w2, w2T, u2, dst, b2col, ones_b2, crow):
            for w, wt, d in zip(w2, w2T, dst):
                step("pe", lambda e, w=w: e.transpose(B7, w, ident[:, :]))
                step("act", lambda e, wt=wt: e.activation(wt, B7, ACT.Copy))
                step("pe", lambda e, wt=wt: e.matmul(B7, wt, u2, start=True, stop=True))
                step("act", lambda e, d=d: e.activation(d, B7, ACT.Copy))
            step("dve", lambda e: e.tensor_scalar(ones_b2, onesF[:, :], b2col, None, ALU.mult))
            step("pe", lambda e: e.matmul(B7, ones_b2, u2, start=True, stop=True))
            step("act", lambda e: e.activation(crow, B7, ACT.Copy))

        ring_sems = {}

        def ring(name, n):
            if name not in ring_sems:
                ring_sems[name] = [Q.sem(f"{name}{i}") for i in range(n)]
            return ring_sems[name]

        def gather(sems, b, T, idx, dst, *after):
            s = sems[b % len(sems)]
            for c in range(CB):
                tok = dma("pool", s, lambda e, c=c: e.indirect_dma_start(
                    out=dst[:, c, :], out_offset=None, in_=T,
                    in_offset=bass.IndirectOffsetOnAxis(ap=idx[:, CB * b + c:CB * b + c + 1], axis=0)), *after)
            return tok

        def pipeline(stages):
            last = max(lag for lag, _ in stages)
            for i in range(NBAT + last):
                for lag, fn in stages:
                    if 0 <= i - lag < NBAT:
                        fn(i - lag)

        def ident4(n):
            return ident[:, :].unsqueeze(1).to_broadcast([P, n, P])

        gs_sem, gx_sem = ring("gs", 10), ring("gx", 1)
        e_sem, s_sem, w_sem, k_sem = ring("le", 3), ring("lsr", 3), ring("lw", 3), ring("lk", 6)
        d_sem, t_sem = ring("ld", 3), ring("ltw", 4)
        o_sem, tab_sem = ring("so", 3), ring("tb", KT)
        tk = {}

        def g0(name, b):
            return tk.get((name, b))

        def put(name, b, tok):
            tk[(name, b)] = tok
            return tok

        def grow(v, g):
            return row(v[g * GE:(g + 1) * GE], GE)

        def backend(b, nh, psT, psB, s, Ob, H, rowsR, after_T, op0, op1, init, srcs=None):
            g, h0 = b // 2, (b % 2) * CB * P
            kr = rowsR[g % len(rowsR)][:, h0:h0 + CB * P]

            def scan(e):
                for h in range(nh):
                    ins = e.tensor_tensor_scan(s[b % 2][:, h, :], kr, psT[h] if srcs is None else srcs[h],
                                               s[(b - 1) % 2][:, h, CB * P - 1:CB * P] if b else init, op0, op1)
                return ins
            put("scan", b, op("dve", scan, after_T, g0("kR", g), g0("scan", b - 1), g0("B", b - 2)))

        def backend2(b, nh, psB, s, Ob, H):
            def B(e):
                for c in range(CB):
                    for h in range(nh):
                        ins = e.transpose(psB[:, (c * nh + h) * P:(c * nh + h + 1) * P],
                                          s[b % 2][:, h, c * P:(c + 1) * P], ident[:, :])
                return ins
            put("B", b, op("pe", B, g0("scan", b), g0("O", b - 1)))
            put("O", b, op("act", lambda e: e.activation(flat(Ob[b % 3]), psB, ACT.Copy),
                           g0("B", b), g0("so", b - 3)))
            put("so", b, dma("sp", o_sem[b % 3], lambda e: e.dma_start(
                H[b * CB * P:(b + 1) * CB * P, :].rearrange("(c p) f -> p c f", p=P), Ob[b % 3]), g0("O", b)))

        def rows_load(b, rowsR, R, n=4):
            if b % 2 == 0:
                g = b // 2
                put("kR", g, dma("sp", k_sem[g % n], lambda e: e.dma_start(rowsR[g % n], grow(R, g)),
                                 g0("scan", b - 2 * n + 1)))

        v_ = vec[:, :, :]
        gsem = gs_sem

        unsorted = {}

        def sort_by_destination(dI, dFt, sFt, wI, dPf):
            L = Queues(nc, ctx, "f_")
            s_l, s_k, s_r = L.sem("f_l"), L.sem("f_k"), L.sem("f_r")
            for eng in Q.q:
                Q.wait(eng, [state["last"]])
                Q.q[eng].append(lambda e, eng=eng: unsorted.update(
                    {eng: e.value_load(flag[0:1, 1:2], min_val=0, max_val=EP)}))
            KW = EP // 8
            keyI = arena.get(NCH, dt=I32)
            eI = arena.get(NCH, dt=I32)
            rk = arena.get(NCH)
            rank = arena.get(NCH)
            rankI = arena.get(NCH, dt=I32)
            neg1 = arena.get(1)
            at = arena.at
            keys = arena.get(KW)
            jk = arena.get(KW, dt=BF16)
            l = L.op("pool", lambda e: e.iota(eI, [[1, NCH]], base=0, channel_multiplier=NCH))
            l = L.op("dve", lambda e: e.tensor_scalar(keyI, dI, 17, 0x40000000, ALU.logical_shift_left,
                                                      ALU.bitwise_or), l)
            l = L.op("dve", lambda e: e.tensor_tensor(keyI, keyI, eI, ALU.bitwise_or), l)
            z = L.op("dve", lambda e: e.memset(neg1, -1.0))
            z = L.op("dve", lambda e: e.memset(rank, 0.0))
            l = L.dma("sp", s_l, lambda e: e.dma_start(keyR.rearrange("(p j) -> p j", j=NCH), keyI), l)
            col = keyI.bitcast(F32)
            loop_sem = L.sem("f_loop")
            for w in range(8):
                k = L.dma("sp", s_k, lambda e, w=w: e.dma_start(
                    keys.bitcast(I32), row(keyR[w * KW:(w + 1) * KW], KW)), l, z)
                L.wait("dve", [k])

                def count(e, w=w):
                    s = L.sems[loop_sem]
                    with e.Fori(0, NCH) as j:
                        e.tensor_scalar(jk, keys, col[:, bass.ds(j, 1)], 0.0, ALU.is_lt, ALU.add,
                                        accum_out=rk[:, bass.ds(j, 1)]).then_inc(s, 1)
                        e.wait_ge(s, j + (w * NCH + 1))
                    e.wait_ge(s, (w + 1) * NCH)
                    return e.tensor_tensor(rank, rank, rk, ALU.add)
                z = L.op("dve", count)
                L.wait("dve", [z])
            l = L.op("dve", lambda e: e.tensor_copy(rankI, rank), z)
            arena.at = at
            J = 14
            FW = 99
            R = [arena.get(J, FW) for _ in range(2)]
            O = [arena.get(J * P) for _ in range(2)]
            L.barrier()
            rl = [[L.sem(f"f_r{i}{n}") for n in range(2)] for i in range(2)]
            rs = [L.sem(f"f_s{i}") for i in range(2)]
            done = {}
            with nc.allow_non_contiguous_dma(reason="edge features beside each other"):
                for q in range(NCH // J):
                    j0, r = q * J, R[q % 2]
                    a = L.dma("sp", rl[q % 2][0], lambda e, r=r, j0=j0: e.dma_start(
                        r[:, :, 0:64], A["ea64"].rearrange("(p j) f -> p j f", j=NCH)[:, j0:j0 + J, :]), done.get(q - 2))
                    b = L.dma("sp", rl[q % 2][1], lambda e, r=r, j0=j0: e.dma_start(
                        r[:, :, 64:96], A["ea32"].rearrange("(p j) f -> p j f", j=NCH)[:, j0:j0 + J, :]), done.get(q - 2))

                    def lists(e, r=r, j0=j0):
                        e.tensor_copy(r[:, :, 96], dFt[:, j0:j0 + J])
                        e.tensor_copy(r[:, :, 97], sFt[:, j0:j0 + J])
                        return e.tensor_copy(r[:, :, 98], wI[:, j0:j0 + J])
                    c = L.op("dve", lists, done.get(q - 2))
                    for j in range(J):
                        done[q] = L.dma("pool", rs[q % 2], lambda e, r=r, j=j, j0=j0: e.indirect_dma_start(
                            out=Rs, out_offset=bass.IndirectOffsetOnAxis(ap=rankI[:, j0 + j:j0 + j + 1], axis=0),
                            in_=r[:, j, :], in_offset=None), a, b, c)
            L.barrier()
            ws = [L.sem(f"f_w{i}") for i in range(2)]
            done, ld = {}, {}
            L.dma("sp", s_l, lambda e: e.dma_start(srt[0:1, 0:1], neg1[0:1, :]))
            for q in range(NCH // J):
                r, o = R[q % 2], O[q % 2]
                a = L.dma("sp", rl[q % 2][0], lambda e, r=r, q=q: e.dma_start(
                    r, Rs[q * J * P:(q + 1) * J * P, :].rearrange("(j p) f -> p j f", p=P)), ld.get(q - 2))

                def tr(e, r=r):
                    for j in range(J):
                        ins = e.transpose(PS[0:FW, j * P:(j + 1) * P], r[:, j, :], ident[:, :])
                    return ins
                ld[q] = t = L.op("pe", tr, a, done.get(q - 1))
                c = L.op("dve", lambda e, o=o: e.tensor_copy(o[0:FW, :], PS[0:FW, 0:J * P]), t, done.get(q - 2))
                L.dma("sp", ws[q % 2], lambda e, o=o, q=q: e.dma_start(
                    eTs[:, q * J * P:(q + 1) * J * P], o[0:96, :]), c)
                done[q] = L.dma("sp", ws[q % 2], lambda e, o=o, q=q: e.dma_start(
                    srt[:, 1 + q * J * P:1 + (q + 1) * J * P], o[96:99, :]), c)
            L.barrier()
            for i, (t, o) in enumerate(((dFt, 1), (sFt, 1), (wI, 1), (dPf, 0))):
                L.dma("sp", s_r, lambda e, i=i, t=t, o=o: e.dma_start(
                    t, srt[i % 3, o:o + EP].rearrange("(p j) -> p j", j=NCH)))
            L.barrier()
            Q.branch(L, lambda eng: unsorted[eng] > 0)

        def edge_features(n0, n, t, c0):
            src = A["ea64T"] if n == 64 else A["ea32T"]
            return (lambda: unsorted["sp"] > 0,
                    lambda e: e.dma_start(t, eTs[n0:n0 + n, c0:c0 + GE]),
                    lambda e: e.dma_start(t, src[:, c0:c0 + GE]))

        def edge_lists():
            w1 = A["L0_gnn_msg_w1"]
            dI = arena.get(NCH, dt=I32)
            dP = arena.get(NCH, dt=I32)
            dPf = arena.get(NCH)
            sI = arena.get(NCH, dt=I32)
            wI = arena.get(NCH)
            dFt = arena.get(NCH)
            sFt = arena.get(NCH)
            kt = arena.get(NCH)
            kb = arena.get(NCH, dt=BF16)
            nb = arena.get(NCH, dt=BF16)

            load([
                lambda e: e.dma_start(dI, A["dst"][1:EP + 1].rearrange("(p j) -> p j", j=NCH)),
                lambda e: e.dma_start(dP, A["dst"][0:EP].rearrange("(p j) -> p j", j=NCH)),
                lambda e: e.dma_start(sI, A["src"].rearrange("(p j) -> p j", j=NCH)),
                lambda e: e.dma_start(wI, A["edge_weight"].rearrange("(p j) -> p j", j=NCH)),
                lambda e: e.dma_start(xn[:, :, :], A["x"].rearrange("(b p) d -> p b d", p=P)),
                lambda e: e.dma_start(W1ab[:, 0:P], w1[0:P, :]),
                lambda e: e.dma_start(W1ab[:, P:2 * P], w1[P:2 * P, :]),
                lambda e: e.dma_start(We[0:64, 0:P], w1[2 * P:2 * P + 64, :]),
                lambda e: e.dma_start(We[64:65, 0:P], A["L0_gnn_msg_b1"].rearrange("(a n) -> a n", a=1)),
                lambda e: e.dma_start(cols[:, 0:1], A["L0_gnn_ln1_g"].rearrange("(n a) -> n a", a=1)),
                lambda e: e.dma_start(cols[:, 1:2], A["L0_gnn_ln1_b"].rearrange("(n a) -> n a", a=1)),
                lambda e: e.dma_start(beta[:, :], row(A["L1_gnn_beta"], 1)),
                lambda e: e.dma_start(epsc[:, :], row(A["L1_gnn_eps"], 1)),
            ])

            def floats(e):
                e.tensor_copy(dFt, dI)
                e.tensor_copy(sFt, sI)
                return e.tensor_copy(dPf, dP)
            step("dve", floats)
            step("dve", lambda e: e.tensor_tensor(kt, dPf, dFt, ALU.is_gt))
            step("dve", lambda e: e.tensor_reduce(small[:, 0, 0:1], kt, AX, ALU.add))
            step("pe", lambda e: e.matmul(PS[:, 0:1], onesF[:, :], small[:, 0, 0:1], start=True, stop=True))
            step("dve", lambda e: e.tensor_copy(flag[:, 1:2], PS[:, 0:1]))
            mark = arena.at
            sort_by_destination(dI, dFt, sFt, wI, dPf)
            arena.at = mark
            rows = arena.get(3, 7, P)
            sampB = arena.get(NCH)
            junk = arena.get(NCH)
            zero = arena.get(TR // P * XW)
            sub = arena.get(NBLK, P)
            op("pool", lambda e: e.memset(zero, 0.0), state["last"])
            zeroed = op("pool", lambda e: e.memset(onep[:, :], 0.0))

            def conv(e):
                e.tensor_tensor(kt, dFt, dPf, ALU.is_equal)
                return e.tensor_scalar(wI, wI, beta[:, 0:1], None, ALU.mult)
            step("dve", conv)

            def conv2(e):
                e.tensor_copy(kb, kt)
                return e.tensor_scalar(nb, kt, -1.0, BIG, ALU.add, ALU.mult)
            step("dve", conv2)
            load([
                lambda e: e.dma_start(dF.rearrange("(p j) -> p j", j=NCH), dFt),
                lambda e: e.dma_start(sF.rearrange("(p j) -> p j", j=NCH), sFt),
                lambda e: e.dma_start(wF.rearrange("(p j) -> p j", j=NCH), wI),
            ])
            load([lambda e, i=i, t=t: e.dma_start(rows[0:112, i, :, :], t.rearrange("(t q p) -> q t p", q=112, p=P))
                  for i, t in enumerate((sF, dF, wF))])
            dma("sp", s_init, lambda e: e.dma_start(keepR.rearrange("(p j) -> p j", j=NCH), kb))
            dma("sp", s_init, lambda e: e.dma_start(negR.rearrange("(p j) -> p j", j=NCH), nb))
            dma("sp", s_init, lambda e: e.dma_start(T0b[NPAD:TR, :], zero[:, 0:2 * P]), zeroed)
            for k in range(KT):
                dma("sp", s_init, lambda e, k=k: e.dma_start(
                    tabs[k].rearrange("(p r) c -> p (r c)", p=P), zero), zeroed)

            def tr_lists(e):
                for i in range(3):
                    for t in range(7):
                        o = 1024 * i + 112 * t + (64 if t >= 4 else 0)
                        ins = e.transpose(PS[:, o:o + 112], rows[0:112, i, t, :], ident[0:112, 0:112])
                return ins
            step("pe", tr_lists)

            def ev_lists(e):
                for i, d in enumerate((srcF, dstF, eF)):
                    e.tensor_copy(d[:, 0:448], PS[:, 1024 * i:1024 * i + 448])
                    ins = e.tensor_copy(d[:, 448:784], PS[:, 1024 * i + 512:1024 * i + 848])
                    if i == 0:
                        e.tensor_copy(srcI[:, 0:448], PS[:, 0:448])
                        e.tensor_copy(srcI[:, 448:784], PS[:, 512:848])
                return ins
            step("dve", ev_lists)

            def first_dst(e):
                e.matmul(PS[:, 3072:3584], onesF[0:1, :], dstF[0:1, 0:512], start=True, stop=True)
                return e.matmul(PS[:, 3584:3856], onesF[0:1, :], dstF[0:1, 512:784], start=True, stop=True)
            step("pe", first_dst)
            step("dve", lambda e: e.tensor_copy(sampB, PS[:, 3072:3856]))
            lists = state["last"]
            L0_tables()
            state["last"] = lists

            for b in range(NBLK):
                step("dve", lambda e, b=b: e.tensor_scalar(junk, sampB, nodeid[:, b:b + 1], 0.0, ALU.is_le, ALU.add,
                                                           accum_out=small[:, 0, b:b + 1]))
            kI = small[:, 1, :].bitcast(I32)
            step("dve", lambda e: e.tensor_scalar(small[:, 2, :], small[:, 0, :], -1.0, 0.0, ALU.add, ALU.max))
            step("dve", lambda e: e.tensor_copy(kI, small[:, 2, :]))
            dFc = dF.rearrange("(s i) -> s i", i=P)
            state["last"], lists = dma("pool", s_g, lambda e: e.indirect_dma_start(
                out=sub[:, 0, :], out_offset=None, in_=dFc,
                in_offset=bass.IndirectOffsetOnAxis(ap=kI[:, 0:1], axis=0)), state["last"]), state["last"]
            for b in range(1, NBLK):
                state["last"] = dma("pool", s_g, lambda e, b=b: e.indirect_dma_start(
                    out=sub[:, b, :], out_offset=None, in_=dFc,
                    in_offset=bass.IndirectOffsetOnAxis(ap=kI[:, b:b + 1], axis=0)))
            gathered, state["last"] = state["last"], lists

            loI, hiI = arena.get(NCH, dt=I32), arena.get(NCH, dt=I32)
            d0B, rel, out_w = arena.get(NG), arena.get(NG, 8), arena.get(NG, 8)

            def digits(e):
                e.tensor_scalar(loI, srcI[:, :], 127, None, ALU.bitwise_and)
                e.tensor_copy(d0B, sampB.rearrange("p (g c) -> p g c", c=8)[:, :, 0])
                e.tensor_scalar(small[:, 12, 0:1], pcol[:, :], -float(NPAD), None, ALU.add)
                return e.tensor_scalar(hiI, srcI[:, :], 7, None, ALU.logical_shift_right)
            step("dve", digits)

            def windows(e):
                e.tensor_copy(loF[:, :], loI)
                e.tensor_copy(hiF[:, :], hiI)
                e.tensor_scalar(wcol[:, :], d0B, small[:, 12, 0:1], None, ALU.add)
                e.tensor_copy(d0I[:, :], d0B)
                return e.tensor_tensor(rel, dstF[:, :].rearrange("p (g c) -> p g c", c=8), bf(d0B, 8), ALU.subtract)
            step("dve", windows)
            step("dve", lambda e: e.tensor_scalar(out_w, rel, float(P), None, ALU.is_ge))
            fl = out_w.rearrange("p g c -> p (g c)")

            def outside(e):
                e.tensor_reduce(small[:, 13, 0:1], fl, AX, ALU.add)
                return e.scalar_tensor_tensor(out=rel.rearrange("p g c -> p (g c)"), in0=dstF[:, :],
                                              scalar=-float(DUMMY), in1=fl, op0=ALU.add, op1=ALU.mult)
            step("dve", outside)
            step("dve", lambda e: e.tensor_scalar(idxG[:, :], rel.rearrange("p g c -> p (g c)"), float(DUMMY), None,
                                                  ALU.add))
            step("pe", lambda e: e.matmul(PS[:, 4000:4001], onesF[:, :], small[:, 13, 0:1], start=True, stop=True))
            step("dve", lambda e: e.tensor_copy(flag[:, 0:1], PS[:, 4000:4001]))
            Q.wait("dve", [gathered])

            def within(e):
                for b in range(NBLK):
                    ins = e.tensor_scalar(sub[:, b, :], sub[:, b, :], nodeid[:, b:b + 1], 0.0, ALU.is_le, ALU.add,
                                          accum_out=small[:, 3, b:b + 1])
                return ins
            step("dve", within)
            step("dve", lambda e: e.scalar_tensor_tensor(out=small[:, 4, :], in0=small[:, 2, :], scalar=float(P),
                                                         in1=small[:, 3, :], op0=ALU.mult, op1=ALU.add))
            step("dve", lambda e: e.tensor_scalar(endI[:, :], small[:, 4, :], -1.0, 0.0, ALU.add, ALU.max))

        def degrees():
            with nc.allow_non_contiguous_dma(reason="3200 counts, once"):
                load([lambda e: e.dma_start(ubR[0:1].rearrange("(a b) -> a b", a=1), onep[0:1, 0:1]),
                      lambda e: e.dma_start(ubR[1:NPAD + 1].rearrange("(b p) -> p b", p=P), small[:, 4, :],
                                            allow_slow_non_contiguous=True)])
                load([lambda e: e.dma_start(small[:, 5, :], ubR[0:NPAD].rearrange("(b p) -> p b", p=P),
                                            allow_slow_non_contiguous=True)])
            step("dve", lambda e: e.tensor_tensor(deg[:, :], small[:, 4, :], small[:, 5, :], ALU.subtract))
            step("dve", lambda e: e.tensor_scalar(has[:, :], deg[:, :], 0.5, None, ALU.is_gt))

        def L0_tables():
            xT = arena.get(NBLK, P)
            big = arena.get(NBLK, 2 * P)
            center(W1ab[:, 0:P], P, P, 0)
            center(W1ab[:, P:2 * P], P, P, 1)
            center(We[0:65, 0:P], P, 65, 2)
            step("dve", lambda e: e.tensor_copy(We[0:65, P:2 * P], We[0:65, 0:P]))
            transposed(xn, xT)
            table(xT, W1ab[:, :], 2 * P, T0, big)
            swapped = T0b[0:NPAD, :].rearrange("(b p) d -> p b d", p=P)
            load([lambda e: e.dma_start(swapped[:, :, 0:P], big[:, :, P:2 * P]),
                  lambda e: e.dma_start(swapped[:, :, P:2 * P], big[:, :, 0:P])])

        def L0_edges():
            Q.barrier()
            arena.reset()
            NR = 8
            Gs = [arena.get(CB, 2 * P) for _ in range(NR)]
            eT = [arena.get(GE) for _ in range(3)]
            sR = [arena.get(GE) for _ in range(3)]
            wR = [arena.get(GE) for _ in range(3)]
            dR = [arena.get(GE) for _ in range(3)]
            kR = [arena.get(GE, dt=BF16) for _ in range(4)]
            Tw = [arena.get(2 * P) for _ in range(4)]
            OT = [arena.get(CB * P) for _ in range(2)]
            rr = [arena.get(2 * CB, P) for _ in range(2)]
            r1, r2 = [flat(r[:, 0:CB, :]) for r in rr], [r[:, CB:2 * CB, :] for r in rr]
            s1 = [arena.get(CB * P) for _ in range(2)]
            OR = [arena.get(2 * CB, P) for _ in range(2)]
            Ob, R2 = [r[:, 0:CB, :] for r in OR], [r[:, CB:2 * CB, :] for r in OR]
            Sm = [arena.get(CB, P) for _ in range(6)]
            Vm = [arena.get(CB, P) for _ in range(2)]
            jl = arena.get(CB, P)
            ja = arena.get(2 * CB, P, dt=BF16)
            X2 = [arena.get(CB, XW) for _ in range(3)]
            cn = [arena.get(CB) for _ in range(8)]
            mF = [arena.get(CB) for _ in range(2)]
            iA = [arena.get(CB, dt=I32) for _ in range(10)]
            var = [arena.get(4 * CB) for _ in range(3)]
            rst = [arena.get(4 * CB) for _ in range(3)]
            nh_, na_ = arena.get(4 * CB), arena.get(4 * CB)
            mm = [arena.get(CB) for _ in range(4)]
            C2 = 2 * CB
            cb = [arena.get(C2) for _ in range(4)]
            mg = [arena.get(C2) for _ in range(4)]
            sg = [arena.get(C2) for _ in range(4)]
            OL = arena.get(C2, P)
            OH = arena.get(C2, NBLK)
            fst = arena.get(C2)
            RH = arena.get(C2, 2, NBLK)
            DM = [arena.get(C2 + 1, NBLK) for _ in range(2)]
            DS = [arena.get(C2 + 1, NBLK) for _ in range(2)]
            DX = arena.get(C2 + 1, NBLK)

            op("dve", lambda e: e.memset(DM[0][:, C2, :], -BIG))
            op("dve", lambda e: e.memset(DS[0][:, C2, :], 0.0))
            for x2 in X2:
                op("dve", lambda e, x2=x2: e.memset(x2[:, :, P:XW], 0.0))
            for t in eT:
                op("dve", lambda e, t=t: e.memset(t[64:65, :], 1.0))
            Q.barrier()
            state["last"] = None
            degrees()
            out_of_window = {}
            Q.q["pool"].append(lambda e: out_of_window.update(v=e.value_load(flag[0:1, 0:1], min_val=0,
                                                                             max_val=EP)))
            psC = PS[:, 0:1024]

            def L0_rows(b):
                if b % 2 == 0:
                    g = b // 2
                    put("eT", g, Q.dma_either("sp", e_sem[g % 3], *edge_features(0, 64, eT[g % 3][0:64, :], g * GE),
                                              g0("C", b - 5)))
                    put("sR", g, dma("sp", s_sem[g % 3], lambda e: e.dma_start(sR[g % 3], grow(sF, g)), g0("S1", b - 5)))
                    put("wR", g, dma("sp", w_sem[g % 3], lambda e: e.dma_start(wR[g % 3], grow(wF, g)), g0("S", b - 5)))
                    put("dR", g, dma("sp", d_sem[g % 3], lambda e: e.dma_start(dR[g % 3], grow(dF, g)), g0("OT", b - 5)))
                    put("kR", g, dma("sp", k_sem[g % 4], lambda e: e.dma_start(kR[g % 4], grow(keepR, g)),
                                     g0("scan", b - 7)))

                    def window(e):
                        v = e.value_load(d0I[0:1, g:g + 1], min_val=0, max_val=NPAD - 1)
                        return e.dma_start(Tw[g % 4], T0b[bass.ds(v, P), :])
                    put("Tw", g, dma("sp", t_sem[g % 4], window, g0("C", b - 7)))

            def L0_gather(b):
                put("gs", b, gather(gs_sem[0:NR], b, T0, srcI, Gs[b % NR], g0("T", b - NR)))

            def L0_outside(b):
                seen = dict(Q.seen["pool"])
                got = g0("gs", b)
                x = gx_sem[0]

                def go(e):
                    with e.If(out_of_window["v"] > 0):
                        e.wait_ge(Q.sems[got[0]], got[1])
                        for c in range(CB):
                            e.indirect_dma_start(
                                out=Gs[b % NR][:, c, :], out_offset=None, in_=T0b[:, :],
                                in_offset=bass.IndirectOffsetOnAxis(ap=idxG[:, CB * b + c:CB * b + c + 1], axis=0),
                                compute_op=ALU.add).then_inc(Q.sems[x], 16)
                        e.wait_ge(Q.sems[x], 16 * CB * (b + 1))
                Q.q["pool"].append(go)
                assert seen == Q.seen["pool"]
                put("gx", b, op("pool", lambda e: e.engine_nop()))

            def L0_OT(b):
                g, h0 = b // 2, b % 2 * CB * P
                put("OT", b, op("dve", lambda e: e.tensor_scalar(OT[b % 2], dR[g % 3][:, h0:h0 + CB * P],
                                                                 wcol[:, g:g + 1], None, ALU.is_equal),
                                g0("dR", g), g0("C", b - 2)))

            def L0_C(b):
                g, h0 = b // 2, b % 2 * CB * P

                def C(e):
                    for c in range(CB):
                        e.matmul(psC[:, c * 2 * P:(c + 1) * 2 * P], eT[g % 3][0:65, h0 + c * P:h0 + (c + 1) * P],
                                 We[0:65, :], start=True, stop=False)
                        ins = e.matmul(psC[:, c * 2 * P:(c + 1) * 2 * P], OT[b % 2][:, c * P:(c + 1) * P],
                                       Tw[g % 4], start=False, stop=True)
                    return ins
                put("C", b, op("pe", C, g0("eT", g), g0("OT", b), g0("Tw", g), g0("t", b - 1)))

            def L0_t(b):
                t = Gs[b % NR]
                put("t", b, op("dve", lambda e: e.tensor_tensor(flat(t), flat(t), psC, ALU.add),
                               g0("gs", b), g0("gx", b), g0("C", b)))

            def L0_S1(b):
                g, h0 = b // 2, b % 2 * CB * P

                def S(e):
                    return e.tensor_tensor(Sm[b % 6], sR[g % 3][:, h0:h0 + CB * P].rearrange("p (c f) -> p c f", f=P),
                                           bf(srcF[:, CB * b:CB * b + CB]), ALU.is_equal)
                put("S1", b, op("dve", S, g0("sR", g), g0("SS", b - 6)))

            def L0_V(b):
                def V(e):
                    for c in range(CB):
                        ins = e.activation(Vm[b % 2][:, c, :], Sm[b % 6][:, c, :], ACT.Copy, bias=-MASK, scale=MASK,
                                           accum_out=cn[b % 8][:, c:c + 1])
                    return ins
                put("V", b, op("act", V, g0("S1", b), g0("ex", b - 2), g0("X", b - 8)))

            def L0_S2(b):
                g, h0 = b // 2, b % 2 * CB * P
                o = b % 2 * CB
                old = g0("RH", 2 * g - 7)

                def first(c):
                    return lambda e: e.tensor_tensor_reduce(jl[:, c, :], Sm[b % 6][:, c, :], ltri[:, :], 1.0, 0.0,
                                                            ALU.mult, ALU.add, cb[g % 4][:, o + c:o + c + 1])

                def largest(c):
                    r = slice(h0 + c * P, h0 + (c + 1) * P)
                    return lambda e: e.tensor_tensor_reduce(Vm[b % 2][:, c, :], Vm[b % 2][:, c, :], wR[g % 3][:, r],
                                                            1.0, -BIG, ALU.add, ALU.max,
                                                            mg[g % 4][:, o + c:o + c + 1])
                mine = [f(c) for c in range(CB) for f in (first, largest)]
                steps, tok = rs_steps(b - 1), None
                after = [g0("V", b), g0("wR", g), g0("S", b - 1), old]
                for k in range(max(len(steps), len(mine))):
                    if k < len(steps):
                        tok = op("dve", steps[k], tok or rs_after(b - 1))
                    if k < len(mine):
                        last = op("dve", mine[k], *after)
                put("S", b, last)
                if steps:
                    put("rs", b - 1, tok)
                    put("rs", b - 2, tok)
                sl = slice(CB * b, CB * b + CB)

                def S3(e):
                    e.tensor_scalar(mm[b % 4], mg[g % 4][:, o:o + CB], -1.0, None, ALU.mult)
                    return e.scalar_tensor_tensor(out=mF[b % 2], in0=cb[g % 4][:, o:o + CB], scalar=float(EP),
                                                  in1=srcF[:, sl], op0=ALU.mult, op1=ALU.add)
                put("S3", b, op("dve", S3, g0("S", b), g0("ex", b - 4), g0("S4", b - 2)))

            def L0_S4(b):
                put("S4", b, op("dve", lambda e: e.tensor_scalar(iA[b % 10], mF[b % 2], pcol[:, 0:1], None, ALU.min),
                                g0("S3", b), g0("sc", b - 10)))

            def L0_sq(b):
                g, o, t = b // 2, b % 2 * CB, Gs[b % NR]

                def sq(e):
                    for c in range(CB):
                        for hh in range(2):
                            i = 2 * (o + c) + hh
                            ins = e.activation(ja[:, 2 * c + hh, :], t[:, c, hh * P:(hh + 1) * P], ACT.Square,
                                               accum_out=var[g % 3][:, i:i + 1])
                    return ins
                put("sq", b, op("act", sq, g0("t", b), g0("rs", 2 * g - 5), g0("sq", b - 1)))

            def L0_ex(b):
                g, o = b // 2, b % 2 * CB

                def ex(e):
                    for c in range(CB):
                        ins = e.activation(Vm[b % 2][:, c, :], Vm[b % 2][:, c, :], ACT.Exp,
                                           bias=mm[b % 4][:, c:c + 1], accum_out=sg[g % 4][:, o + c:o + c + 1])
                    return ins
                put("ex", b, op("act", ex, g0("S3", b), g0("S", b), g0("RH", 2 * g - 7)))

            def rs_steps(b):
                if b % 2 == 0 or b < 0:
                    return []
                v, r = var[b // 2 % 3], rst[b // 2 % 3]
                return [lambda e: e.tensor_scalar(v, v, 1.0 / P, EPS, ALU.mult, ALU.add)] + \
                    rsqrt_steps(v, r, nh_, na_)

            def rs_after(b):
                return [g0("sq", b), g0("D", b - 6)]

            def L0_rs(b):
                if b == NBAT - 1:
                    toks = rs_after(b)
                    for fn in rs_steps(b):
                        toks = [op("dve", fn, *toks)]
                    put("rs", b, toks[0])
                    put("rs", b - 1, toks[0])

            def L0_A(b):
                if b % 2 == 0:
                    return
                g = b // 2
                sl = slice(C2 * g, C2 * g + C2)

                def onehot(e):
                    e.tensor_tensor(OL, bc(iotaf[:, :], C2), bf(loF[:, sl]), ALU.is_equal)
                    e.tensor_tensor(OH, bc(iotaf[:, 0:NBLK], C2), bf(hiF[:, sl], NBLK), ALU.is_equal)
                    return e.tensor_scalar(fst, cb[g % 4], 0.5, None, ALU.is_lt)
                tok = op("dve", onehot, g0("Z", b - 2), g0("S", b), g0("RH", b - 2))
                tok = op("dve", lambda e: e.tensor_tensor(OH, OH, bf(fst, NBLK), ALU.mult), tok)

                def rh(e):
                    e.tensor_tensor(RH[:, :, 0, :], OH, bf(mg[g % 4], NBLK), ALU.mult)
                    return e.tensor_tensor(RH[:, :, 1, :], OH, bf(sg[g % 4], NBLK), ALU.mult)
                put("RH", b, op("dve", rh, tok, g0("ex", b)))

            def L0_Z(b):
                if b % 2 == 0:
                    return

                def Z(e):
                    for c in range(C2):
                        ins = e.matmul(bank(7)[:, c * 50:(c + 1) * 50], OL[:, c, :],
                                       RH[:, c, :, :].rearrange("p a b -> p (a b)"), start=True, stop=True)
                    return ins
                put("Z", b, op("pe", Z, g0("RH", b), g0("mul", b - 2)))

            zz = bank(7, 50 * C2).rearrange("p (c t n) -> p c t n", t=2, n=NBLK)

            def L0_dm(b):
                if b % 2 == 0:
                    return
                g = b // 2
                dm, dmn = DM[g % 2], DM[(g + 1) % 2]
                tok = op("dve", lambda e: e.tensor_scalar(dm[:, 0:C2, :], zz[:, :, 1, :], 0.5, -BIG, ALU.is_lt,
                                                          ALU.mult), g0("Z", b), g0("df", b - 4))
                tok = op("dve", lambda e: e.tensor_tensor(dm[:, 0:C2, :], dm[:, 0:C2, :], zz[:, :, 0, :], ALU.add),
                         tok)
                tok = op("dve", lambda e: e.tensor_reduce(dmn[:, C2, :], dm.rearrange("p s n -> p n s"), AX,
                                                          ALU.max), tok, g0("df", b - 2))
                put("df", b, op("dve", lambda e: e.tensor_tensor(DX, dm, bc(dmn[:, C2, :], C2 + 1), ALU.subtract),
                                tok, g0("mul", b - 2)))

            def L0_DX(b):
                if b % 2:
                    put("DX", b, op("act", lambda e: e.activation(DX, DX, ACT.Exp), g0("df", b)))

            def L0_mul(b):
                if b % 2 == 0:
                    return
                ds, dsn = DS[b // 2 % 2], DS[(b // 2 + 1) % 2]

                def mul(e):
                    e.tensor_tensor(ds[:, 0:C2, :], DX[:, 0:C2, :], zz[:, :, 1, :], ALU.mult)
                    return e.tensor_tensor(ds[:, C2, :], DX[:, C2, :], ds[:, C2, :], ALU.mult)
                put("mul", b, op("dve", mul, g0("DX", b), g0("red", b - 2)))
                put("red", b, op("dve", lambda e: e.tensor_reduce(dsn[:, C2, :], ds.rearrange("p s n -> p n s"), AX,
                                                                  ALU.add), g0("mul", b)))

            ND = 3

            def L0_D(b):
                o = b % 2 * C2
                t = Gs[b % NR].rearrange("p c (h f) -> p (c h) f", h=2)[:, 0:C2 - ND, :]
                put("D", b, [g0("Da", b), op("dve", lambda e: e.tensor_tensor(
                    t, t, bf(rst[b // 2 % 3][:, o:o + C2 - ND]), ALU.mult), g0("rs", b), g0("sq", b))])

            def L0_Da(b):
                o = b % 2 * C2
                t = Gs[b % NR].rearrange("p c (h f) -> p (c h) f", h=2)

                def scale(e):
                    for k in range(C2 - ND, C2):
                        ins = e.activation(t[:, k, :], t[:, k, :], ACT.Copy, scale=rst[b // 2 % 3][:, o + k:o + k + 1])
                    return ins
                put("Da", b, op("act", scale, g0("rs", b), g0("sq", b)))

            def L0_T(b):
                t = Gs[b % NR]

                def T(e):
                    for c in range(CB):
                        for hh in range(2):
                            ins = e.transpose(bank(2 + hh)[:, c * P:(c + 1) * P], t[:, c, hh * P:(hh + 1) * P],
                                              ident[:, :])
                    return ins
                put("T", b, op("pe", T, g0("D", b), g0("r", b - 1)))

            def L0_r(b):
                def r(e):
                    return e.activation(flat(rr[b % 2]), PS[:, 1024:2048], ACT.Relu, bias=cols[:, 1:2],
                                        scale=cols[:, 0:1])
                put("r", b, op("act", r, g0("T", b), g0("scan", b - 2), g0("B", b - 2)))

            def L0_scan(b):
                g, h0 = b // 2, b % 2 * CB * P
                put("scan", b, op("dve", lambda e: e.tensor_tensor_scan(
                    s1[b % 2], kR[g % 4][:, h0:h0 + CB * P], r1[b % 2],
                    s1[(b - 1) % 2][:, CB * P - 1:CB * P] if b else 0.0, ALU.mult, ALU.add),
                    g0("r", b), g0("kR", g), g0("scan", b - 1), g0("B", b - 2)))

            def L0_B(b):
                def B(e):
                    for c in range(CB):
                        e.transpose(bank(4)[:, c * P:(c + 1) * P], s1[b % 2][:, c * P:(c + 1) * P], ident[:, :])
                    for c in range(CB):
                        ins = e.transpose(bank(5)[:, c * P:(c + 1) * P], r2[b % 2][:, c, :], ident[:, :])
                    return ins
                put("B", b, op("pe", B, g0("scan", b), g0("r", b), g0("O", b - 1), g0("R2", b - 1)))

            def L0_OR(b):
                tok = op("act", lambda e: e.activation(flat(OR[b % 2]), PS[:, 2048:3072], ACT.Copy),
                         g0("B", b), g0("SS", b - 2), g0("so", b - 2))
                put("R2", b, tok)
                put("O", b, tok)
                put("so", b, dma("sp", o_sem[b % 2], lambda e: e.dma_start(
                    H0[b * CB * P:(b + 1) * CB * P, :].rearrange("(c p) f -> p c f", p=P), Ob[b % 2]), g0("O", b)))

            def L0_SS(b):
                def SS(e):
                    for c in range(CB):
                        ins = e.matmul(bank(6)[:, c * P:(c + 1) * P], Sm[b % 6][:, c, :], R2[b % 2][:, c, :],
                                       start=True, stop=True)
                    return ins
                put("SS", b, op("pe", SS, g0("R2", b), g0("S1", b), g0("X", b - 1)))

            def L0_X(b):
                def X(e):
                    e.activation(X2[b % 3][:, :, P], cn[b % 8], ACT.Copy, bias=float(P), scale=1.0 / MASK)
                    return e.activation(X2[b % 3][:, :, 0:P], bank(6).rearrange("p (c f) -> p c f", f=P), ACT.Copy)
                put("X", b, op("act", X, g0("SS", b), g0("sc", b - 3)))

            def L0_scatter(b):
                toks = []
                for c in range(CB):
                    k = CB * b + c
                    prev = tk.get(("tab", k - KT))
                    tok = dma("pool", tab_sem[k % KT], lambda e, c=c, k=k: e.indirect_dma_start(
                        out=tabs[k % KT], out_offset=bass.IndirectOffsetOnAxis(ap=iA[b % 10][:, c:c + 1], axis=0),
                        in_=X2[b % 3][:, c, :], in_offset=None, compute_op=ALU.add), g0("X", b), g0("S4", b), prev)
                    put("tab", k, tok)
                    toks.append(tok)
                put("sc", b, toks)

            pipeline([(0, L0_rows), (9, L0_scatter), (8, L0_X), (3, L0_t), (8, L0_mul), (3, L0_V), (6, L0_T),
                      (7, L0_B), (2, L0_C),
                      (2, L0_S1), (4, L0_ex), (6, L0_r), (7, L0_dm), (3, L0_S2), (7, L0_OR), (4, L0_rs), (6, L0_Z),
                      (5, L0_Da), (5, L0_D), (5, L0_A), (3, L0_S4), (7, L0_SS), (3, L0_sq), (7, L0_DX), (1, L0_OT),
                      (6, L0_scan), (1, L0_outside), (0, L0_gather)])
            last = g0("red", NBAT - 1)
            op("dve", lambda e: e.tensor_copy(Mx[:, :], DM[NG % 2][:, C2, :]), last)
            op("dve", lambda e: e.tensor_copy(Sx[:, :], DS[NG % 2][:, C2, :]), last)

        def L0_nodes_L1_table():
            Q.barrier()
            arena.reset()
            state["last"] = None
            tk.clear()
            F, Y, Z = [arena.get(NBLK, P) for _ in range(3)]
            tb = [arena.get(NBLK, XW) for _ in range(KT)]
            xT, aT, Tb, xb = [arena.get(NBLK, P) for _ in range(4)]
            tX = arena.get(NBLK, XW)
            w2T, b2r, wM = arena.get(P), arena.get(P), arena.get(P)
            load([lambda e: e.dma_start(wA[:, 0:P], A["L0_gnn_msg_w2"][:, :]),
                  lambda e: e.dma_start(wA[:, P:2 * P], A["L0_gnn_upd_w2"][:, :]),
                  lambda e: e.dma_start(wB[:, 0:P], A["L0_gnn_upd_w1"][0:P, :]),
                  lambda e: e.dma_start(wB[:, P:2 * P], A["L0_gnn_upd_w1"][P:2 * P, :])] +
                 [lambda e, i=i, n=n: e.dma_start(cols[:, i:i + 1], A[n].rearrange("(n a) -> n a", a=1))
                  for i, n in ((4, "L0_gnn_msg_b2"), (5, "L0_gnn_ln2_g"), (6, "L0_gnn_ln2_b"))] +
                 [lambda e, i=i, n=n: e.dma_start(v_[:, i, 0:P], row(A[n], P)) for i, n in
                  ((1, "L0_gnn_upd_b1"), (4, "L0_gnn_upd_b2"))])
            tbs = ring("tbl", KT)
            loaded = [dma("sp", tbs[k], lambda e, k=k: e.dma_start(
                tb[k], tabs[k][0:NPAD, :].rearrange("(b p) d -> p b d", p=P))) for k in range(KT)]
            ends = gather_ends(H0, F)
            center(wB[:, 0:P], P, P, 0)
            center(wB[:, P:2 * P], P, P, 1)
            center(v_[:, 1, 0:P], P, P, 2)
            folded([wA[:, 0:P]], [w2T], wB[:, P:2 * P], [wM], cols[:, 4:5], b2r, v_[:, 0, 0:P])
            step("dve", lambda e: e.scalar_tensor_tensor(out=xb, in0=xn[:, :, :], scalar=2.0, in1=bc(v_[:, 4, 0:P]),
                                                         op0=ALU.mult, op1=ALU.add))
            prepared = state["last"]

            def tails(e):
                e.memset(tX[:, :, P + 1:XW], 0.0)
                return e.tensor_copy(tX[:, :, P], Mx[:, :])
            step("dve", tails)
            step("dve", lambda e: e.tensor_scalar(small[:, 3, :], Sx[:, :], 0.5, None, ALU.is_lt))
            step("dve", lambda e: e.tensor_tensor(small[:, 3, :], small[:, 3, :], Sx[:, :], ALU.add))
            for k in range(1, KT):
                state["last"] = op("dve", lambda e, k=k: e.tensor_tensor(tb[0], tb[0], tb[k], ALU.add),
                                   state["last"], loaded[0], loaded[k])
            step("dve", lambda e: e.tensor_tensor(small[:, 11, :], deg[:, :], tb[0][:, :, P], ALU.add))
            step("dve", lambda e: e.tensor_tensor(Tb, bc(v_[:, 0, 0:P]), bf(small[:, 11, :]), ALU.mult))
            step("dve", lambda e: e.tensor_tensor(Tb, Tb, bc(v_[:, 1, 0:P]), ALU.add))
            added, state["last"] = state["last"], prepared
            halves([turn(xn), out_of_psum(xT)])
            state["last"] = [added, state["last"]]
            stored = T1.rearrange("(b p) d -> p b d", p=P)
            halves([
                on("dve", lambda e, s: e.tensor_tensor(F[:, s, :], F[:, s, :], bf(has[:, s]), ALU.mult)),
                on("dve", lambda e, s: e.tensor_tensor(F[:, s, :], F[:, s, :], tb[0][:, s, 0:P], ALU.add)),
                turn(F), out_of_psum(aT), times([(xT, wB[:, 0:P]), (aT, wM)]),
                on("dve", lambda e, s: e.tensor_tensor(Y[:, s, :], PN[:, s, :], Tb[:, s, :], ALU.add))] +
                rstd(Y, Z) + [scaled(Y, Y, 9), turn(Y),
                out_of_psum(aT, ACT.Relu, scale=cols[:, 5:6], bias=cols[:, 6:7]), times([(aT, wA[:, P:2 * P])]),
                on("dve", lambda e, s: e.tensor_tensor(Y[:, s, :], PN[:, s, :], xb[:, s, :], ALU.add))] +
                norm_to_x(Y, Z) + [
                row_sums(xn, Z, 0, ACT.Square),
                on("dve", lambda e, s: e.tensor_scalar(small[:, 1, s], small[:, 0, s], 1e-35, None, ALU.max))] +
                inverse_root(1, 2) + [
                on("dve", lambda e, s: e.tensor_tensor(small[:, 2, s], small[:, 2, s], small[:, 0, s], ALU.mult)),
                on("dve", lambda e, s: e.tensor_scalar(small[:, 2, s], small[:, 2, s], 1e-12, None, ALU.max)),
                on("dve", lambda e, s: e.tensor_tensor(small[:, 2, s], small[:, 2, s], small[:, 3, s], ALU.mult)),
                on("dve", lambda e, s: e.reciprocal(small[:, 4, s], small[:, 2, s])),
                on("dve", lambda e, s: e.tensor_tensor(tX[:, s, 0:P], xn[:, s, :], bf(small[:, 4, s]), ALU.mult)),
                lambda a, b: load([lambda e: e.dma_start(stored[:, a:b, :], tX[:, a:b, :])])], ends)

        def L1_edges():
            Q.barrier()
            arena.reset()
            tk.clear()
            G = [arena.get(CB, XW) for _ in range(6)]
            kR = [arena.get(GE, dt=BF16) for _ in range(6)]
            s1 = [arena.get(1, CB * P) for _ in range(2)]
            Ob = [arena.get(CB, P) for _ in range(3)]
            pm = [arena.get(CB) for _ in range(4)]
            pp = [arena.get(CB) for _ in range(4)]
            eq, er = [arena.get(256) for _ in range(2)], [arena.get(256) for _ in range(2)]
            e3 = [arena.get(3, 256, dt=BF16) for _ in range(2)]
            raw = [t.rearrange("f (q c) -> (f q) c", q=4) for t in (eTs[64:96, :], A["ea32T"])]
            cut = S32.rearrange("(k f) (q c) -> (f q) k c", f=32, q=4)
            q_sem = ring("sS", 2)

            def cut_load(b):
                if b % 2 == 0:
                    g = b // 2
                    sl = slice(256 * g, 256 * g + 256)
                    put("eq", g, Q.dma_either("sp", e_sem[g % 2], lambda: unsorted["sp"] > 0,
                                              lambda e: e.dma_start(eq[g % 2], raw[0][:, sl]),
                                              lambda e: e.dma_start(eq[g % 2], raw[1][:, sl]),
                                              g0("r1", g - 2), g0("c1", g - 2)))

            def cut_1(b):
                if b % 2 == 0:
                    g = b // 2
                    put("c1", g, op("act", lambda e: e.activation(e3[g % 2][:, 0, :], eq[g % 2], ACT.Copy),
                                    g0("eq", g), g0("sS", g - 2)))

            def cut_r(b):
                if b % 2 == 0:
                    g = b // 2
                    put("r1", g, op("dve", lambda e: e.tensor_tensor(er[g % 2], eq[g % 2], e3[g % 2][:, 0, :],
                                                                     ALU.subtract), g0("c1", g), g0("c3", g - 2)))

            def cut_2(b):
                if b % 2 == 0:
                    g = b // 2
                    put("c2", g, op("act", lambda e: e.activation(e3[g % 2][:, 1, :], er[g % 2], ACT.Copy),
                                    g0("r1", g)))

            def cut_3(b):
                if b % 2 == 0:
                    g = b // 2
                    put("c3", g, op("dve", lambda e: e.tensor_tensor(e3[g % 2][:, 2, :], er[g % 2], e3[g % 2][:, 1, :],
                                                                     ALU.subtract), g0("c2", g)))

            def cut_store(b):
                if b % 2 == 0:
                    g = b // 2
                    sl = slice(256 * g, 256 * g + 256)
                    dma("sp", q_sem[g % 2], lambda e: e.dma_start(cut[:, 0:3, sl], e3[g % 2]), g0("c3", g))
                    put("sS", g, dma("sp", q_sem[g % 2], lambda e: e.dma_start(cut[:, 3, sl], e3[g % 2][:, 0, :]),
                                     g0("c3", g)))

            def L1_load(b):
                put("gs", b, gather(gsem[0:6], b, T1, srcI, G[b % 6], g0("T", b - 6)))

            def L1_front(b):
                put("pm", b, op("dve", lambda e: e.tensor_tensor(pm[b % 4], eF[:, CB * b:CB * b + CB],
                                                                 G[b % 6][:, :, P], ALU.subtract),
                                g0("gs", b), g0("p", b - 4)))
                put("p", b, op("act", lambda e: e.activation(pp[b % 4], pm[b % 4], ACT.Exp), g0("pm", b), g0("D", b - 4)))
                G_ = G[b % 6][:, :, 0:P]
                put("D", b, op("dve", lambda e: e.tensor_tensor(G_, G_, bf(pp[b % 4]), ALU.mult), g0("p", b)))

                def T(e):
                    for c in range(CB):
                        ins = e.transpose(bank(b % 3)[:, c * P:(c + 1) * P], G[b % 6][:, c, 0:P], ident[:, :])
                    return ins
                put("T", b, op("pe", T, g0("D", b), g0("gs", b), g0("scan", b - 3)))

            pipeline([(0, lambda b: rows_load(b, kR, keepR, 6)), (0, cut_load),
                      (4, lambda b: backend2(b, 1, bank(3), s1, Ob, H1)),
                      (3, lambda b: backend(b, 1, [bank(b % 3)], None, s1, Ob, H1, kR, g0("T", b), ALU.mult, ALU.add, 0.0)),
                      (2, L1_front), (6, cut_store), (2, cut_1), (3, cut_r), (4, cut_2), (5, cut_3),
                      (0, L1_load)])

        def L1_nodes_L2_table():
            Q.barrier()
            arena.reset()
            state["last"] = None
            tk.clear()
            F, Z, xT = [arena.get(NBLK, P) for _ in range(3)]
            big = arena.get(NBLK, 2 * P)
            ends = gather_ends(H1, F)
            step("dve", lambda e: e.tensor_scalar(small[:, 0, 0:1], epsc[:, :], 2.0, None, ALU.add))
            step("dve", lambda e: e.tensor_scalar(Z, xn[:, :, :], small[:, 0, 0:1], None, ALU.mult))
            W1 = A["L2_gnn_W1"]
            load([lambda e: e.dma_start(W1ab[:, :], W1[0:P, :]),
                  lambda e: e.dma_start(wD[:, :], row(A["L2_gnn_b1"], 2 * P))] +
                 [lambda e, k=k: e.dma_start(wC[32 * k:32 * k + 32, :], W1[P:P + 32, :]) for k in range(4)] +
                 [lambda e, i=i, n=n: e.dma_start(cols[:, 2 * i:2 * i + 2], A[n].rearrange("(h n) -> n h", n=P),
                                                  allow_slow_non_contiguous=True)
                  for i, n in enumerate(("L2_gnn_g1", "L2_gnn_be1"))])
            center(W1ab[:, :], 2 * P, P, 0)
            center(wC[:, :], 2 * P, P, 1)
            center(wD[:, :], 2 * P, P, 2)
            cut = [arena.get(2 * P, dt=BF16) for _ in range(3)]
            step("dve", lambda e: e.tensor_copy(cut[0], wC[:, :]))
            step("dve", lambda e: e.tensor_tensor(wC[:, :], wC[:, :], cut[0], ALU.subtract))
            step("dve", lambda e: e.tensor_copy(cut[1], wC[:, :]))
            step("dve", lambda e: e.tensor_tensor(cut[2], wC[:, :], cut[1], ALU.subtract))

            def stacks(e):
                e.tensor_copy(wX[0:96, :], cut[0][0:96, :])
                e.tensor_copy(wX[96:128, :], cut[1][96:128, :])
                e.tensor_copy(wY[0:32, :], cut[2][0:32, :])
                e.tensor_copy(wY[32:64, :], cut[1][32:64, :])
                return e.tensor_copy(wY[64:96, :], cut[1][64:96, :])
            step("dve", stacks)
            Y = arena.get(NBLK, P)
            halves([
                on("dve", lambda e, s: e.tensor_tensor(Y[:, s, :], F[:, s, :], bf(has[:, s]), ALU.mult)),
                on("dve", lambda e, s: e.tensor_tensor(Y[:, s, :], Y[:, s, :], Z[:, s, :], ALU.add))] +
                norm_to_x(Y, F) + [turn(xn), out_of_psum(xT)], ends)
            table(xT, W1ab[:, :], 2 * P, T2, big, wD[:, :])

        def L2_edges():
            Q.barrier()
            arena.reset()
            tk.clear()
            G = [arena.get(CB, 2 * P) for _ in range(10)]
            kR = [arena.get(GE, dt=BF16) for _ in range(6)]
            eT = [arena.get(GE, dt=BF16) for _ in range(3)]
            hT = [arena.get(2, CB * P) for _ in range(2)]
            s2 = [arena.get(2, CB * P) for _ in range(2)]
            Ob = [arena.get(CB, 2 * P) for _ in range(3)]
            ja = arena.get(CB, 2 * P, dt=BF16)
            C4 = 4 * CB
            var = [arena.get(C4) for _ in range(3)]
            rst = [arena.get(C4) for _ in range(3)]
            nh_, na_ = arena.get(C4), arena.get(C4)

            def L2_rows(b):
                rows_load(b, kR, keepR, 6)
                if b % 2 == 0:
                    g = b // 2
                    put("eT", g, dma("sp", e_sem[g % 3], lambda e: e.dma_start(eT[g % 3], S32[:, g * GE:(g + 1) * GE]),
                                     g0("C", b - 5)))

            def L2_load(b):
                put("gs", b, gather(gsem, b, T2, srcI, G[b % 10], g0("T", b - 10)))

            psC = PS[:, 0:1024]

            def L2_front(b):
                g, h0 = b // 2, (b % 2) * CB * P

                def C(e):
                    for c in range(CB):
                        o, r = psC[:, c * 2 * P:(c + 1) * 2 * P], slice(h0 + c * P, h0 + (c + 1) * P)
                        e.matmul(o, eT[g % 3][:, r], wX[:, :], start=True, stop=False)
                        ins = e.matmul(o, eT[g % 3][0:96, r], wY[0:96, :], start=False, stop=True)
                    return ins
                put("C", b, op("pe", C, g0("eT", g), g0("t", b - 1)))

            def L2_t(b):
                t = G[b % 10]
                put("t", b, op("dve", lambda e: e.tensor_tensor(flat(t), flat(t), psC, ALU.add), g0("gs", b), g0("C", b)))


            def L2_sq(b):
                q, o, t = b // 4, b % 4 * CB, G[b % 10]

                def sq(e):
                    for c in range(CB):
                        ins = e.activation(ja[:, c, :], t[:, c, :], ACT.Square, accum_out=var[q % 3][:, o + c:o + c + 1])
                    return ins
                put("sq", b, op("act", sq, g0("t", b), g0("rs", 4 * q - 9), g0("sq", b - 1)))

            def L2_rstd(b):
                if b % 4 != 3:
                    return
                v, r = var[b // 4 % 3], rst[b // 4 % 3]
                tok = op("dve", lambda e: e.tensor_scalar(v, v, 1.0 / (2 * P), EPS, ALU.mult, ALU.add), g0("sq", b))
                tok = rsqrt(v, r, nh_, na_, tok, g0("T", b - 12))
                for k in range(4):
                    put("rs", b - k, tok)

            def L2_D(b):
                t, r = G[b % 10], rst[b // 4 % 3][:, b % 4 * CB:b % 4 * CB + CB]
                put("D", b, op("dve", lambda e: e.tensor_tensor(t, t, bf(r, 2 * P), ALU.mult),
                               g0("rs", b), g0("sq", b)))

            def L2_T(b):
                t = G[b % 10]

                def T(e):
                    for h in range(2):
                        for c in range(CB):
                            ins = e.transpose(bank(2 + h)[:, c * P:(c + 1) * P], t[:, c, h * P:(h + 1) * P],
                                              ident[:, :])
                    return ins
                put("T", b, op("pe", T, g0("D", b), g0("sq", b), g0("r", b - 1)))

            def L2_r(b):
                def r(e):
                    for h in range(2):
                        ins = e.activation(hT[b % 2][:, h, :], bank(2 + h), ACT.Gelu, bias=cols[:, 2 + h:3 + h],
                                           scale=cols[:, h:h + 1])
                    return ins
                put("r", b, op("act", r, g0("T", b), g0("scan", b - 2)))

            def L2_scan(b):
                backend(b, 2, None, None, s2, Ob, H2, kR, g0("r", b), ALU.mult, ALU.add, 0.0,
                        srcs=[hT[b % 2][:, 0, :], hT[b % 2][:, 1, :]])

            def L2_back(b):
                backend2(b, 2, PS[:, 2048:3072], s2, Ob, H2)

            pipeline([(0, L2_rows), (3, L2_t), (9, L2_T), (2, L2_front), (9, L2_r), (11, L2_back), (3, L2_sq), (10, L2_scan),
                      (4, L2_rstd), (8, L2_D), (0, L2_load)])


        def L2_nodes_L3_table():
            Q.barrier()
            arena.reset()
            state["last"] = None
            tk.clear()
            F = arena.get(NBLK, 2 * P)
            Y, Z, xT, aT, bT, Tb = [arena.get(NBLK, P) for _ in range(6)]
            w2T = [arena.get(P) for _ in range(2)]
            wM = [arena.get(P) for _ in range(2)]
            b2r = arena.get(P)
            load([lambda e: e.dma_start(wA[:, 0:P], A["L2_gnn_W2"][0:P, :]),
                  lambda e: e.dma_start(wA[:, P:2 * P], A["L2_gnn_W2"][P:2 * P, :]),
                  lambda e: e.dma_start(wB[:, 0:P], A["L2_gnn_Wu"][0:P, :]),
                  lambda e: e.dma_start(wB[:, P:2 * P], A["L2_gnn_Wu"][P:2 * P, :]),
                  lambda e: e.dma_start(wC[:, 0:P], A["WaT"][:, :]),
                  lambda e: e.dma_start(wD[:, 0:P], A["WbT"][:, :]),
                  lambda e: e.dma_start(cols[:, 4:5], A["L2_gnn_b2"].rearrange("(n a) -> n a", a=1))] +
                 [lambda e, i=i, n=n: e.dma_start(v_[:, i, 0:P], row(A[n], P)) for i, n in (
                     (1, "L2_gnn_bu"), (2, "L2_gnn_gu"), (3, "L2_gnn_beu"), (4, "L3_gnn_b"))])
            ends = gather_ends(H2, F)
            center(wB[:, 0:P], P, P, 0)
            center(wB[:, P:2 * P], P, P, 1)
            center(v_[:, 1, 0:P], P, P, 2)
            step("dve", lambda e: e.tensor_tensor(wC[:, 0:P], wC[:, 0:P], wD[:, 0:P], ALU.subtract))
            folded([wA[:, 0:P], wA[:, P:2 * P]], w2T, wB[:, P:2 * P], wM, cols[:, 4:5], b2r, v_[:, 0, 0:P])
            prepared = state["last"]
            step("dve", lambda e: e.tensor_tensor(Tb, bc(v_[:, 0, 0:P]), bf(deg[:, :]), ALU.mult))
            step("dve", lambda e: e.tensor_tensor(Tb, Tb, bc(v_[:, 1, 0:P]), ALU.add))
            added, state["last"] = state["last"], prepared
            halves([turn(xn), out_of_psum(xT)])
            state["last"] = [added, state["last"]]
            stored = T3.rearrange("(b p) d -> p b d", p=P)
            halves([
                on("dve", lambda e, s: e.tensor_tensor(F[:, s, :], F[:, s, :], bf(has[:, s], 2 * P), ALU.mult)),
                turn(F[:, :, 0:P]), out_of_psum(aT), turn(F[:, :, P:2 * P]), out_of_psum(bT),
                times([(xT, wB[:, 0:P]), (aT, wM[0]), (bT, wM[1])]),
                on("dve", lambda e, s: e.tensor_tensor(Y[:, s, :], PN[:, s, :], Tb[:, s, :], ALU.add))] +
                rstd(Y, Z) + [scaled(Y, Y, 9),
                on("dve", lambda e, s: e.tensor_tensor(Y[:, s, :], Y[:, s, :], bc(v_[:, 2, 0:P], s.stop - s.start),
                                                       ALU.mult)),
                on("dve", lambda e, s: e.tensor_tensor(Y[:, s, :], Y[:, s, :], bc(v_[:, 3, 0:P], s.stop - s.start),
                                                       ALU.add)),
                on("act", lambda e, s: e.activation(Y[:, s, :], Y[:, s, :], ACT.Gelu)),
                on("dve", lambda e, s: e.scalar_tensor_tensor(out=Y[:, s, :], in0=xn[:, s, :], scalar=2.0,
                                                              in1=Y[:, s, :], op0=ALU.mult, op1=ALU.add))] +
                norm_to_x(Y, Z) + [
                turn(xn), out_of_psum(xT), times([(xT, wD[:, 0:P])]), out_of_psum(Z),
                lambda a, b: load([lambda e: e.dma_start(stored[:, a:b, :], Z[:, a:b, :])])], ends)

        def L3_edges():
            Q.barrier()
            arena.reset()
            tk.clear()
            G = [arena.get(CB, P) for _ in range(6)]
            kR = [arena.get(GE, dt=BF16) for _ in range(6)]
            s1 = [arena.get(1, CB * P) for _ in range(2)]
            Ob = [arena.get(CB, P) for _ in range(3)]

            def L3_load(b):
                put("gs", b, gather(gsem[0:6], b, T3, srcI, G[b % 6], g0("T", b - 6)))

            def L3_front(b):
                def T(e):
                    for c in range(CB):
                        ins = e.transpose(bank(b % 3)[:, c * P:(c + 1) * P], G[b % 6][:, c, :], ident[:, :])
                    return ins
                put("T", b, op("pe", T, g0("gs", b), g0("scan", b - 3)))

            pipeline([(0, lambda b: rows_load(b, kR, negR, 6)),
                      (4, lambda b: backend2(b, 1, bank(3), s1, Ob, H3)),
                      (3, lambda b: backend(b, 1, [bank(b % 3)], None, s1, Ob, H3, kR, g0("T", b), ALU.add, ALU.max, -BIG)),
                      (2, L3_front), (0, L3_load)])

        def L3_nodes():
            Q.barrier()
            arena.reset()
            state["last"] = None
            tk.clear()
            F, Y, Z, xT, base = [arena.get(NBLK, P) for _ in range(5)]
            ends = gather_ends(H3, F)
            halves([turn(xn), out_of_psum(xT), times([(xT, wC[:, 0:P])]),
                    on("dve", lambda e, s: e.tensor_tensor(base[:, s, :], PN[:, s, :],
                                                           bc(v_[:, 4, 0:P], s.stop - s.start), ALU.add))])
            nf = N // P

            def store(a, b):
                c = min(b, nf)
                load([lambda e: e.dma_start(out[a * P:c * P, :].rearrange("(b p) d -> p b d", p=P), xn[:, a:c, :])])
                if b > nf:
                    load([lambda e: e.dma_start(out[nf * P:N, :], xn[0:N - nf * P, nf, :])])
            halves([
                on("dve", lambda e, s: e.tensor_tensor(Y[:, s, :], base[:, s, :], F[:, s, :], ALU.add)),
                on("dve", lambda e, s: e.tensor_tensor(Y[:, s, :], Y[:, s, :], bf(has[:, s]), ALU.mult)),
                on("dve", lambda e, s: e.tensor_tensor(Y[:, s, :], Y[:, s, :], xn[:, s, :], ALU.add))] +
                norm_to_x(Y, Z) + [store], ends)
            Q.barrier()

        edge_lists()
        L0_edges()
        L0_nodes_L1_table()
        L1_edges()
        L1_nodes_L2_table()
        L2_edges()
        L2_nodes_L3_table()
        L3_edges()
        L3_nodes()

        block = ctx.enter_context(nc.Block())

        @block.sync
        def _(e):
            for f in Q.q["sp"]:
                f(e)

        @block.tensor
        def _(e):
            for f in Q.q["pe"]:
                f(e)

        @block.vector
        def _(e):
            for f in Q.q["dve"]:
                f(e)

        @block.scalar
        def _(e):
            for f in Q.q["act"]:
                f(e)

        @block.gpsimd
        def _(e):
            for f in Q.q["pool"]:
                f(e)


def kernel(**inputs):
    import numpy as np
    import concourse.bacc as bacc
    from concourse.bass_utils import run_bass_kernel_spmd

    a = {k: np.asarray(v) for k, v in inputs.items()}

    def padded(v, n, fill):
        return np.concatenate([v, np.full((n - v.shape[0],) + v.shape[1:], fill, v.dtype)], 0)

    x = padded(a.pop("x"), NPAD, 0)
    src = padded(a.pop("src"), EP, DUMMY)
    dst = a.pop("dst")
    dst = np.concatenate([np.full((1,), -1, dst.dtype), padded(dst, EP, DUMMY)])
    ew = padded(a.pop("edge_weight"), EP, 0)
    e32 = padded(a.pop("edge_attr_32"), EP, 0)
    e64 = padded(a.pop("edge_attr_64"), EP, 0)
    W = a.pop("L3_gnn_W")
    arrays = {"x": x, "src": src, "dst": dst, "edge_weight": ew, "ea32": e32, "ea64": e64, "ea32T": np.ascontiguousarray(e32.T), "ea64T": np.ascontiguousarray(e64.T),
              "WaT": np.ascontiguousarray(W[:, 0:P].T), "WbT": np.ascontiguousarray(W[:, P:2 * P].T)}
    arrays.update(a)
    nc = bacc.Bacc("TRN2", target_bir_lowering=False, num_devices=1)
    feed, A = {}, {}
    for name, v in arrays.items():
        feed[f"in_{name}"] = np.ascontiguousarray(v)
        A[name] = nc.dram_tensor(f"in_{name}", v.shape, mybir.dt.from_np(v.dtype), kind="ExternalInput").ap()
    out = nc.dram_tensor("out_x", (N, P), F32, kind="ExternalOutput").ap()
    build(nc, A, out)
    r = run_bass_kernel_spmd(nc, [feed], core_ids=[0])
    return r.results[0]["out_x"]
```
